# Optimizing a Trainium2 kernel written in Bass

```python
import numpy as np
import jax
import jax.numpy as jnp

def _softmax(x, axis=-1):
    return jax.nn.softmax(x, axis=axis)

def _gelu(x):
    return jax.nn.gelu(x, approximate=True)

def _silu(x):
    return jax.nn.silu(x)

def _sigmoid(x):
    return jax.nn.sigmoid(x)

def _layernorm(x, axis=-1, eps=1e-05):
    m = jnp.mean(x, axis=axis, keepdims=True)
    v = jnp.var(x, axis=axis, keepdims=True)
    return (x - m) / jnp.sqrt(v + eps)

def _scatter_add(tgt, idx, src, axis=0):
    return tgt.at[idx].add(src)

def _segment_sum(src, seg, n):
    return jax.ops.segment_sum(src, seg, n)
kernel_name = 'mk_sandwich_d1_jaxref_r8_749b90'

def setup_inputs(seed: int=0):
    np.random.seed(seed)
    _w = jnp.asarray

    def _L0_attn_setup():
        import jax, jax.numpy as jnp
        import numpy as np
        EPS = 1e-06

        def rms_norm(x, scale):
            x32 = x.astype(jnp.float32)
            mean2 = jnp.mean(jnp.square(x32), axis=-1, keepdims=True)
            return x32 * jax.lax.rsqrt(mean2 + EPS) * scale
        key = jax.random.key(seed)
        ks = jax.random.split(key, 7)
        B, S, E, H, D = (2, 256, 256, 16, 128)
        w_std = 1.0 / np.sqrt(E)
        x = jax.random.normal(ks[0], (B, S, E), jnp.float32)
        wq = jax.random.normal(ks[1], (E, H, D), jnp.float32) * w_std
        wk = jax.random.normal(ks[2], (E, H, D), jnp.float32) * w_std
        wv = jax.random.normal(ks[3], (E, H, D), jnp.float32) * w_std
        wo = jax.random.normal(ks[4], (H, D, E), jnp.float32) * (1.0 / np.sqrt(H * D))
        q_scale = jnp.ones((D,), jnp.float32)
        k_scale = jnp.ones((D,), jnp.float32)
        return {'x': x, 'wq': wq, 'wk': wk, 'wv': wv, 'wo': wo, 'q_scale': q_scale, 'k_scale': k_scale}
    _L0_attn_in = _L0_attn_setup()

    def _L0_ffn_setup():
        import jax, jax.numpy as jnp
        import numpy as np
        import math
        B, S, D = (2, 256, 256)
        H, HD = (16, 128)
        E, I = (4, 256)
        TOP_K = 2
        ROPE_THETA = 10000.0

        def _layernorm(x, w, b):
            mu = jnp.mean(x, axis=-1, keepdims=True)
            var = jnp.mean(jnp.square(x - mu), axis=-1, keepdims=True)
            return (x - mu) * jax.lax.rsqrt(var + 1e-05) * w + b

        def _rotate_half(x):
            x1, x2 = jnp.split(x, 2, axis=-1)
            return jnp.concatenate((-x2, x1), axis=-1)

        def _attention(h, wq, bq, wk, bk, wv, bv, wo, bo):
            b, s, _ = h.shape
            q = (h @ wq + bq).reshape(b, s, H, HD).transpose(0, 2, 1, 3)
            k = (h @ wk + bk).reshape(b, s, H, HD).transpose(0, 2, 1, 3)
            v = (h @ wv + bv).reshape(b, s, H, HD).transpose(0, 2, 1, 3)
            inv_freq = 1.0 / ROPE_THETA ** (jnp.arange(0, HD, 2, dtype=jnp.float32) / HD)
            freqs = jnp.arange(s, dtype=jnp.float32)[:, None] * inv_freq[None, :]
            emb = jnp.concatenate((freqs, freqs), axis=-1)
            cos = jnp.cos(emb)[None, None]
            sin = jnp.sin(emb)[None, None]
            q = q * cos + _rotate_half(q) * sin
            k = k * cos + _rotate_half(k) * sin
            scores = jnp.einsum('bhqd,bhkd->bhqk', q, k) / math.sqrt(HD)
            causal = jnp.tril(jnp.ones((s, s), bool))
            scores = jnp.where(causal[None, None], scores, jnp.finfo(jnp.float32).min)
            probs = jax.nn.softmax(scores.astype(jnp.float32), axis=-1).astype(q.dtype)
            out = jnp.einsum('bhqk,bhkd->bhqd', probs, v)
            out = out.transpose(0, 2, 1, 3).reshape(b, s, H * HD)
            return out @ wo + bo

        def _moe(h, w_gate, we1, be1, we2, be2):
            b, s, d = h.shape
            x = h.reshape(-1, d)
            t = x.shape[0]
            raw = jax.nn.softmax(x @ w_gate, axis=-1)
            top_vals, top_idx = jax.lax.top_k(raw, TOP_K)
            w = jax.nn.softmax(top_vals, axis=-1)
            comb = jnp.zeros((t, E), x.dtype).at[jnp.arange(t)[:, None], top_idx].add(w)
            hmid = jax.nn.gelu(jnp.einsum('td,edi->tei', x, we1) + be1[None], approximate=False)
            eout = jnp.einsum('tei,eid->ted', hmid, we2) + be2[None]
            out = jnp.einsum('te,ted->td', comb, eout)
            return out.reshape(b, s, d)
        key = jax.random.key(seed)
        ks = jax.random.split(key, 20)
        s = 0.02
        p = {'hidden_states': jax.random.normal(ks[0], (B, S, D), jnp.float32), 'wq': jax.random.normal(ks[1], (D, H * HD), jnp.float32) * s, 'bq': jnp.zeros((H * HD,), jnp.float32), 'wk': jax.random.normal(ks[2], (D, H * HD), jnp.float32) * s, 'bk': jnp.zeros((H * HD,), jnp.float32), 'wv': jax.random.normal(ks[3], (D, H * HD), jnp.float32) * s, 'bv': jnp.zeros((H * HD,), jnp.float32), 'wo': jax.random.normal(ks[4], (H * HD, D), jnp.float32) * s, 'bo': jnp.zeros((D,), jnp.float32), 'ln1_w': jnp.ones((D,), jnp.float32), 'ln1_b': jnp.zeros((D,), jnp.float32), 'ln2_w': jnp.ones((D,), jnp.float32), 'ln2_b': jnp.zeros((D,), jnp.float32), 'w_gate': jax.random.normal(ks[5], (D, E), jnp.float32) * s, 'we1': jax.random.normal(ks[6], (E, D, I), jnp.float32) * s, 'be1': jnp.zeros((E, I), jnp.float32), 'we2': jax.random.normal(ks[7], (E, I, D), jnp.float32) * s, 'be2': jnp.zeros((E, D), jnp.float32)}
        return p
    _L0_ffn_in = _L0_ffn_setup()
    _d = {'L0_attn_x': _L0_attn_in['x'], 'L0_attn_wq': _L0_attn_in['wq'], 'L0_attn_wk': _L0_attn_in['wk'], 'L0_attn_wv': _L0_attn_in['wv'], 'L0_attn_wo': _L0_attn_in['wo'], 'L0_attn_q_scale': _L0_attn_in['q_scale'], 'L0_attn_k_scale': _L0_attn_in['k_scale'], 'L0_ffn_wq': _L0_ffn_in['wq'], 'L0_ffn_bq': _L0_ffn_in['bq'], 'L0_ffn_wk': _L0_ffn_in['wk'], 'L0_ffn_bk': _L0_ffn_in['bk'], 'L0_ffn_wv': _L0_ffn_in['wv'], 'L0_ffn_bv': _L0_ffn_in['bv'], 'L0_ffn_wo': _L0_ffn_in['wo'], 'L0_ffn_bo': _L0_ffn_in['bo'], 'L0_ffn_ln1_w': _L0_ffn_in['ln1_w'], 'L0_ffn_ln1_b': _L0_ffn_in['ln1_b'], 'L0_ffn_ln2_w': _L0_ffn_in['ln2_w'], 'L0_ffn_ln2_b': _L0_ffn_in['ln2_b'], 'L0_ffn_w_gate': _L0_ffn_in['w_gate'], 'L0_ffn_we1': _L0_ffn_in['we1'], 'L0_ffn_be1': _L0_ffn_in['be1'], 'L0_ffn_we2': _L0_ffn_in['we2'], 'L0_ffn_be2': _L0_ffn_in['be2']}
    _x0 = _d['L0_attn_x']
    _d['L0_attn_x'] = jax.random.normal(jax.random.fold_in(jax.random.key(seed), 1), (8, 256, 256), dtype=_x0.dtype)
    del _x0
    return _d

def reference(L0_attn_x, L0_attn_wq, L0_attn_wk, L0_attn_wv, L0_attn_wo, L0_attn_q_scale, L0_attn_k_scale, L0_ffn_wq, L0_ffn_bq, L0_ffn_wk, L0_ffn_bk, L0_ffn_wv, L0_ffn_bv, L0_ffn_wo, L0_ffn_bo, L0_ffn_ln1_w, L0_ffn_ln1_b, L0_ffn_ln2_w, L0_ffn_ln2_b, L0_ffn_w_gate, L0_ffn_we1, L0_ffn_be1, L0_ffn_we2, L0_ffn_be2):

    def _L0_attn_ref(x, wq, wk, wv, wo, q_scale, k_scale):
        import jax, jax.numpy as jnp
        import numpy as np
        EPS = 1e-06

        def rms_norm(x, scale):
            x32 = x.astype(jnp.float32)
            mean2 = jnp.mean(jnp.square(x32), axis=-1, keepdims=True)
            return x32 * jax.lax.rsqrt(mean2 + EPS) * scale
        q = jnp.einsum('bse,ehd->bshd', x, wq)
        k = jnp.einsum('bse,ehd->bshd', x, wk)
        v = jnp.einsum('bse,ehd->bshd', x, wv)
        qn = rms_norm(q, q_scale)
        kn = rms_norm(k, k_scale)
        scores = jnp.einsum('bqhd,bkhd->bhqk', qn, kn)
        attn = jax.nn.softmax(scores, axis=-1)
        out = jnp.einsum('bhqk,bkhd->bqhd', attn, v)
        return jnp.einsum('bqhd,hde->bqe', out, wo)

    def _L0_ffn_ref(hidden_states, wq, bq, wk, bk, wv, bv, wo, bo, ln1_w, ln1_b, ln2_w, ln2_b, w_gate, we1, be1, we2, be2):
        import jax, jax.numpy as jnp
        import numpy as np
        import math
        B, S, D = (2, 256, 256)
        H, HD = (16, 128)
        E, I = (4, 256)
        TOP_K = 2
        ROPE_THETA = 10000.0

        def _layernorm(x, w, b):
            mu = jnp.mean(x, axis=-1, keepdims=True)
            var = jnp.mean(jnp.square(x - mu), axis=-1, keepdims=True)
            return (x - mu) * jax.lax.rsqrt(var + 1e-05) * w + b

        def _rotate_half(x):
            x1, x2 = jnp.split(x, 2, axis=-1)
            return jnp.concatenate((-x2, x1), axis=-1)

        def _attention(h, wq, bq, wk, bk, wv, bv, wo, bo):
            b, s, _ = h.shape
            q = (h @ wq + bq).reshape(b, s, H, HD).transpose(0, 2, 1, 3)
            k = (h @ wk + bk).reshape(b, s, H, HD).transpose(0, 2, 1, 3)
            v = (h @ wv + bv).reshape(b, s, H, HD).transpose(0, 2, 1, 3)
            inv_freq = 1.0 / ROPE_THETA ** (jnp.arange(0, HD, 2, dtype=jnp.float32) / HD)
            freqs = jnp.arange(s, dtype=jnp.float32)[:, None] * inv_freq[None, :]
            emb = jnp.concatenate((freqs, freqs), axis=-1)
            cos = jnp.cos(emb)[None, None]
            sin = jnp.sin(emb)[None, None]
            q = q * cos + _rotate_half(q) * sin
            k = k * cos + _rotate_half(k) * sin
            scores = jnp.einsum('bhqd,bhkd->bhqk', q, k) / math.sqrt(HD)
            causal = jnp.tril(jnp.ones((s, s), bool))
            scores = jnp.where(causal[None, None], scores, jnp.finfo(jnp.float32).min)
            probs = jax.nn.softmax(scores.astype(jnp.float32), axis=-1).astype(q.dtype)
            out = jnp.einsum('bhqk,bhkd->bhqd', probs, v)
            out = out.transpose(0, 2, 1, 3).reshape(b, s, H * HD)
            return out @ wo + bo

        def _moe(h, w_gate, we1, be1, we2, be2):
            b, s, d = h.shape
            x = h.reshape(-1, d)
            t = x.shape[0]
            raw = jax.nn.softmax(x @ w_gate, axis=-1)
            top_vals, top_idx = jax.lax.top_k(raw, TOP_K)
            w = jax.nn.softmax(top_vals, axis=-1)
            comb = jnp.zeros((t, E), x.dtype).at[jnp.arange(t)[:, None], top_idx].add(w)
            hmid = jax.nn.gelu(jnp.einsum('td,edi->tei', x, we1) + be1[None], approximate=False)
            eout = jnp.einsum('tei,eid->ted', hmid, we2) + be2[None]
            out = jnp.einsum('te,ted->td', comb, eout)
            return out.reshape(b, s, d)
        a = _attention(_layernorm(hidden_states, ln1_w, ln1_b), wq, bq, wk, bk, wv, bv, wo, bo)
        h = hidden_states + a
        m = _moe(_layernorm(h, ln2_w, ln2_b), w_gate, we1, be1, we2, be2)
        return h + m
    x = L0_attn_x
    x = x + _layernorm(_L0_attn_ref(_layernorm(x, axis=-1), L0_attn_wq, L0_attn_wk, L0_attn_wv, L0_attn_wo, L0_attn_q_scale, L0_attn_k_scale), axis=-1)
    x = x + _layernorm(_L0_ffn_ref(_layernorm(x, axis=-1), L0_ffn_wq, L0_ffn_bq, L0_ffn_wk, L0_ffn_bk, L0_ffn_wv, L0_ffn_bv, L0_ffn_wo, L0_ffn_bo, L0_ffn_ln1_w, L0_ffn_ln1_b, L0_ffn_ln2_w, L0_ffn_ln2_b, L0_ffn_w_gate, L0_ffn_we1, L0_ffn_be1, L0_ffn_we2, L0_ffn_be2), axis=-1)
    return x

_drawn_inputs = setup_inputs


def setup_inputs(seed=0):
    import zlib

    import numpy as np

    out = dict(_drawn_inputs(seed))
    spreads = {'L0_attn_q_scale': (1.0, 0.2),
     'L0_attn_k_scale': (1.0, 0.2),
     'L0_ffn_bq': (0.0, 0.8),
     'L0_ffn_bk': (0.0, 0.8),
     'L0_ffn_bv': (0.0, 0.1),
     'L0_ffn_bo': (0.0, 0.1),
     'L0_ffn_ln1_w': (1.0, 0.6),
     'L0_ffn_ln1_b': (0.0, 0.655),
     'L0_ffn_ln2_w': (1.0, 0.6),
     'L0_ffn_ln2_b': (0.0, 0.8),
     'L0_ffn_be1': (0.0, 0.8),
     'L0_ffn_be2': (0.0, 0.284)}
    factors = {'L0_ffn_wq': 8.0, 'L0_ffn_wk': 8.0, 'L0_ffn_we1': 3.358, 'L0_ffn_we2': 3.12}
    for name, (base, spread) in spreads.items():
        noise = np.random.default_rng([zlib.crc32(name.encode()), seed]).standard_normal(out[name].shape)
        drawn = base * np.exp(spread * noise) if base else spread * noise
        out[name] = jnp.asarray(drawn.astype(out[name].dtype))
    for name, factor in factors.items():
        out[name] = (out[name] * factor).astype(out[name].dtype)
    return out
```

```python
from contextlib import ExitStack

import numpy as np
import concourse.bass as bass
from concourse import mybir

F32 = mybir.dt.float32
F32R = mybir.dt.float32r
BF16 = mybir.dt.bfloat16
ALU = mybir.AluOpType
ACT = mybir.ActivationFunctionType
X = mybir.AxisListType.X

P = 128
NB, T, E = 8, 256, 256
H, D = 16, 128
GH = 4
NG = H // GH
NT, NE = T // P, E // P
UL = NG * NB
GW = GH * D
NX, IM = 4, 256
STEPS = 8
SLOTS = 2 * STEPS
NSTEP = (2 * NG + 1) * STEPS
AHEAD = STEPS + 1
LAG = UL - NB + 1
LN_EPS, RMS_EPS = 1e-5, 1e-6
PASSES = ((0, 0), (0, 1), (1, 0))


def build(nc, x, weights, qk_scale, bias_qk, bv, bo, ln1, ln2, w_gate, be1, be2, rope, masks, ident, out):
    x1_dram = nc.dram_tensor("x1_dram", (NB, P, NT, E), F32).ap()
    x_d = x.rearrange("b (t p) e -> b p t e", p=P)
    out_d = out.rearrange("b (t p) e -> b p t e", p=P)

    with ExitStack() as ctx:
        def sb(name, shape, dt=F32):
            return ctx.enter_context(nc.sbuf_tensor(name, [P, *shape], dt))

        def sem(name):
            return ctx.enter_context(nc.semaphore(name))

        w_part = [sb("w_high", [SLOTS * GW], F32R), sb("w_low", [SLOTS * GW], F32R)]
        w_stage = sb("w_stage", [2 * GW])
        xT_part = [sb("xT_high", [NB, NE, T], F32R), sb("xT_low", [NB, NE, T], F32R)]
        xq_part = [sb("xq_high", [NE, T], F32R), sb("xq_low", [NE, T], F32R)]
        xv_part = [sb("xv_high", [NE, T], F32R), sb("xv_low", [NE, T], F32R)]
        y = sb("y", [NB, NT, E])
        bias_sb = sb("bias_sb", [2, 2 * GW])
        qk = sb("qk", [4, GW])
        scratch = sb("scratch", [2, GW])
        rot_a = sb("rot_a", [2, GW])
        rot_b = sb("rot_b", [2, GW])
        sumsq = sb("sumsq", [4, GH])
        meansq = sb("meansq", [4, GH])
        rstd_qk = sb("rstd_qk", [4, GH])
        qkT = sb("qkT", [2, GH, T])
        v = sb("v", [NT, GW])
        probs = sb("probs", [GH, NT, T])
        neg_max = sb("neg_max", [GH, NT])
        row_sum = sb("row_sum", [GH, NT])
        inv_sum = sb("inv_sum", [GH, NT])
        probsT = sb("probsT", [2, NT, T])
        oT_part = [sb("oT_high", [GH, T], F32R), sb("oT_low", [GH, T], F32R)]
        res = sb("res", [NT, E])
        xn = sb("xn", [NT, E])
        xT_full = sb("xT_full", [NE, T])
        stats = sb("stats", [NT, 6])
        mean_var = sb("mean_var", [NT, 2])
        var_eps = sb("var_eps", [NT])
        rstd = sb("rstd", [NT])
        minus_half = sb("minus_half", [16])
        eps_sum = sb("eps_sum", [GH])
        pause = sb("pause", [1])
        ident_sb = sb("ident_sb", [P])
        mask_sb = sb("mask_sb", [2, P], BF16)
        rope_sb = sb("rope_sb", [2, NT, D])
        qk_scale_sb = sb("qk_scale_sb", [2])
        qk_root_sb = sb("qk_root_sb", [2])
        bv_sb = sb("bv_sb", [H])
        bo_sb = sb("bo_sb", [E])
        ln_sb = sb("ln_sb", [2, 2, NE])
        w_gate_sb = sb("w_gate_sb", [NE, NX])
        logits = sb("logits", [NB * NT, NX])
        be1_sb = sb("be1_sb", [NX * NE])
        gate = [sb(f"gate{i}", [NB * NT, NX]) for i in range(3)]
        gate_1 = [sb(f"gate_1{i}", [NB * NT]) for i in range(4)]
        beats = sb("beats", [NB * NT, NX, NX])
        comb_tg = sb("comb_tg", [2 * NT, NX])
        gelu_full = [scratch[:, i, :] for i in range(2)]
        gelu_part = [w[:, STEPS * GW:(STEPS + 4) * GW].rearrange("p (s c) -> p s c", s=4) for w in w_part]
        acc = qk[:, :, 0:GW].rearrange("p a (t e) -> p a t e", t=NT)
        be2_sb = probs[:, :, :, :].rearrange("p a b c -> p (a b c)")[:, 0:NX * E].rearrange("p (x e) -> p x e", x=NX)

        def bank(name):
            return ctx.enter_context(nc.psum_tensor(name, [P, 512], F32))
        ps_proj = [bank("ps_proj0"), bank("ps_proj1")]
        ps_tr = [bank("ps_tr0"), bank("ps_tr1")]
        ps_s = [bank("ps_s0"), bank("ps_s1")]
        ps_o = bank("ps_o")
        ps_y = bank("ps_y")

        const_in = sem("const_in")
        half_set = sem("half_set")
        root_set = sem("root_set")
        w_in = sem("w_in")
        w_high_done = sem("w_high_done")
        w_split = sem("w_split")
        bias_in = sem("bias_in")
        xq_in = sem("xq_in")
        xv_in = sem("xv_in")
        proj_done = sem("proj_done")
        sq_done = sem("sq_done")
        sumsq_done = sem("sumsq_done")
        meansq_done = sem("meansq_done")
        rstd_qk_done = sem("rstd_qk_done")
        qk_biased = sem("qk_biased")
        rot_a_done = sem("rot_a_done")
        rot_b_done = sem("rot_b_done")
        qk_ready = sem("qk_ready")
        v_copied = sem("v_copied")
        tr_done = sem("tr_done")
        qkT_copied = sem("qkT_copied")
        s_done = sem("s_done")
        max_done = sem("max_done")
        exp_done = sem("exp_done")
        inv_done = sem("inv_done")
        probs_done = sem("probs_done")
        probsT_copied = sem("probsT_copied")
        pv_done = sem("pv_done")
        o_high_done = sem("o_high_done")
        o_low_done = sem("o_low_done")
        y_done = sem("y_done")
        y_added = sem("y_added")
        res_in = sem("res_in")
        res_free = sem("res_free")
        x1_ready = sem("x1_ready")
        x1_out = sem("x1_out")
        ln_stats = sem("ln_stats")
        ln_aggr = sem("ln_aggr")
        ln_var = sem("ln_var")
        ln_rstd = sem("ln_rstd")
        ln_done = sem("ln_done")
        h0_done = sem("h0_done")
        z_done = sem("z_done")
        xn_ready = sem("xn_ready")
        xT_done = sem("xT_done")
        xT_copied = sem("xT_copied")
        xT_high_done = sem("xT_high_done")
        xT_ready = sem("xT_ready")
        logits_done = sem("logits_done")
        logits_copied = sem("logits_copied")
        gate_step = sem("gate_step")
        gate_exp = sem("gate_exp")
        be2_in = sem("be2_in")
        be2_may_load = sem("be2_may_load")
        h1_done = sem("h1_done")
        gelu_done = sem("gelu_done")
        gelu_high_done = sem("gelu_high_done")
        gelu_low_done = sem("gelu_low_done")
        moe_done = sem("moe_done")
        moe_added = sem("moe_added")
        comb_set = sem("comb_set")
        acc_step = sem("acc_step")
        out_ready = sem("out_ready")
        out_stored = sem("out_stored")

        block = ctx.enter_context(nc.Block())

        N_CONST = 13

        def w_cols(unit, step, lo, n, part):
            group = unit // NB
            return w_part[part][:, bass.ds((group % 2) * (STEPS * GW) + step * GW + lo, n)]

        def seq(unit):
            return unit % NB

        @block.sync
        def _(sp):
            for dst, src in ((ident_sb[:], ident), (mask_sb[:], masks), (rope_sb[:], rope),
                             (qk_scale_sb[:], qk_scale), (bv_sb[:], bv), (bo_sb[:], bo.partition_broadcast(P)),
                             (ln_sb[:, 0], ln1), (ln_sb[:, 1], ln2), (w_gate_sb[:], w_gate), (be1_sb[:], be1)):
                sp.dma_start(dst, src).then_inc(const_in, 16)

            def load_weight(s):
                if not isinstance(s, int) or s >= 2:
                    sp.wait_ge(w_split, s - 1)
                if not isinstance(s, int) or s >= 1:
                    sp.wait_ge(w_in, 16 * s)
                sp.dma_start(w_stage[:, bass.ds((s % 2) * GW, GW)],
                             weights[bass.ds(s, 1)].rearrange("s p c -> p (s c)")).then_inc(w_in, 16)

            def load_xq(V):
                for part in range(2):
                    sp.dma_start(xq_part[part][:].bitcast(F32), xT_part[part][:, bass.ds(seq(V), 1)]
                                 .rearrange("p b c t -> p (b c) t").bitcast(F32)).then_inc(xq_in, 16)

            def load_xv(V):
                for part in range(2):
                    sp.dma_start(xv_part[part][:].bitcast(F32), xT_part[part][:, bass.ds(seq(V), 1)]
                                 .rearrange("p b c t -> p (b c) t").bitcast(F32)).then_inc(xv_in, 16)

            def load_bias(g):
                sp.dma_start(bias_sb[:, g % 2, :], bias_qk[g:g + 1, :].rearrange("g c -> (g c)")
                             .partition_broadcast(P)).then_inc(bias_in, 16)

            sp.dma_start(res[:], x_d[0]).then_inc(res_in, 16)
            for s in range(2):
                load_weight(s)
            for b in range(1, NB):
                sp.wait_ge(res_free, b)
                sp.dma_start(res[:], x_d[b]).then_inc(res_in, 16)
                load_weight(b + 1)
            sp.wait_ge(xT_ready, 1)
            load_xq(0)
            load_xv(0)
            sp.wait_ge(proj_done, 4)
            sp.wait_ge(xT_ready, NB)
            load_xq(1)

            def unit(U, last=False):
                V = U + 1
                if not last:
                    sp.wait_ge(proj_done, 6 * U + 6)
                    load_xv(V)
                    load_weight(U + AHEAD)
                    if not (isinstance(V, int) and V == 2 * UL - 1):
                        sp.wait_ge(proj_done, 6 * V + 4)
                        load_xq(V + 1)

            def first_epilogue(b):
                sp.wait_ge(res_free, b + NB)
                sp.wait_ge(x1_out, 16 * b)
                sp.dma_start(res[:], x_d[bass.ds(b, 1)].rearrange("b p t e -> p (b t) e")).then_inc(res_in, 16)

            def store_x1(b):
                sp.wait_ge(x1_ready, b + 1)
                sp.dma_start(x1_dram[bass.ds(b, 1)].rearrange("b p t e -> p (b t) e"), res[:]).then_inc(x1_out, 16)

            with sp.Fori(0, LAG) as U:
                unit(U)
            with sp.Fori(LAG, UL - 1) as U:
                first_epilogue(U - LAG)
                store_x1(U - LAG)
                unit(U)
            for g in range(2):
                load_bias(g)
            first_epilogue(NB - 2)
            store_x1(NB - 2)
            sp.wait_ge(xT_ready, NB + 2)
            unit(UL - 1)
            first_epilogue(NB - 1)
            store_x1(NB - 1)
            sp.wait_ge(xT_ready, 2 * NB)
            for g in range(NG - 1):
                with sp.Fori(UL + g * NB, UL + (g + 1) * NB) as U:
                    unit(U)
                if g + 2 < NG:
                    sp.wait_ge(qk_biased, 4 * (g + 1) * NB)
                    load_bias(g + 2)
            with sp.Fori(UL + 3 * NB, 2 * UL - 2) as U:
                unit(U)
            unit(2 * UL - 2)

            sp.wait_ge(be2_may_load, 1)
            sp.dma_start(be2_sb, be2.partition_broadcast(P).rearrange("p (x e) -> p x e", x=NX)).then_inc(be2_in, 16)
            with sp.Fori(0, NB) as b:
                sp.wait_ge(res_free, b + 2 * NB)
                sp.dma_start(res[:], x1_dram[bass.ds(b, 1)].rearrange("b p t e -> p (b t) e")).then_inc(res_in, 16)
                sp.wait_ge(out_ready, b + 1)
                sp.dma_start(out_d[bass.ds(b, 1)].rearrange("b p t e -> p (b t) e"), xn[:]).then_inc(out_stored, 16)
            sp.wait_ge(x1_out, 16 * NB)
            sp.wait_ge(out_stored, 16 * NB)

        @block.gpsimd
        def _(pool):
            pool.memset(minus_half[:], -0.5)
            pool.memset(eps_sum[:], D * RMS_EPS).then_inc(half_set, 1)
            pool.wait_ge(half_set, 1)

            def split_weight(s):
                src = w_stage[:, bass.ds((s % 2) * GW, GW)]
                high = w_part[0][:, bass.ds((s % SLOTS) * GW, GW)]
                low = w_part[1][:, bass.ds((s % SLOTS) * GW, GW)]
                pool.wait_ge(w_in, 16 * s + 16)
                pool.tensor_copy(high, src).then_inc(w_high_done, 1)
                pool.wait_ge(w_high_done, s + 1)
                pool.tensor_tensor(low, src, high.bitcast(F32), ALU.subtract).then_inc(w_split, 1)

            def ln_power(k):
                pool.wait_ge(ln_var, k + 1)
                pool.tensor_tensor(rstd[:], var_eps[:], minus_half[:, 0:NT], ALU.pow).then_inc(ln_rstd, 1)

            def rms_power(V, i):
                pool.wait_ge(sumsq_done, 4 * V + i + 1)
                pool.tensor_tensor(meansq[:, i], sumsq[:, i], eps_sum[:], ALU.add).then_inc(meansq_done, 1)
                pool.wait_ge(meansq_done, 4 * V + i + 1)
                pool.tensor_tensor(rstd_qk[:, i], meansq[:, i], minus_half[:, 0:GH], ALU.pow).then_inc(rstd_qk_done, 1)

            def rotate_a(V, i):
                n = 4 * (V - UL) + i
                pool.wait_ge(qk_biased, n + 1)
                if not isinstance(V, int) or V > UL or i >= 2:
                    pool.wait_ge(qk_ready, 4 * V + i - 1)
                cos = rope_sb[:, 0, i % 2].unsqueeze(1).to_broadcast([P, GH, D])
                pool.tensor_tensor(rot_a[:, i % 2].rearrange("p (h d) -> p h d", h=GH),
                                   scratch[:, i % 2].rearrange("p (h d) -> p h d", h=GH), cos,
                                   ALU.mult).then_inc(rot_a_done, 1)

            def qk_part(V, layer):
                for i in range(4):
                    rms_power(V, i) if layer == 0 else rotate_a(V, i)

            def split_ahead(U):
                pool.wait_ge(proj_done, 6 * U + 6)
                pool.wait_ge(y_done, U)
                split_weight(U + AHEAD)

            for s in range(2):
                split_weight(s)
            for b in range(NB):
                ln_power(b)
                if b + 2 < AHEAD:
                    split_weight(b + 2)
            qk_part(0, 0)
            with pool.Fori(0, LAG) as U:
                qk_part(U + 1, 0)
                split_ahead(U)
            with pool.Fori(LAG, UL - 1) as U:
                for j in range(3):
                    ln_power(NB + 3 * (U - LAG) + j)
                qk_part(U + 1, 0)
                split_ahead(U)
            for j in range(3):
                ln_power(NB + 3 * (NB - 2) + j)
            qk_part(UL, 1)
            split_ahead(UL - 1)
            for j in range(3):
                ln_power(NB + 3 * (NB - 1) + j)
            with pool.Fori(UL, UL + LAG) as U:
                qk_part(U + 1, 1)
                split_ahead(U)
            with pool.Fori(UL + LAG, 2 * UL - 1) as U:
                ln_power(4 * NB + U - UL - LAG)
                qk_part(U + 1, 1)
                split_ahead(U)
            for j in range(2):
                ln_power(5 * NB - 2 + j)
            with pool.Fori(0, NB) as b:
                ln_power(5 * NB + b)

        @block.scalar
        def _(act):
            act.wait_ge(const_in, 16 * 10)
            act.activation(qk_root_sb[:], qk_scale_sb[:], ACT.Copy, scale=float(D) ** 0.5).then_inc(root_set, 1)
            act.wait_ge(root_set, 1)

            def copy_qkT(U, j, layer):
                which, pair = j % 2, j // 2
                act.wait_ge(tr_done, 8 * U + j + 1)
                dst = qkT[:, which, 2 * pair:2 * pair + 2].rearrange("p h t -> p (h t)")
                if layer == 0:
                    scale = qk_root_sb[:, which:which + 1]
                else:
                    scale = float(D) ** -0.5 if which == 0 else 1.0
                act.activation(dst, ps_tr[j % 2][:], ACT.Copy, scale=scale).then_inc(qkT_copied, 1)

            def square(V, i):
                act.wait_ge(proj_done, 6 * V + i + 1)
                if i >= 2:
                    act.wait_ge(sumsq_done, 4 * V + i - 1)
                else:
                    act.wait_ge(sumsq_done, 4 * V)
                act.activation(scratch[:, i % 2], ps_proj[i % 2][:], ACT.Square).then_inc(sq_done, 1)

            def exp_head(U, h, layer):
                act.wait_ge(max_done, 4 * U + h + 1)
                for t in range(NT):
                    n = T if layer == 0 or t else P
                    last = act.activation(probs[:, h, t, 0:n], ps_s[h % 2][:, t * T:t * T + n], ACT.Exp,
                                          bias=neg_max[:, h, t:t + 1], accum_out=row_sum[:, h, t:t + 1])
                last.then_inc(exp_done, 1)

            def copy_v(U, t, V):
                act.wait_ge(proj_done, 6 * V + 5 + t)
                if t == 0:
                    act.wait_ge(pv_done, 4 * U + 4)
                act.activation(v[:, t], ps_proj[t][:], ACT.Copy).then_inc(v_copied, 1)

            def o_high(U, pair, layer):
                act.wait_ge(pv_done, 4 * U + 2 * pair + 2)
                for h in range(2):
                    bias = 0.0 if layer == 0 else bv_sb[:, bass.ds(((U - UL) // NB) * GH + 2 * pair + h, 1)]
                    if layer == 0:
                        if h == 0:
                            last = act.activation(oT_part[0][:, 2 * pair:2 * pair + 2].rearrange("p h t -> p (h t)"),
                                                  ps_o[:], ACT.Copy)
                    else:
                        last = act.activation(oT_part[0][:, 2 * pair + h], ps_o[:, h * T:(h + 1) * T], ACT.Identity, bias=bias)
                last.then_inc(o_high_done, 1)

            def xT_out(n, b, which):
                act.wait_ge(xT_done, n + 1)
                for c in range(NE):
                    src = ps_s[0][:, c * T:(c + 1) * T]
                    if which is None:
                        last = act.activation(xT_full[:, c], src, ACT.Copy)
                    else:
                        last = act.activation(xT_full[:, c], src, ACT.Identity, bias=ln_sb[:, which, 1, c:c + 1],
                                              scale=ln_sb[:, which, 0, c:c + 1])
                last.then_inc(xT_copied, 1)
                act.wait_ge(xT_copied, n + 1)
                act.activation(xT_part[0][:, bass.ds(b, 1)].rearrange("p b c t -> p (b c t)"),
                               xT_full[:].rearrange("p c t -> p (c t)"), ACT.Copy).then_inc(xT_high_done, 1)

            def unit(U, layer, next_layer):
                V = U + 1
                for j in range(4):
                    copy_qkT(U, j, layer)
                if next_layer == 0:
                    square(V, 0)
                    square(V, 1)
                exp_head(U, 0, layer)
                exp_head(U, 1, layer)
                if next_layer == 0:
                    square(V, 2)
                exp_head(U, 2, layer)
                if next_layer == 0:
                    square(V, 3)
                exp_head(U, 3, layer)
                o_high(U, 0, layer)
                o_high(U, 1, layer)
                if next_layer is not None:
                    copy_v(U, 0, V)
                    copy_v(U, 1, V)

            with act.Fori(0, 1) as b:
                xT_out(b, b, None)
            with act.Fori(1, NB) as b:
                xT_out(b, b, None)
            for i in range(4):
                square(0, i)
            for t in range(NT):
                act.wait_ge(proj_done, 5 + t)
                act.activation(v[:, t], ps_proj[t][:], ACT.Copy).then_inc(v_copied, 1)
            with act.Fori(0, LAG) as U:
                unit(U, 0, 0)
            with act.Fori(LAG, UL - 1) as U:
                unit(U, 0, 0)
                xT_out(U - LAG + NB, U - LAG, 0)
            unit(UL - 1, 0, 1)
            for b in (NB - 2, NB - 1):
                xT_out(NB + b, b, 0)
            with act.Fori(UL, UL + LAG) as U:
                unit(U, 1, 1)
            with act.Fori(UL + LAG, 2 * UL - 1) as U:
                unit(U, 1, 1)
                xT_out(U - UL - LAG + 2 * NB, U - UL - LAG, 1)
            unit(2 * UL - 1, 1, None)
            for b in (NB - 2, NB - 1):
                xT_out(2 * NB + b, b, 1)

            for k in range(2):
                act.wait_ge(gate_step, (2, 13)[k])
                act.activation(gate[(1, 2)[k]][:], gate[0][:], ACT.Exp).then_inc(gate_exp, 1)
            with act.Fori(0, NB // 2) as g:
                for m in range(8):
                    act.wait_ge(h1_done, 8 * g + m + 1)
                    if m >= 2:
                        act.wait_ge(gelu_low_done, 8 * g + m - 1)
                    else:
                        act.wait_ge(gelu_low_done, 8 * g)
                    act.activation(gelu_full[m % 2], ps_proj[m % 2][:], ACT.Gelu,
                                   bias=be1_sb[:, m:m + 1]).then_inc(gelu_done, 1)
                    act.wait_ge(gelu_done, 8 * g + m + 1)
                    act.wait_ge(moe_done, 8 * g + (2 * (m // 2) - 2 if m >= 4 else 0))
                    act.activation(gelu_part[0][:, m % 4], gelu_full[m % 2], ACT.Copy).then_inc(gelu_high_done, 1)

        @block.vector
        def _(dve):
            def layer_norm(src, dst, k):
                for t in range(NT):
                    last = dve.bn_stats(stats[:, t], src(t))
                last.then_inc(ln_stats, 1)
                dve.wait_ge(ln_stats, k + 1)
                dve.memset(pause[:], 0.0)
                for t in range(NT):
                    last = dve.bn_aggr(mean_var[:, t], stats[:, t])
                last.then_inc(ln_aggr, 1)
                dve.wait_ge(ln_aggr, k + 1)
                dve.tensor_scalar(var_eps[:], mean_var[:, :, 1], LN_EPS, None, ALU.add).then_inc(ln_var, 1)
                dve.wait_ge(ln_rstd, k + 1)
                for t in range(NT):
                    last = dve.tensor_scalar(dst(t), src(t), mean_var[:, t, 0:1], rstd[:, t:t + 1], ALU.subtract, ALU.mult)
                return last

            def y_tile(b):
                return lambda t: y[:, bass.ds(b, 1), t].rearrange("p b e -> p (b e)")

            def tile_of(buf):
                return lambda t: buf[:, t]

            def xT_low(n, b):
                low = xT_part[1][:, bass.ds(b, 1)].rearrange("p b c t -> p (b c t)")
                high = xT_part[0][:, bass.ds(b, 1)].rearrange("p b c t -> p (b c t)").bitcast(F32)
                dve.wait_ge(xT_high_done, n + 1)
                dve.tensor_tensor(low, xT_full[:].rearrange("p c t -> p (c t)"), high, ALU.subtract).then_inc(xT_ready, 1)

            def sum_squares(V, i):
                dve.wait_ge(sq_done, 4 * V + i + 1)
                dve.tensor_reduce(sumsq[:, i], scratch[:, i % 2].rearrange("p (h d) -> p h d", h=GH),
                                  axis=X, op=ALU.add).then_inc(sumsq_done, 1)

            def scale_qk(V, i):
                dve.wait_ge(rstd_qk_done, 4 * V + i + 1)
                if i == 0:
                    dve.wait_ge(tr_done, 8 * V - 4)
                dve.tensor_tensor(qk[:, i].rearrange("p (h d) -> p h d", h=GH),
                                  ps_proj[i % 2][:].rearrange("p (h d) -> p h d", h=GH),
                                  rstd_qk[:, i].unsqueeze(2).to_broadcast([P, GH, D]), ALU.mult).then_inc(qk_ready, 1)

            def add_bias(V, i):
                n = 4 * (V - UL) + i
                dve.wait_ge(proj_done, 6 * V + i + 1)
                if not isinstance(V, int) or V > UL or i >= 2:
                    dve.wait_ge(rot_a_done, n - 1)
                bias = bias_sb[:].rearrange("p g c -> p (g c)")[
                    :, bass.ds((((V - UL) // NB) % 2) * (2 * GW) + (i // 2) * GW, GW)]
                dve.tensor_tensor(scratch[:, i % 2], ps_proj[i % 2][:], bias, ALU.add).then_inc(qk_biased, 1)

            def rotate_b(V, i):
                n = 4 * (V - UL) + i
                dve.wait_ge(qk_biased, n + 1)
                swapped = scratch[:, i % 2].rearrange("p (h s d) -> p h s d", h=GH, s=2)[:, :, ::-1, :]
                sin = rope_sb[:, 1, i % 2].rearrange("p (s d) -> p s d", s=2).unsqueeze(1).to_broadcast([P, GH, 2, D // 2])
                dve.tensor_tensor(rot_b[:, i % 2].rearrange("p (h s d) -> p h s d", h=GH, s=2), swapped, sin,
                                  ALU.mult).then_inc(rot_b_done, 1)

            def rotate_sum(V, i):
                n = 4 * (V - UL) + i
                dve.wait_ge(rot_a_done, n + 1)
                dve.wait_ge(rot_b_done, n + 1)
                if i == 0:
                    dve.wait_ge(tr_done, 8 * V - 4)
                dve.tensor_tensor(qk[:, i], rot_a[:, i % 2], rot_b[:, i % 2], ALU.add).then_inc(qk_ready, 1)

            def row_max(U, h, layer):
                dve.wait_ge(s_done, 4 * U + h + 1)
                if layer == 0:
                    last = dve.tensor_reduce(neg_max[:, h], ps_s[h % 2][:].rearrange("p (t k) -> p t k", t=NT),
                                             axis=X, op=ALU.max, negate=True)
                else:
                    dve.tensor_reduce(neg_max[:, h, 0:1], ps_s[h % 2][:, 0:P], axis=X, op=ALU.max, negate=True)
                    last = dve.tensor_reduce(neg_max[:, h, 1:2], ps_s[h % 2][:, T:2 * T], axis=X, op=ALU.max, negate=True)
                last.then_inc(max_done, 1)

            def normalise(U, h, layer):
                dve.wait_ge(exp_done, 4 * U + h + 1)
                dve.reciprocal(inv_sum[:, h], row_sum[:, h]).then_inc(inv_done, 1)
                dve.wait_ge(inv_done, 4 * U + h + 1)
                for t in range(NT):
                    n = T if layer == 0 or t else P
                    last = dve.tensor_scalar(probs[:, h, t, 0:n], probs[:, h, t, 0:n], inv_sum[:, h, t:t + 1], None, ALU.mult)
                last.then_inc(probs_done, 1)

            def copy_probsT(U, h, layer):
                dve.wait_ge(tr_done, 8 * U + 5 + h)
                dst = probsT[:, h % 2].rearrange("p k q -> p (k q)")
                if layer == 0:
                    last = dve.tensor_copy(dst, ps_tr[h % 2][:])
                else:
                    dve.tensor_copy(dst[:, 0:T], ps_tr[h % 2][:, 0:T])
                    last = dve.tensor_copy(dst[:, T + P:2 * T], ps_tr[h % 2][:, T + P:2 * T])
                last.then_inc(probsT_copied, 1)

            def o_low(U, pair, layer):
                dve.wait_ge(o_high_done, 2 * U + pair + 1)
                if layer == 0:
                    last = dve.tensor_tensor(oT_part[1][:, 2 * pair:2 * pair + 2].rearrange("p h t -> p (h t)"), ps_o[:],
                                             oT_part[0][:, 2 * pair:2 * pair + 2].rearrange("p h t -> p (h t)").bitcast(F32),
                                             ALU.subtract)
                else:
                    for h in range(2):
                        bias = bv_sb[:, bass.ds(((U - UL) // NB) * GH + 2 * pair + h, 1)]
                        last = dve.scalar_tensor_tensor(oT_part[1][:, 2 * pair + h], ps_o[:, h * T:(h + 1) * T], bias,
                                                        oT_part[0][:, 2 * pair + h].bitcast(F32), ALU.add, ALU.subtract)
                last.then_inc(o_low_done, 1)

            def add_y(U):
                dve.wait_ge(y_done, U + 1)
                y_b = y[:, bass.ds(seq(U), 1)].rearrange("p b t e -> p (b t e)")
                dve.tensor_tensor(y_b, ps_y[:], y_b, ALU.add).then_inc(y_added, 1)

            def epilogue_1(b):
                k = NB + 3 * b
                dve.wait_ge(y_added, UL - NB + b + 1)
                layer_norm(y_tile(b), tile_of(xn), k).then_inc(z_done, 1)
                dve.wait_ge(z_done, b + 1)
                dve.wait_ge(res_in, 16 * (NB + b) + 16)
                dve.tensor_tensor(res[:].rearrange("p t e -> p (t e)"), res[:].rearrange("p t e -> p (t e)"),
                                  xn[:].rearrange("p t e -> p (t e)"), ALU.add).then_inc(x1_ready, 1)
                dve.wait_ge(x1_ready, b + 1)
                layer_norm(tile_of(res), tile_of(xn), k + 1).then_inc(h0_done, 1)
                dve.wait_ge(h0_done, b + 1)
                for t in range(NT):
                    last = dve.tensor_tensor(y_tile(b)(t), xn[:, t], bo_sb[:], ALU.add)
                layer_norm(tile_of(xn), tile_of(xn), k + 2).then_inc(xn_ready, 1)
                dve.sem_inc(res_free, 1)

            def epilogue_2(b):
                dve.wait_ge(y_added, 2 * UL - NB + b + 1)
                layer_norm(y_tile(b), tile_of(xn), 4 * NB + b).then_inc(xn_ready, 1)

            def copy_logits(b):
                dve.wait_ge(logits_done, b + 1)
                dve.tensor_copy(logits[:, bass.ds(b * NT, NT)].rearrange("p t x -> p (t x)"),
                                ps_s[1][:, 0:NT * NX]).then_inc(logits_copied, 1)

            def qk_first(V, i, layer):
                if layer == 0:
                    sum_squares(V, i)
                elif layer == 1:
                    add_bias(V, i)
                    rotate_b(V, i)

            def qk_last(V, i, layer):
                if layer == 0:
                    scale_qk(V, i)
                elif layer == 1:
                    rotate_sum(V, i)

            def unit(U, layer, nl):
                V = U + 1
                qk_first(V, 0, nl)
                qk_first(V, 1, nl)
                row_max(U, 0, layer)
                qk_last(V, 0, nl)
                row_max(U, 1, layer)
                qk_last(V, 1, nl)
                normalise(U, 0, layer)
                qk_first(V, 2, nl)
                row_max(U, 2, layer)
                normalise(U, 1, layer)
                copy_probsT(U, 0, layer)
                qk_last(V, 2, nl)
                qk_first(V, 3, nl)
                normalise(U, 2, layer)
                row_max(U, 3, layer)
                copy_probsT(U, 1, layer)
                copy_probsT(U, 2, layer)
                qk_last(V, 3, nl)
                normalise(U, 3, layer)
                o_low(U, 0, layer)
                copy_probsT(U, 3, layer)
                o_low(U, 1, layer)
                add_y(U)

            dve.memset(y[:], 0.0)
            for b in range(NB):
                dve.wait_ge(res_in, 16 * b + 16)
                if b:
                    dve.wait_ge(xT_done, b)
                layer_norm(tile_of(res), tile_of(xn), b).then_inc(xn_ready, 1)
                dve.wait_ge(xn_ready, b + 1)
                dve.sem_inc(res_free, 1)
                xT_low(b, b)
            for i in range(4):
                sum_squares(0, i)
                dve.wait_ge(rstd_qk_done, i + 1)
                dve.tensor_tensor(qk[:, i].rearrange("p (h d) -> p h d", h=GH),
                                  ps_proj[i % 2][:].rearrange("p (h d) -> p h d", h=GH),
                                  rstd_qk[:, i].unsqueeze(2).to_broadcast([P, GH, D]), ALU.mult).then_inc(qk_ready, 1)
            dve.wait_ge(const_in, 16 * 10)
            with dve.Fori(0, LAG) as U:
                unit(U, 0, 0)
            with dve.Fori(LAG, UL - 1) as U:
                epilogue_1(U - LAG)
                unit(U, 0, 0)
                xT_low(U - LAG + NB, U - LAG)
            epilogue_1(NB - 2)
            dve.wait_ge(bias_in, 32)
            unit(UL - 1, 0, 1)
            xT_low(2 * NB - 2, NB - 2)
            epilogue_1(NB - 1)
            xT_low(2 * NB - 1, NB - 1)
            for g in range(NG - 1):
                with dve.Fori(UL + g * NB, UL + (g + 1) * NB - 1) as U:
                    unit(U, 1, 1)
                dve.wait_ge(bias_in, 16 * (g + 2))
                unit(UL + (g + 1) * NB - 1, 1, 1)
            unit(UL + LAG - 1, 1, 1)
            with dve.Fori(UL + LAG, 2 * UL - 1) as U:
                epilogue_2(U - UL - LAG)
                unit(U, 1, 1)
                xT_low(U - UL - LAG + 2 * NB, U - UL - LAG)
                copy_logits(U - UL - LAG)
            epilogue_2(NB - 2)
            unit(2 * UL - 1, 1, None)
            dve.wait_ge(pv_done, 8 * UL)
            dve.sem_inc(be2_may_load, 1)
            xT_low(3 * NB - 2, NB - 2)
            copy_logits(NB - 2)
            epilogue_2(NB - 1)
            xT_low(3 * NB - 1, NB - 1)
            copy_logits(NB - 1)

            steps = [0]

            def link(instruction):
                steps[0] += 1
                instruction.then_inc(gate_step, 1)
                dve.wait_ge(gate_step, steps[0])

            shape = [P, NB * NT, NX]
            dve.wait_ge(logits_copied, NB)
            link(dve.tensor_reduce(gate_1[0][:], logits[:], axis=X, op=ALU.max))
            link(dve.tensor_tensor(gate[0][:], logits[:], gate_1[0][:].unsqueeze(2).to_broadcast(shape), ALU.subtract))
            dve.wait_ge(gate_exp, 1)
            link(dve.tensor_reduce(gate_1[0][:], gate[1][:], axis=X, op=ALU.add))
            link(dve.reciprocal(gate_1[1][:], gate_1[0][:]))
            raw = gate[1]
            link(dve.tensor_tensor(raw[:], gate[1][:], gate_1[1][:].unsqueeze(2).to_broadcast(shape), ALU.mult))
            link(dve.memset(beats[:], 0.0))
            for j in range(NX):
                for lo, hi, op in ((0, j, ALU.is_gt), (j + 1, NX, ALU.is_ge)):
                    if hi > lo:
                        last = dve.tensor_tensor(beats[:, :, j, lo:hi],
                                                 raw[:, :, j:j + 1].to_broadcast([P, NB * NT, hi - lo]),
                                                 raw[:, :, lo:hi], op)
            link(last)
            link(dve.tensor_reduce(gate[2][:], beats[:].rearrange("p t j e -> p t e j"), axis=X, op=ALU.add))
            link(dve.tensor_scalar(gate[2][:], gate[2][:], 1.5, None, ALU.is_lt))
            chosen = gate[2]
            link(dve.tensor_copy(beats[:, :, 0], chosen[:]))
            link(dve.tensor_reduce(gate_1[2][:], raw[:], axis=X, op=ALU.max))
            link(dve.memset(gate_1[3][:], 0.0))
            link(dve.tensor_tensor(gate[0][:], raw[:], gate_1[2][:].unsqueeze(2).to_broadcast(shape), ALU.subtract))
            dve.wait_ge(gate_exp, 2)
            link(dve.tensor_tensor(gate[0][:], gate[2][:], beats[:, :, 0], ALU.mult))
            link(dve.tensor_reduce(gate_1[0][:], gate[0][:], axis=X, op=ALU.add))
            link(dve.reciprocal(gate_1[1][:], gate_1[0][:]))
            link(dve.tensor_tensor(gate[0][:], gate[0][:], gate_1[1][:].unsqueeze(2).to_broadcast(shape), ALU.mult))
            comb = gate[0]
            dve.wait_ge(be2_in, 16)

            with dve.Fori(0, NB // 2) as g:
                dve.tensor_copy(comb_tg[:], comb[:, bass.ds(4 * g, 4)]).then_inc(comb_set, 1)
                dve.wait_ge(comb_set, g + 1)
                for e in range(NX):
                    for t in range(4):
                        prev = y[:, bass.ds(2 * g + t // 2, 1), t % 2].rearrange("p b e -> p (b e)") if e == 0 \
                            else acc[:, t // 2, t % 2]
                        last = dve.scalar_tensor_tensor(acc[:, t // 2, t % 2], be2_sb[:, e], comb_tg[:, t, e:e + 1],
                                                        prev, ALU.mult, ALU.add)
                    last.then_inc(acc_step, 1)
                    dve.wait_ge(acc_step, 4 * g + e + 1)

                def gelu_low(m):
                    dve.wait_ge(gelu_high_done, 8 * g + m + 1)
                    dve.tensor_tensor(gelu_part[1][:, m % 4], gelu_full[m % 2], gelu_part[0][:, m % 4].bitcast(F32),
                                      ALU.subtract).then_inc(gelu_low_done, 1)

                def add_expert(e):
                    for p in range(2):
                        dve.wait_ge(moe_done, 8 * g + 2 * e + p + 1)
                        if e:
                            dve.wait_ge(moe_added, 8 * g + 2 * e + p - 1)
                        for t in range(2):
                            last = dve.scalar_tensor_tensor(acc[:, p, t], ps_tr[p][:, t * E:(t + 1) * E],
                                                            comb_tg[:, 2 * p + t, e:e + 1], acc[:, p, t], ALU.mult, ALU.add)
                        last.then_inc(moe_added, 1)

                for e in range(NX):
                    gelu_low(2 * e)
                    gelu_low(2 * e + 1)
                    if e:
                        add_expert(e - 1)
                add_expert(NX - 1)
                dve.wait_ge(moe_added, 8 * g + 8)
                for p in range(2):
                    b = 2 * g + p
                    dve.wait_ge(out_stored, 16 * b)
                    layer_norm(lambda t: acc[:, p, t], tile_of(xn), 5 * NB + b).then_inc(z_done, 1)
                    dve.wait_ge(z_done, NB + b + 1)
                    dve.wait_ge(res_in, 16 * (2 * NB + b) + 16)
                    dve.tensor_tensor(xn[:].rearrange("p t e -> p (t e)"), res[:].rearrange("p t e -> p (t e)"),
                                      xn[:].rearrange("p t e -> p (t e)"), ALU.add).then_inc(out_ready, 1)
                    dve.wait_ge(out_ready, b + 1)
                    dve.sem_inc(res_free, 1)

        @block.tensor
        def _(pe):
            pe.wait_ge(const_in, 16 * 10)

            def project(V, i, layer):
                m, t = i // 2, i % 2
                if i == 0:
                    pe.wait_ge(xq_in, 32 * V + 32)
                if i == 4:
                    pe.wait_ge(xv_in, 32 * V + 32)
                if isinstance(V, int) and V == 0:
                    pe.wait_ge(w_split, 2 * m + 2)
                    if i >= 2:
                        pe.wait_ge(qk_ready, i - 1)
                else:
                    if i == 0:
                        pe.wait_ge(w_split, V + STEPS)
                    if i < 2:
                        pe.wait_ge(v_copied, 2 * V - 1 + i)
                    elif layer == 0:
                        pe.wait_ge(qk_ready, 4 * V + i - 1)
                    else:
                        pe.wait_ge(qk_biased, 4 * (V - UL) + i - 1)
                src = xv_part if m == 2 else xq_part
                n = 0
                for c in range(NE):
                    for a, w in PASSES:
                        last = pe.matmul(ps_proj[i % 2][:], src[a][:, c, t * P:(t + 1) * P], w_cols(V, 2 * m + c, 0, GW, w),
                                         start=(n == 0), stop=(n == 5))
                        n += 1
                last.then_inc(proj_done, 1)

            def transpose_qk(U, j):
                which, pair = j % 2, j // 2
                if j == 0:
                    pe.wait_ge(qk_ready, 4 * U + 4)
                if j < 2:
                    pe.wait_ge(probsT_copied, 4 * U)
                else:
                    pe.wait_ge(qkT_copied, 4 * U + j - 1)
                for hh in range(2):
                    for t in range(NT):
                        h = 2 * pair + hh
                        last = pe.transpose(ps_tr[j % 2][:, hh * T + t * P:hh * T + (t + 1) * P],
                                            qk[:, 2 * which + t, h * D:(h + 1) * D], ident_sb[:])
                last.then_inc(tr_done, 1)

            def scores(U, h, layer):
                if h % 2 == 0:
                    pe.wait_ge(qkT_copied, 4 * U + h + 2)
                if h >= 2:
                    pe.wait_ge(exp_done, 4 * U + h - 1)
                else:
                    pe.wait_ge(exp_done, 4 * U)
                for t in range(NT):
                    n = T if layer == 0 or t else P
                    dst = ps_s[h % 2][:, t * T:t * T + n]
                    last = pe.matmul(dst, qkT[:, 0, h, t * P:(t + 1) * P], qkT[:, 1, h, 0:n], start=True, stop=True)
                    if layer == 1:
                        last = pe.matmul(ps_s[h % 2][:, t * T + n - P:t * T + n], mask_sb[:, 0], mask_sb[:, 1],
                                         start=False, stop=True, skip_group_check=True)
                last.then_inc(s_done, 1)

            def transpose_probs(U, h, layer):
                pe.wait_ge(probs_done, 4 * U + h + 1)
                if h < 2:
                    pe.wait_ge(qkT_copied, 4 * U + 3 + h)
                else:
                    pe.wait_ge(probsT_copied, 4 * U + h - 1)
                for k in range(NT):
                    for q in range(NT):
                        if layer == 0 or k <= q:
                            last = pe.transpose(ps_tr[h % 2][:, k * T + q * P:k * T + (q + 1) * P],
                                                probs[:, h, q, k * P:(k + 1) * P], ident_sb[:])
                last.then_inc(tr_done, 1)

            def probs_v(U, h, layer):
                pe.wait_ge(probsT_copied, 4 * U + h + 1)
                if h == 0:
                    pe.wait_ge(v_copied, 2 * U + 2)
                    pe.wait_ge(o_low_done, 2 * U)
                if h == 2:
                    pe.wait_ge(o_low_done, 2 * U + 1)
                base = (h % 2) * T
                pe.matmul(ps_o[:, base:base + T], v[:, 0, h * D:(h + 1) * D], probsT[:, h % 2, 0], start=True, stop=(layer == 1))
                q0 = 0 if layer == 0 else P
                pe.matmul(ps_o[:, base + q0:base + T], v[:, 1, h * D:(h + 1) * D], probsT[:, h % 2, 1, q0:T],
                          start=False, stop=True, skip_group_check=(layer == 1)).then_inc(pv_done, 1)

            def out_project(U, h):
                if h == 0:
                    pe.wait_ge(y_added, U)
                if h % 2 == 0:
                    pe.wait_ge(o_low_done, 2 * U + h // 2 + 1)
                for t in range(NT):
                    for a, w in PASSES:
                        last = pe.matmul(ps_y[:, t * E:(t + 1) * E], oT_part[a][:, h, t * P:(t + 1) * P],
                                         w_cols(U, 6 + h // 2, (h % 2) * E, E, w),
                                         start=(h == 0 and t == 0 and (a, w) == (0, 0)), stop=(h == GH - 1),
                                         skip_group_check=True)
                if h == GH - 1:
                    last.then_inc(y_done, 1)

            def transpose_x(n):
                pe.wait_ge(xn_ready, n + 1)
                for c in range(NE):
                    for t in range(NT):
                        last = pe.transpose(ps_s[0][:, c * T + t * P:c * T + (t + 1) * P], xn[:, t, c * P:(c + 1) * P], ident_sb[:])
                last.then_inc(xT_done, 1)
                pe.wait_ge(xT_copied, n + 1)

            def gate_logits(b):
                for t in range(NT):
                    for c in range(NE):
                        last = pe.matmul(ps_s[1][:, t * NX:(t + 1) * NX], xT_full[:, c, t * P:(t + 1) * P], w_gate_sb[:, c],
                                         start=(c == 0), stop=(c == NE - 1))
                last.then_inc(logits_done, 1)
                pe.wait_ge(logits_copied, b + 1)

            def unit(U, layer, nl):
                V = U + 1
                for j in range(4):
                    transpose_qk(U, j)
                if nl is not None:
                    project(V, 0, nl)
                    project(V, 1, nl)
                scores(U, 0, layer)
                scores(U, 1, layer)
                if nl is not None:
                    project(V, 2, nl)
                scores(U, 2, layer)
                if nl is not None:
                    project(V, 3, nl)
                transpose_probs(U, 0, layer)
                scores(U, 3, layer)
                transpose_probs(U, 1, layer)
                probs_v(U, 0, layer)
                transpose_probs(U, 2, layer)
                probs_v(U, 1, layer)
                if nl is not None:
                    project(V, 4, nl)
                out_project(U, 0)
                out_project(U, 1)
                transpose_probs(U, 3, layer)
                probs_v(U, 2, layer)
                probs_v(U, 3, layer)
                if nl is not None:
                    project(V, 5, nl)
                out_project(U, 2)
                out_project(U, 3)

            transpose_x(0)
            with pe.Fori(1, NB) as b:
                transpose_x(b)
            for i in range(6):
                project(0, i, 0)
            with pe.Fori(0, LAG) as U:
                unit(U, 0, 0)
            with pe.Fori(LAG, UL - 1) as U:
                unit(U, 0, 0)
                transpose_x(U - LAG + NB)
            unit(UL - 1, 0, 1)
            transpose_x(2 * NB - 2)
            transpose_x(2 * NB - 1)
            with pe.Fori(UL, UL + LAG) as U:
                unit(U, 1, 1)
            with pe.Fori(UL + LAG, 2 * UL - 1) as U:
                unit(U, 1, 1)
                transpose_x(U - UL - LAG + 2 * NB)
                gate_logits(U - UL - LAG)
            unit(2 * UL - 1, 1, None)
            for b in (NB - 2, NB - 1):
                transpose_x(2 * NB + b)
                gate_logits(b)

            pe.wait_ge(w_split, NSTEP)
            pe.wait_ge(xT_ready, 3 * NB)
            with pe.Fori(0, NB // 2) as g:
                def expert_in(m):
                    e, ic = m // 2, m % 2
                    pe.wait_ge(gelu_done, 8 * g + (m - 1 if m >= 2 else 0))
                    n = 0
                    for c in range(NE):
                        for a, w in PASSES:
                            last = pe.matmul(ps_proj[m % 2][:].rearrange("p (b t) -> p b t", b=2),
                                             w_part[a][:, (2 * e) * GW + c * IM + ic * P:(2 * e) * GW + c * IM + (ic + 1) * P],
                                             xT_part[w][:, bass.ds(2 * g, 2), c], start=(n == 0), stop=(n == 5))
                            n += 1
                    last.then_inc(h1_done, 1)

                def expert_out(e):
                    pe.wait_ge(gelu_low_done, 8 * g + 2 * e + 2)
                    for p in range(2):
                        pe.wait_ge(moe_added, 8 * g + (2 * e - 1 + p if e else 0))
                        for t in range(2):
                            n = 0
                            for ic in range(2):
                                for a, w in PASSES:
                                    lo = (2 * e + 1) * GW + ic * E
                                    last = pe.matmul(ps_tr[p][:, t * E:(t + 1) * E],
                                                     gelu_part[a][:, (2 * e + ic) % 4, (2 * p + t) * P:(2 * p + t + 1) * P],
                                                     w_part[w][:, lo:lo + E], start=(n == 0), stop=(n == 5))
                                    n += 1
                        last.then_inc(moe_done, 1)

                for e in range(NX):
                    expert_in(2 * e)
                    expert_in(2 * e + 1)
                    if e:
                        expert_out(e - 1)
                expert_out(NX - 1)
    return nc


def kernel(**inputs):
    import concourse.bacc as _bacc
    from concourse.bass_utils import run_bass_kernel_spmd as _run

    a = {k.replace("L0_", ""): np.asarray(v_) for k, v_ in inputs.items()}

    pieces = []
    for blk in ("attn", "ffn"):
        wq, wk, wv, wo = (a[f"{blk}_w{c}"] for c in "qkvo")
        wo = wo.reshape(H, D, E)
        for g in range(NG):
            for w in (wq, wk, wv):
                w = w.reshape(E, H * D)[:, g * GW:(g + 1) * GW]
                pieces += [w[0:P], w[P:2 * P]]
            for j in range(2):
                pieces.append(wo[g * GH + 2 * j:g * GH + 2 * j + 2].transpose(1, 0, 2).reshape(P, GW))
    for e in range(NX):
        for w in (a["ffn_we1"][e], a["ffn_we2"][e]):
            pieces.append(w.reshape(2, P, 256).transpose(1, 0, 2).reshape(P, GW))

    def column(v_):
        return np.ascontiguousarray(v_.reshape(-1, P).T)

    inv_freq = (1.0 / 10000.0 ** (np.arange(0, D, 2, dtype=np.float32) / np.float32(D))).astype(np.float32)
    angle = np.arange(T, dtype=np.float32)[:, None] * inv_freq[None, :]
    cos, sin = np.cos(angle), np.sin(angle)
    rope = np.stack([np.concatenate([cos, cos], 1), np.concatenate([-sin, sin], 1)])
    rope = rope.reshape(2, NT, P, D).transpose(2, 0, 1, 3).astype(np.float32)
    bf16 = mybir.dt.np(BF16) if hasattr(mybir.dt, "np") else __import__("ml_dtypes").bfloat16
    fill = np.where(np.arange(P)[:, None] >= np.arange(P)[None, :], 0.0, -3.0e38)
    masks = np.stack([np.eye(P), fill], 1).astype(bf16)

    arrays = {
        "x": a["attn_x"],
        "weights": np.stack(pieces),
        "qk_scale": np.stack([a["attn_q_scale"], a["attn_k_scale"]], 1),
        "bias_qk": np.concatenate([a["ffn_bq"].reshape(NG, GW), a["ffn_bk"].reshape(NG, GW)], 1),
        "bv": column(a["ffn_bv"]),
        "bo": a["ffn_bo"],
        "ln1": np.stack([column(a["ffn_ln1_w"]), column(a["ffn_ln1_b"])], 1),
        "ln2": np.stack([column(a["ffn_ln2_w"]), column(a["ffn_ln2_b"])], 1),
        "w_gate": a["ffn_w_gate"].reshape(NE, P, NX).transpose(1, 0, 2),
        "be1": a["ffn_be1"].reshape(NX * IM // P, P).T,
        "be2": a["ffn_be2"].reshape(-1),
        "rope": rope,
        "masks": masks,
        "ident": np.eye(P, dtype=np.float32),
    }
    nc = _bacc.Bacc("TRN2", target_bir_lowering=False, num_devices=1)
    arrays = {f"in_{k}": np.ascontiguousarray(v_) for k, v_ in arrays.items()}
    args = [nc.dram_tensor(k, v_.shape, mybir.dt.from_np(v_.dtype), kind="ExternalInput").ap() for k, v_ in arrays.items()]
    out = nc.dram_tensor("out", (NB, T, E), F32, kind="ExternalOutput").ap()
    build(nc, *args, out)
    r = _run(nc, [arrays], core_ids=[0])
    return r.results[0]["out"]
```

```python
from contextlib import ExitStack

import numpy as np
import concourse.bass as bass
from concourse import mybir

F32 = mybir.dt.float32
F32R = mybir.dt.float32r
BF16 = mybir.dt.bfloat16
ALU = mybir.AluOpType
ACT = mybir.ActivationFunctionType
X = mybir.AxisListType.X

P = 128
NB, T, E = 8, 256, 256
H, D = 16, 128
GH = 4
NG = H // GH
NT, NE = T // P, E // P
UL = NG * NB
GW = GH * D
NX, IM = 4, 256
STEPS = 8
SLOTS = 2 * STEPS
NSTEP = (2 * NG + 1) * STEPS
AHEAD = STEPS + 1
LAG = UL - NB + 1
PRE = 3
LN_EPS, RMS_EPS = 1e-5, 1e-6
PASSES = ((0, 0), (0, 1), (1, 0))


def build(nc, x, weights, qk_scale, bias_qk, bv, bo, ln1, ln2, w_gate, be1, be2, rope, masks, ident, out):
    x1_dram = nc.dram_tensor("x1_dram", (NB, P, NT, E), F32).ap()
    x_d = x.rearrange("b (t p) e -> b p t e", p=P)
    out_d = out.rearrange("b (t p) e -> b p t e", p=P)

    with ExitStack() as ctx:
        def sb(name, shape, dt=F32):
            return ctx.enter_context(nc.sbuf_tensor(name, [P, *shape], dt))

        def sem(name):
            return ctx.enter_context(nc.semaphore(name))

        w_part = [sb("w_high", [SLOTS * GW], F32R), sb("w_low", [SLOTS * GW], F32R)]
        w_stage = sb("w_stage", [2 * GW])
        xT_part = [sb("xT_high", [NB, NE, T], F32R), sb("xT_low", [NB, NE, T], F32R)]
        xq_part = [sb("xq_high", [NE, T], F32R), sb("xq_low", [NE, T], F32R)]
        xv_part = [sb("xv_high", [NE, T], F32R), sb("xv_low", [NE, T], F32R)]
        y = sb("y", [NB, NT, E])
        bias_sb = sb("bias_sb", [2, 2 * GW])
        qk = sb("qk", [4, GW])
        scratch = sb("scratch", [2, GW])
        rot_a = sb("rot_a", [2, GW])
        rot_b = sb("rot_b", [2, GW])
        sumsq = sb("sumsq", [4, GH])
        meansq = sb("meansq", [4, GH])
        rstd_qk = sb("rstd_qk", [4, GH])
        qkT_part = [sb("qkT_high", [2, GH, T], F32R), sb("qkT_low", [2, GH, T], F32R)]
        v = sb("v", [NT, GW])
        probs = sb("probs", [GH, NT, T])
        neg_max = sb("neg_max", [GH, NT])
        row_sum = sb("row_sum", [GH, NT])
        inv_sum = sb("inv_sum", [GH, NT])
        probsT = sb("probsT", [2, NT, T])
        oT_part = [sb("oT_high", [GH, T], F32R), sb("oT_low", [GH, T], F32R)]
        res = sb("res", [NT, E])
        xn = sb("xn", [NT, E])
        xT_full = sb("xT_full", [NE, T])
        stats = sb("stats", [NT, 6])
        mean_var = sb("mean_var", [NT, 2])
        var_eps = sb("var_eps", [NT])
        rstd = sb("rstd", [NT])
        minus_half = sb("minus_half", [16])
        eps_sum = sb("eps_sum", [GH])
        pause = sb("pause", [1])
        ident_sb = sb("ident_sb", [P])
        mask_sb = sb("mask_sb", [2, P], BF16)
        rope_sb = sb("rope_sb", [2, NT, D])
        qk_scale_sb = sb("qk_scale_sb", [2])
        qk_root_sb = sb("qk_root_sb", [2])
        bv_sb = sb("bv_sb", [H])
        bo_sb = sb("bo_sb", [E])
        ln_sb = sb("ln_sb", [2, 2, NE])
        w_gate_sb = sb("w_gate_sb", [NE, NX])
        logits = sb("logits", [NB * NT, NX])
        be1_sb = sb("be1_sb", [NX * NE])
        gate = [sb(f"gate{i}", [NB * NT, NX]) for i in range(3)]
        gate_1 = [sb(f"gate_1{i}", [NB * NT]) for i in range(4)]
        beats = sb("beats", [NB * NT, NX, NX])
        comb_tg = sb("comb_tg", [2 * NT, NX])
        gelu_full = [scratch[:, i, :] for i in range(2)]
        gelu_part = [w[:, STEPS * GW:(STEPS + 4) * GW].rearrange("p (s c) -> p s c", s=4) for w in w_part]
        acc = qk[:, :, 0:GW].rearrange("p a (t e) -> p a t e", t=NT)
        be2_sb = probs[:, :, :, :].rearrange("p a b c -> p (a b c)")[:, 0:NX * E].rearrange("p (x e) -> p x e", x=NX)

        def bank(name):
            return ctx.enter_context(nc.psum_tensor(name, [P, 512], F32))
        ps_proj = [bank("ps_proj0"), bank("ps_proj1")]
        ps_tr = [bank("ps_tr0"), bank("ps_tr1")]
        ps_s = [bank("ps_s0"), bank("ps_s1")]
        ps_o = bank("ps_o")
        ps_y = bank("ps_y")

        const_in = sem("const_in")
        half_set = sem("half_set")
        root_set = sem("root_set")
        w_in = sem("w_in")
        w_high_done = sem("w_high_done")
        w_split = sem("w_split")
        bias_in = sem("bias_in")
        xq_in = sem("xq_in")
        xv_in = sem("xv_in")
        proj_done = sem("proj_done")
        sq_done = sem("sq_done")
        sumsq_done = sem("sumsq_done")
        meansq_done = sem("meansq_done")
        rstd_qk_done = sem("rstd_qk_done")
        qk_biased = sem("qk_biased")
        rot_a_done = sem("rot_a_done")
        rot_b_done = sem("rot_b_done")
        qk_ready = sem("qk_ready")
        v_copied = sem("v_copied")
        tr_done = sem("tr_done")
        qkT_high_done = sem("qkT_high_done")
        qkT_low_done = sem("qkT_low_done")
        s_done = sem("s_done")
        max_done = sem("max_done")
        exp_done = sem("exp_done")
        inv_done = sem("inv_done")
        probs_done = sem("probs_done")
        probsT_copied = sem("probsT_copied")
        pv_done = sem("pv_done")
        o_high_done = sem("o_high_done")
        o_low_done = sem("o_low_done")
        y_done = sem("y_done")
        y_added = sem("y_added")
        res_in = sem("res_in")
        res_free = sem("res_free")
        x1_ready = sem("x1_ready")
        x1_out = sem("x1_out")
        ln_stats = sem("ln_stats")
        ln_aggr = sem("ln_aggr")
        ln_var = sem("ln_var")
        ln_rstd = sem("ln_rstd")
        ln_done = sem("ln_done")
        h0_done = sem("h0_done")
        z_done = sem("z_done")
        xn_ready = sem("xn_ready")
        xT_done = sem("xT_done")
        xT_copied = sem("xT_copied")
        xT_high_done = sem("xT_high_done")
        xT_ready = sem("xT_ready")
        logits_done = sem("logits_done")
        logits_copied = sem("logits_copied")
        gate_step = sem("gate_step")
        gate_exp = sem("gate_exp")
        be2_in = sem("be2_in")
        be2_may_load = sem("be2_may_load")
        h1_done = sem("h1_done")
        gelu_done = sem("gelu_done")
        gelu_high_done = sem("gelu_high_done")
        gelu_low_done = sem("gelu_low_done")
        moe_done = sem("moe_done")
        moe_added = sem("moe_added")
        comb_set = sem("comb_set")
        acc_step = sem("acc_step")
        out_ready = sem("out_ready")
        out_stored = sem("out_stored")

        block = ctx.enter_context(nc.Block())

        N_CONST = 13

        def w_cols(unit, step, lo, n, part):
            group = unit // NB
            return w_part[part][:, bass.ds((group % 2) * (STEPS * GW) + step * GW + lo, n)]

        def seq(unit):
            return unit % NB

        def qkT_of(part, which, pair):
            return qkT_part[part][:, which, 2 * pair:2 * pair + 2].rearrange("p h t -> p (h t)")

        def score_scale(which, layer):
            if layer == 0:
                return qk_root_sb[:, which:which + 1]
            return float(D) ** -0.5 if which == 0 else 1.0

        @block.sync
        def _(sp):
            def load_weight(s):
                if not isinstance(s, int) or s >= 2:
                    sp.wait_ge(w_split, s - 1)
                if not isinstance(s, int) or s >= 1:
                    sp.wait_ge(w_in, 16 * s)
                sp.dma_start(w_stage[:, bass.ds((s % 2) * GW, GW)],
                             weights[bass.ds(s, 1)].rearrange("s p c -> p (s c)")).then_inc(w_in, 16)

            def load_xq(V):
                for part in range(2):
                    sp.dma_start(xq_part[part][:].bitcast(F32), xT_part[part][:, bass.ds(seq(V), 1)]
                                 .rearrange("p b c t -> p (b c) t").bitcast(F32)).then_inc(xq_in, 16)

            def load_xv(V):
                for part in range(2):
                    sp.dma_start(xv_part[part][:].bitcast(F32), xT_part[part][:, bass.ds(seq(V), 1)]
                                 .rearrange("p b c t -> p (b c) t").bitcast(F32)).then_inc(xv_in, 16)

            def load_bias(g):
                sp.dma_start(bias_sb[:, g % 2, :], bias_qk[g:g + 1, :].rearrange("g c -> (g c)")
                             .partition_broadcast(P)).then_inc(bias_in, 16)

            sp.dma_start(res[:], x_d[0]).then_inc(res_in, 16)
            for s in range(2):
                load_weight(s)
            for b in range(1, PRE):
                sp.wait_ge(res_free, b)
                sp.dma_start(res[:], x_d[b]).then_inc(res_in, 16)
                load_weight(b + 1)
            sp.wait_ge(xT_ready, 1)
            load_xq(0)
            load_xv(0)
            for s in range(PRE + 1, AHEAD):
                load_weight(s)
            sp.wait_ge(proj_done, 4)
            sp.wait_ge(xT_ready, 2)
            load_xq(1)

            def unit(U, xT_count=None):
                V = U + 1
                sp.wait_ge(proj_done, 6 * U + 6)
                load_xv(V)
                load_weight(U + AHEAD)
                if not (isinstance(V, int) and V == 2 * UL - 1):
                    sp.wait_ge(proj_done, 6 * V + 4)
                    if xT_count is not None:
                        sp.wait_ge(xT_ready, xT_count)
                    load_xq(V + 1)

            def load_x(b):
                sp.wait_ge(res_free, b)
                sp.dma_start(res[:], x_d[bass.ds(b, 1)].rearrange("b p t e -> p (b t) e")).then_inc(res_in, 16)

            def first_epilogue(b):
                sp.wait_ge(res_free, b + NB)
                sp.wait_ge(x1_out, 16 * b)
                sp.dma_start(res[:], x_d[bass.ds(b, 1)].rearrange("b p t e -> p (b t) e")).then_inc(res_in, 16)

            def store_x1(b):
                sp.wait_ge(x1_ready, b + 1)
                sp.dma_start(x1_dram[bass.ds(b, 1)].rearrange("b p t e -> p (b t) e"), res[:]).then_inc(x1_out, 16)

            with sp.Fori(0, NB - PRE) as U:
                load_x(U + PRE)
                unit(U, U + PRE)
            with sp.Fori(NB - PRE, LAG) as U:
                unit(U)
            with sp.Fori(LAG, UL - 1) as U:
                first_epilogue(U - LAG)
                store_x1(U - LAG)
                unit(U, U - LAG + NB)
            load_bias(0)
            first_epilogue(NB - 2)
            store_x1(NB - 2)
            unit(UL - 1, NB + 2)
            sp.wait_ge(bias_in, 16)
            load_bias(1)
            first_epilogue(NB - 1)
            store_x1(NB - 1)
            unit(UL, NB + 3)
            sp.wait_ge(xT_ready, 2 * NB)
            for g in range(NG - 1):
                with sp.Fori(UL + 1 if g == 0 else UL + g * NB, UL + (g + 1) * NB) as U:
                    unit(U)
                if g + 2 < NG:
                    sp.wait_ge(qk_biased, 4 * (g + 1) * NB)
                    sp.wait_ge(bias_in, 16 * (g + 2))
                    load_bias(g + 2)
            with sp.Fori(UL + 3 * NB, 2 * UL - 2) as U:
                unit(U)
            unit(2 * UL - 2)

            sp.wait_ge(be2_may_load, 1)
            sp.dma_start(be2_sb, be2.partition_broadcast(P).rearrange("p (x e) -> p x e", x=NX)).then_inc(be2_in, 16)
            with sp.Fori(0, NB) as b:
                sp.wait_ge(res_free, b + 2 * NB)
                sp.dma_start(res[:], x1_dram[bass.ds(b, 1)].rearrange("b p t e -> p (b t) e")).then_inc(res_in, 16)
                sp.wait_ge(out_ready, b + 1)
                sp.dma_start(out_d[bass.ds(b, 1)].rearrange("b p t e -> p (b t) e"), xn[:]).then_inc(out_stored, 16)
            sp.wait_ge(x1_out, 16 * NB)
            sp.wait_ge(out_stored, 16 * NB)

        @block.gpsimd
        def _(pool):
            pool.memset(minus_half[:], -0.5)
            pool.memset(eps_sum[:], D * RMS_EPS).then_inc(half_set, 1)
            pool.wait_ge(half_set, 1)

            def split_weight(s):
                src = w_stage[:, bass.ds((s % 2) * GW, GW)]
                high = w_part[0][:, bass.ds((s % SLOTS) * GW, GW)]
                low = w_part[1][:, bass.ds((s % SLOTS) * GW, GW)]
                pool.wait_ge(w_in, 16 * s + 16)
                pool.tensor_copy(high, src).then_inc(w_high_done, 1)
                pool.wait_ge(w_high_done, s + 1)
                pool.tensor_tensor(low, src, high.bitcast(F32), ALU.subtract).then_inc(w_split, 1)

            def ln_power(k):
                pool.wait_ge(ln_var, k + 1)
                pool.tensor_tensor(rstd[:], var_eps[:], minus_half[:, 0:NT], ALU.pow).then_inc(ln_rstd, 1)

            def rms_power(V, i):
                pool.wait_ge(sumsq_done, 4 * V + i + 1)
                pool.tensor_tensor(meansq[:, i], sumsq[:, i], eps_sum[:], ALU.add).then_inc(meansq_done, 1)
                pool.wait_ge(meansq_done, 4 * V + i + 1)
                pool.tensor_tensor(rstd_qk[:, i], meansq[:, i], minus_half[:, 0:GH], ALU.pow).then_inc(rstd_qk_done, 1)

            def rotate_a(V, i):
                n = 4 * (V - UL) + i
                pool.wait_ge(qk_biased, n + 1)
                if not isinstance(V, int) or V > UL or i >= 2:
                    pool.wait_ge(qk_ready, 4 * V + i - 1)
                cos = rope_sb[:, 0, i % 2].unsqueeze(1).to_broadcast([P, GH, D])
                pool.tensor_tensor(rot_a[:, i % 2].rearrange("p (h d) -> p h d", h=GH),
                                   scratch[:, i % 2].rearrange("p (h d) -> p h d", h=GH), cos,
                                   ALU.mult).then_inc(rot_a_done, 1)

            def qk_part(V, layer):
                for i in range(4):
                    rms_power(V, i) if layer == 0 else rotate_a(V, i)

            def split_ahead(U):
                pool.wait_ge(proj_done, 6 * U + 6)
                pool.wait_ge(y_done, U)
                split_weight(U + AHEAD)

            for b in range(PRE):
                ln_power(b)
                split_weight(2 * b)
                split_weight(2 * b + 1)
            for s in range(2 * PRE, AHEAD):
                split_weight(s)
            qk_part(0, 0)
            with pool.Fori(0, NB - PRE) as U:
                ln_power(U + PRE)
                qk_part(U + 1, 0)
                split_ahead(U)
            with pool.Fori(NB - PRE, LAG) as U:
                qk_part(U + 1, 0)
                split_ahead(U)
            with pool.Fori(LAG, UL - 1) as U:
                for i in range(4):
                    if i < 3:
                        ln_power(NB + 3 * (U - LAG) + i)
                    rms_power(U + 1, i)
                split_ahead(U)
            for j in range(2):
                for i in range(4):
                    if i < 3:
                        ln_power(NB + 3 * (NB - 2 + j) + i)
                    rotate_a(UL + j, i)
                split_ahead(UL - 1 + j)
            with pool.Fori(UL + 1, UL + LAG) as U:
                qk_part(U + 1, 1)
                split_ahead(U)
            with pool.Fori(UL + LAG, 2 * UL - 1) as U:
                ln_power(4 * NB + U - UL - LAG)
                qk_part(U + 1, 1)
                split_ahead(U)
            for j in range(2):
                ln_power(5 * NB - 2 + j)
            with pool.Fori(0, NB) as b:
                ln_power(5 * NB + b)

        @block.scalar
        def _(act):
            for dst, src in ((ident_sb[:], ident), (qk_scale_sb[:], qk_scale), (mask_sb[:], masks), (rope_sb[:], rope),
                             (bv_sb[:], bv), (bo_sb[:], bo.partition_broadcast(P)),
                             (ln_sb[:, 0], ln1), (ln_sb[:, 1], ln2), (w_gate_sb[:], w_gate), (be1_sb[:], be1)):
                act.dma_start(dst, src).then_inc(const_in, 16)
            act.wait_ge(const_in, 16 * 10)
            act.activation(qk_root_sb[:], qk_scale_sb[:], ACT.Copy, scale=float(D) ** 0.5).then_inc(root_set, 1)
            act.wait_ge(root_set, 1)

            def copy_qkT(U, j, layer):
                which, pair = j % 2, j // 2
                act.wait_ge(tr_done, 8 * U + j + 1)
                act.activation(qkT_of(0, which, pair), ps_tr[j % 2][:], ACT.Copy,
                               scale=score_scale(which, layer)).then_inc(qkT_high_done, 1)

            def copy_probsT(U, h, layer):
                act.wait_ge(tr_done, 8 * U + 5 + h)
                if h < 2:
                    act.wait_ge(pv_done, 4 * U)
                else:
                    act.wait_ge(pv_done, 4 * U + h - 1)
                dst = probsT[:, h % 2].rearrange("p k q -> p (k q)")
                if layer == 0:
                    last = act.activation(dst, ps_tr[h % 2][:], ACT.Copy)
                else:
                    act.activation(dst[:, 0:T], ps_tr[h % 2][:, 0:T], ACT.Copy)
                    last = act.activation(dst[:, T + P:2 * T], ps_tr[h % 2][:, T + P:2 * T], ACT.Copy)
                last.then_inc(probsT_copied, 1)

            def square(V, i):
                act.wait_ge(proj_done, 6 * V + i + 1)
                if i >= 2:
                    act.wait_ge(sumsq_done, 4 * V + i - 1)
                else:
                    act.wait_ge(sumsq_done, 4 * V)
                act.activation(scratch[:, i % 2], ps_proj[i % 2][:], ACT.Square).then_inc(sq_done, 1)

            def exp_head(U, h, layer):
                act.wait_ge(max_done, 4 * U + h + 1)
                for t in range(NT):
                    n = T if layer == 0 or t else P
                    last = act.activation(probs[:, h, t, 0:n], ps_s[h % 2][:, t * T:t * T + n], ACT.Exp,
                                          bias=neg_max[:, h, t:t + 1], accum_out=row_sum[:, h, t:t + 1])
                last.then_inc(exp_done, 1)

            def copy_v(U, t, V):
                act.wait_ge(proj_done, 6 * V + 5 + t)
                if t == 0:
                    act.wait_ge(pv_done, 4 * U + 4)
                act.activation(v[:, t], ps_proj[t][:], ACT.Copy).then_inc(v_copied, 1)

            def o_high(U, pair, layer):
                act.wait_ge(pv_done, 4 * U + 2 * pair + 2)
                for h in range(2):
                    bias = 0.0 if layer == 0 else bv_sb[:, bass.ds(((U - UL) // NB) * GH + 2 * pair + h, 1)]
                    if layer == 0:
                        if h == 0:
                            last = act.activation(oT_part[0][:, 2 * pair:2 * pair + 2].rearrange("p h t -> p (h t)"),
                                                  ps_o[:], ACT.Copy)
                    else:
                        last = act.activation(oT_part[0][:, 2 * pair + h], ps_o[:, h * T:(h + 1) * T], ACT.Identity, bias=bias)
                last.then_inc(o_high_done, 1)

            def xT_out(n, b, which):
                act.wait_ge(xT_done, n + 1)
                for c in range(NE):
                    src = ps_s[0][:, c * T:(c + 1) * T]
                    if which is None:
                        last = act.activation(xT_full[:, c], src, ACT.Copy)
                    else:
                        last = act.activation(xT_full[:, c], src, ACT.Identity, bias=ln_sb[:, which, 1, c:c + 1],
                                              scale=ln_sb[:, which, 0, c:c + 1])
                last.then_inc(xT_copied, 1)
                act.wait_ge(xT_copied, n + 1)
                act.activation(xT_part[0][:, bass.ds(b, 1)].rearrange("p b c t -> p (b c t)"),
                               xT_full[:].rearrange("p c t -> p (c t)"), ACT.Copy).then_inc(xT_high_done, 1)

            def unit_1(U, nl, finish=None):
                V = U + 1
                copy_qkT(U, 0, 0)
                copy_qkT(U, 1, 0)
                if nl == 0:
                    square(V, 0)
                copy_qkT(U, 2, 0)
                exp_head(U, 0, 0)
                copy_qkT(U, 3, 0)
                if nl == 0:
                    square(V, 1)
                exp_head(U, 1, 0)
                copy_probsT(U, 0, 0)
                if nl == 0:
                    square(V, 2)
                exp_head(U, 2, 0)
                copy_probsT(U, 1, 0)
                exp_head(U, 3, 0)
                o_high(U, 0, 0)
                copy_probsT(U, 2, 0)
                if nl == 0:
                    square(V, 3)
                copy_probsT(U, 3, 0)
                o_high(U, 1, 0)
                if finish:
                    finish()
                copy_v(U, 0, V)
                copy_v(U, 1, V)

            def unit_2(U, nl, finish=None):
                V = U + 1
                for j in range(4):
                    copy_qkT(U, j, 1)
                exp_head(U, 0, 1)
                exp_head(U, 1, 1)
                copy_probsT(U, 0, 1)
                copy_probsT(U, 1, 1)
                exp_head(U, 2, 1)
                o_high(U, 0, 1)
                exp_head(U, 3, 1)
                copy_probsT(U, 2, 1)
                copy_probsT(U, 3, 1)
                o_high(U, 1, 1)
                if finish:
                    finish()
                if nl is not None:
                    copy_v(U, 0, V)
                    copy_v(U, 1, V)

            for b in range(PRE):
                xT_out(b, b, None)
            for i in range(4):
                square(0, i)
            for t in range(NT):
                act.wait_ge(proj_done, 5 + t)
                act.activation(v[:, t], ps_proj[t][:], ACT.Copy).then_inc(v_copied, 1)
            with act.Fori(0, NB - PRE) as U:
                unit_1(U, 0, lambda: xT_out(U + PRE, U + PRE, None))
            with act.Fori(NB - PRE, LAG) as U:
                unit_1(U, 0)
            with act.Fori(LAG, UL - 1) as U:
                unit_1(U, 0, lambda: xT_out(U - LAG + NB, U - LAG, 0))
            unit_1(UL - 1, 1, lambda: xT_out(2 * NB - 2, NB - 2, 0))
            unit_2(UL, 1, lambda: xT_out(2 * NB - 1, NB - 1, 0))
            with act.Fori(UL + 1, UL + LAG) as U:
                unit_2(U, 1)
            with act.Fori(UL + LAG, 2 * UL - 1) as U:
                unit_2(U, 1, lambda: xT_out(U - UL - LAG + 2 * NB, U - UL - LAG, 1))
            unit_2(2 * UL - 1, None, lambda: xT_out(3 * NB - 2, NB - 2, 1))
            xT_out(3 * NB - 1, NB - 1, 1)

            for k in range(2):
                act.wait_ge(gate_step, (2, 13)[k])
                act.activation(gate[(1, 2)[k]][:], gate[0][:], ACT.Exp).then_inc(gate_exp, 1)
            with act.Fori(0, NB // 2) as g:
                for m in range(8):
                    act.wait_ge(h1_done, 8 * g + m + 1)
                    if m >= 2:
                        act.wait_ge(gelu_low_done, 8 * g + m - 1)
                    else:
                        act.wait_ge(gelu_low_done, 8 * g)
                    act.activation(gelu_full[m % 2], ps_proj[m % 2][:], ACT.Gelu,
                                   bias=be1_sb[:, m:m + 1]).then_inc(gelu_done, 1)
                    act.wait_ge(gelu_done, 8 * g + m + 1)
                    act.wait_ge(moe_done, 8 * g + (2 * (m // 2) - 2 if m >= 4 else 0))
                    act.activation(gelu_part[0][:, m % 4], gelu_full[m % 2], ACT.Copy).then_inc(gelu_high_done, 1)

        @block.vector
        def _(dve):
            def ln_step_stats(src):
                for t in range(NT):
                    last = dve.bn_stats(stats[:, t], src(t))
                last.then_inc(ln_stats, 1)

            def ln_step_mean(k):
                dve.wait_ge(ln_stats, k + 1)
                dve.memset(pause[:], 0.0)
                for t in range(NT):
                    last = dve.bn_aggr(mean_var[:, t], stats[:, t])
                last.then_inc(ln_aggr, 1)

            def ln_step_var(k):
                dve.wait_ge(ln_aggr, k + 1)
                dve.tensor_scalar(var_eps[:], mean_var[:, :, 1], LN_EPS, None, ALU.add).then_inc(ln_var, 1)

            def ln_step_out(src, dst, k):
                dve.wait_ge(ln_rstd, k + 1)
                for t in range(NT):
                    last = dve.tensor_scalar(dst(t), src(t), mean_var[:, t, 0:1], rstd[:, t:t + 1], ALU.subtract, ALU.mult)
                return last

            def layer_norm(src, dst, k):
                ln_step_stats(src)
                ln_step_mean(k)
                ln_step_var(k)
                return ln_step_out(src, dst, k)

            def y_tile(b):
                return lambda t: y[:, bass.ds(b, 1), t].rearrange("p b e -> p (b e)")

            def tile_of(buf):
                return lambda t: buf[:, t]

            def xT_low(n, b):
                low = xT_part[1][:, bass.ds(b, 1)].rearrange("p b c t -> p (b c t)")
                high = xT_part[0][:, bass.ds(b, 1)].rearrange("p b c t -> p (b c t)").bitcast(F32)
                dve.wait_ge(xT_high_done, n + 1)
                dve.tensor_tensor(low, xT_full[:].rearrange("p c t -> p (c t)"), high, ALU.subtract).then_inc(xT_ready, 1)

            def low_qkT(U, j, layer):
                which, pair = j % 2, j // 2
                dve.wait_ge(qkT_high_done, 4 * U + j + 1)
                dve.scalar_tensor_tensor(qkT_of(1, which, pair), ps_tr[j % 2][:], score_scale(which, layer),
                                         qkT_of(0, which, pair).bitcast(F32), ALU.mult, ALU.subtract).then_inc(qkT_low_done, 1)

            def sum_squares(V, i):
                dve.wait_ge(sq_done, 4 * V + i + 1)
                dve.tensor_reduce(sumsq[:, i], scratch[:, i % 2].rearrange("p (h d) -> p h d", h=GH),
                                  axis=X, op=ALU.add).then_inc(sumsq_done, 1)

            def scale_qk(V, i):
                dve.wait_ge(rstd_qk_done, 4 * V + i + 1)
                dve.wait_ge(tr_done, 8 * V - (5 if i < 2 else 4))
                dve.tensor_tensor(qk[:, i].rearrange("p (h d) -> p h d", h=GH),
                                  ps_proj[i % 2][:].rearrange("p (h d) -> p h d", h=GH),
                                  rstd_qk[:, i].unsqueeze(2).to_broadcast([P, GH, D]), ALU.mult).then_inc(qk_ready, 1)

            def add_bias(V, i):
                n = 4 * (V - UL) + i
                dve.wait_ge(proj_done, 6 * V + i + 1)
                if i == 0:
                    dve.wait_ge(bias_in, 16 * ((V - UL) // NB + 1))
                if not isinstance(V, int) or V > UL or i >= 2:
                    dve.wait_ge(rot_a_done, n - 1)
                    dve.wait_ge(rot_b_done, n - 1)
                bias = bias_sb[:].rearrange("p g c -> p (g c)")[
                    :, bass.ds((((V - UL) // NB) % 2) * (2 * GW) + (i // 2) * GW, GW)]
                dve.tensor_tensor(scratch[:, i % 2], ps_proj[i % 2][:], bias, ALU.add).then_inc(qk_biased, 1)

            def rotate_b(V, i):
                n = 4 * (V - UL) + i
                dve.wait_ge(qk_biased, n + 1)
                if not isinstance(V, int) or V > UL or i >= 2:
                    dve.wait_ge(qk_ready, 4 * V + i - 1)
                swapped = scratch[:, i % 2].rearrange("p (h s d) -> p h s d", h=GH, s=2)[:, :, ::-1, :]
                sin = rope_sb[:, 1, i % 2].rearrange("p (s d) -> p s d", s=2).unsqueeze(1).to_broadcast([P, GH, 2, D // 2])
                dve.tensor_tensor(rot_b[:, i % 2].rearrange("p (h s d) -> p h s d", h=GH, s=2), swapped, sin,
                                  ALU.mult).then_inc(rot_b_done, 1)

            def rotate_sum(V, i):
                n = 4 * (V - UL) + i
                dve.wait_ge(rot_a_done, n + 1)
                dve.wait_ge(rot_b_done, n + 1)
                dve.wait_ge(tr_done, 8 * V - (5 if i < 2 else 4))
                dve.tensor_tensor(qk[:, i], rot_a[:, i % 2], rot_b[:, i % 2], ALU.add).then_inc(qk_ready, 1)

            def row_max(U, h, layer):
                dve.wait_ge(s_done, 4 * U + h + 1)
                if layer == 0:
                    last = dve.tensor_reduce(neg_max[:, h], ps_s[h % 2][:].rearrange("p (t k) -> p t k", t=NT),
                                             axis=X, op=ALU.max, negate=True)
                else:
                    dve.tensor_reduce(neg_max[:, h, 0:1], ps_s[h % 2][:, 0:P], axis=X, op=ALU.max, negate=True)
                    last = dve.tensor_reduce(neg_max[:, h, 1:2], ps_s[h % 2][:, T:2 * T], axis=X, op=ALU.max, negate=True)
                last.then_inc(max_done, 1)

            def normalise(U, h, layer):
                dve.wait_ge(exp_done, 4 * U + h + 1)
                dve.reciprocal(inv_sum[:, h], row_sum[:, h]).then_inc(inv_done, 1)
                dve.wait_ge(inv_done, 4 * U + h + 1)
                for t in range(NT):
                    n = T if layer == 0 or t else P
                    last = dve.tensor_scalar(probs[:, h, t, 0:n], probs[:, h, t, 0:n], inv_sum[:, h, t:t + 1], None, ALU.mult)
                last.then_inc(probs_done, 1)

            def o_low(U, pair, layer):
                dve.wait_ge(o_high_done, 2 * U + pair + 1)
                if layer == 0:
                    last = dve.tensor_tensor(oT_part[1][:, 2 * pair:2 * pair + 2].rearrange("p h t -> p (h t)"), ps_o[:],
                                             oT_part[0][:, 2 * pair:2 * pair + 2].rearrange("p h t -> p (h t)").bitcast(F32),
                                             ALU.subtract)
                else:
                    for h in range(2):
                        bias = bv_sb[:, bass.ds(((U - UL) // NB) * GH + 2 * pair + h, 1)]
                        last = dve.scalar_tensor_tensor(oT_part[1][:, 2 * pair + h], ps_o[:, h * T:(h + 1) * T], bias,
                                                        oT_part[0][:, 2 * pair + h].bitcast(F32), ALU.add, ALU.subtract)
                last.then_inc(o_low_done, 1)

            def add_y(U):
                dve.wait_ge(y_done, U + 1)
                y_b = y[:, bass.ds(seq(U), 1)].rearrange("p b t e -> p (b t e)")
                dve.tensor_tensor(y_b, ps_y[:], y_b, ALU.add).then_inc(y_added, 1)

            def prologue(b, k, first=True):
                if k == 0:
                    dve.wait_ge(res_in, 16 * b + 16)
                    ln_step_stats(tile_of(res))
                elif k == 1:
                    ln_step_mean(b)
                elif k == 2:
                    ln_step_var(b)
                elif k == 3:
                    if not isinstance(b, int) or b > 0:
                        dve.wait_ge(xT_done, b)
                    ln_step_out(tile_of(res), tile_of(xn), b).then_inc(xn_ready, 1)
                elif k == 4:
                    dve.wait_ge(xn_ready, b + 1)
                    dve.sem_inc(res_free, 1)

            def epilogue_1(b, k):
                n = NB + 3 * b
                if k == 0:
                    dve.wait_ge(y_added, UL - NB + b + 1)
                    ln_step_stats(y_tile(b))
                elif k in (1, 5, 9):
                    ln_step_mean(n + k // 4)
                elif k in (2, 6, 10):
                    ln_step_var(n + k // 4)
                elif k == 3:
                    dve.wait_ge(xT_done, NB + b)
                    ln_step_out(y_tile(b), tile_of(xn), n).then_inc(z_done, 1)
                elif k == 4:
                    dve.wait_ge(z_done, b + 1)
                    dve.wait_ge(res_in, 16 * (NB + b) + 16)
                    dve.tensor_tensor(res[:].rearrange("p t e -> p (t e)"), res[:].rearrange("p t e -> p (t e)"),
                                      xn[:].rearrange("p t e -> p (t e)"), ALU.add).then_inc(x1_ready, 1)
                    dve.wait_ge(x1_ready, b + 1)
                    ln_step_stats(tile_of(res))
                elif k == 7:
                    ln_step_out(tile_of(res), tile_of(xn), n + 1).then_inc(h0_done, 1)
                elif k == 8:
                    dve.wait_ge(h0_done, b + 1)
                    ln_step_stats(tile_of(xn))
                elif k == 11:
                    for t in range(NT):
                        dve.tensor_tensor(y_tile(b)(t), xn[:, t], bo_sb[:], ALU.add)
                    ln_step_out(tile_of(xn), tile_of(xn), n + 2).then_inc(xn_ready, 1)
                    dve.sem_inc(res_free, 1)

            def epilogue_2(b, k):
                if k == 0:
                    dve.wait_ge(y_added, 2 * UL - NB + b + 1)
                    ln_step_stats(y_tile(b))
                elif k == 1:
                    ln_step_mean(4 * NB + b)
                elif k == 2:
                    ln_step_var(4 * NB + b)
                elif k == 3:
                    ln_step_out(y_tile(b), tile_of(xn), 4 * NB + b).then_inc(xn_ready, 1)

            def copy_logits(b):
                dve.wait_ge(logits_done, b + 1)
                dve.tensor_copy(logits[:, bass.ds(b * NT, NT)].rearrange("p t x -> p (t x)"),
                                ps_s[1][:, 0:NT * NX]).then_inc(logits_copied, 1)

            def qk_first(V, i, layer):
                if layer == 0:
                    sum_squares(V, i)
                elif layer == 1:
                    add_bias(V, i)
                    rotate_b(V, i)

            def qk_last(V, i, layer):
                if layer == 0:
                    scale_qk(V, i)
                elif layer == 1:
                    rotate_sum(V, i)

            def nothing(k):
                pass

            def unit_1(U, nl, step=nothing, n=None, b=None):
                V = U + 1
                low_qkT(U, 0, 0)
                low_qkT(U, 1, 0)
                step(0)
                qk_first(V, 0, nl)
                step(1)
                row_max(U, 0, 0)
                step(2)
                low_qkT(U, 2, 0)
                qk_last(V, 0, nl)
                row_max(U, 1, 0)
                step(3)
                normalise(U, 0, 0)
                step(4)
                low_qkT(U, 3, 0)
                step(5)
                qk_first(V, 1, nl)
                step(6)
                normalise(U, 1, 0)
                row_max(U, 2, 0)
                step(7)
                qk_last(V, 1, nl)
                step(8)
                row_max(U, 3, 0)
                step(9)
                qk_first(V, 2, nl)
                step(10)
                normalise(U, 2, 0)
                qk_last(V, 2, nl)
                step(11)
                normalise(U, 3, 0)
                o_low(U, 0, 0)
                qk_first(V, 3, nl)
                qk_last(V, 3, nl)
                o_low(U, 1, 0)
                if n is not None:
                    xT_low(n, b)
                add_y(U)

            def unit_2(U, nl, step=nothing, n=None, b=None):
                V = U + 1
                low_qkT(U, 0, 1)
                low_qkT(U, 1, 1)
                step(0)
                if nl:
                    add_bias(V, 0)
                step(1)
                row_max(U, 0, 1)
                step(2)
                low_qkT(U, 2, 1)
                row_max(U, 1, 1)
                step(3)
                low_qkT(U, 3, 1)
                step(4)
                normalise(U, 0, 1)
                step(5)
                normalise(U, 1, 1)
                step(6)
                if nl:
                    add_bias(V, 1)
                step(7)
                row_max(U, 2, 1)
                step(8)
                if nl:
                    rotate_b(V, 0)
                    add_bias(V, 2)
                step(9)
                row_max(U, 3, 1)
                step(10)
                if nl:
                    rotate_b(V, 1)
                normalise(U, 2, 1)
                step(11)
                normalise(U, 3, 1)
                o_low(U, 0, 1)
                if nl:
                    add_bias(V, 3)
                    rotate_sum(V, 0)
                    rotate_sum(V, 1)
                    rotate_b(V, 2)
                    rotate_sum(V, 2)
                o_low(U, 1, 1)
                if nl:
                    rotate_b(V, 3)
                    rotate_sum(V, 3)
                if n is not None:
                    xT_low(n, b)
                add_y(U)

            dve.memset(y[:], 0.0)
            for b in range(PRE):
                for k in range(5):
                    prologue(b, k)
                xT_low(b, b)
            for i in range(4):
                sum_squares(0, i)
                dve.wait_ge(rstd_qk_done, i + 1)
                dve.tensor_tensor(qk[:, i].rearrange("p (h d) -> p h d", h=GH),
                                  ps_proj[i % 2][:].rearrange("p (h d) -> p h d", h=GH),
                                  rstd_qk[:, i].unsqueeze(2).to_broadcast([P, GH, D]), ALU.mult).then_inc(qk_ready, 1)
            dve.wait_ge(const_in, 16 * 10)
            dve.wait_ge(root_set, 1)
            with dve.Fori(0, NB - PRE) as U:
                unit_1(U, 0, lambda k: prologue(U + PRE, k), U + PRE, U + PRE)
            with dve.Fori(NB - PRE, LAG) as U:
                unit_1(U, 0)
            with dve.Fori(LAG, UL - 1) as U:
                unit_1(U, 0, lambda k: epilogue_1(U - LAG, k), U - LAG + NB, U - LAG)
            unit_1(UL - 1, 1, lambda k: epilogue_1(NB - 2, k), 2 * NB - 2, NB - 2)
            unit_2(UL, 1, lambda k: epilogue_1(NB - 1, k), 2 * NB - 1, NB - 1)
            with dve.Fori(UL + 1, UL + LAG) as U:
                unit_2(U, 1)
            with dve.Fori(UL + LAG, 2 * UL - 1) as U:
                unit_2(U, 1, lambda k: epilogue_2(U - UL - LAG, k), U - UL - LAG + 2 * NB, U - UL - LAG)
                copy_logits(U - UL - LAG)
            unit_2(2 * UL - 1, None, lambda k: epilogue_2(NB - 2, k), 3 * NB - 2, NB - 2)
            copy_logits(NB - 2)
            dve.wait_ge(pv_done, 8 * UL)
            dve.sem_inc(be2_may_load, 1)
            for k in range(4):
                epilogue_2(NB - 1, k)
            xT_low(3 * NB - 1, NB - 1)
            copy_logits(NB - 1)

            steps = [0]

            def link(instruction):
                steps[0] += 1
                instruction.then_inc(gate_step, 1)
                dve.wait_ge(gate_step, steps[0])

            shape = [P, NB * NT, NX]
            dve.wait_ge(logits_copied, NB)
            link(dve.tensor_reduce(gate_1[0][:], logits[:], axis=X, op=ALU.max))
            link(dve.tensor_tensor(gate[0][:], logits[:], gate_1[0][:].unsqueeze(2).to_broadcast(shape), ALU.subtract))
            dve.wait_ge(gate_exp, 1)
            link(dve.tensor_reduce(gate_1[0][:], gate[1][:], axis=X, op=ALU.add))
            link(dve.reciprocal(gate_1[1][:], gate_1[0][:]))
            raw = gate[1]
            link(dve.tensor_tensor(raw[:], gate[1][:], gate_1[1][:].unsqueeze(2).to_broadcast(shape), ALU.mult))
            link(dve.memset(beats[:], 0.0))
            for j in range(NX):
                for lo, hi, op in ((0, j, ALU.is_gt), (j + 1, NX, ALU.is_ge)):
                    if hi > lo:
                        last = dve.tensor_tensor(beats[:, :, j, lo:hi],
                                                 raw[:, :, j:j + 1].to_broadcast([P, NB * NT, hi - lo]),
                                                 raw[:, :, lo:hi], op)
            link(last)
            link(dve.tensor_reduce(gate[2][:], beats[:].rearrange("p t j e -> p t e j"), axis=X, op=ALU.add))
            link(dve.tensor_scalar(gate[2][:], gate[2][:], 1.5, None, ALU.is_lt))
            chosen = gate[2]
            link(dve.tensor_copy(beats[:, :, 0], chosen[:]))
            link(dve.tensor_reduce(gate_1[2][:], raw[:], axis=X, op=ALU.max))
            link(dve.memset(gate_1[3][:], 0.0))
            link(dve.tensor_tensor(gate[0][:], raw[:], gate_1[2][:].unsqueeze(2).to_broadcast(shape), ALU.subtract))
            dve.wait_ge(gate_exp, 2)
            link(dve.tensor_tensor(gate[0][:], gate[2][:], beats[:, :, 0], ALU.mult))
            link(dve.tensor_reduce(gate_1[0][:], gate[0][:], axis=X, op=ALU.add))
            link(dve.reciprocal(gate_1[1][:], gate_1[0][:]))
            link(dve.tensor_tensor(gate[0][:], gate[0][:], gate_1[1][:].unsqueeze(2).to_broadcast(shape), ALU.mult))
            comb = gate[0]
            dve.wait_ge(be2_in, 16)

            with dve.Fori(0, NB // 2) as g:
                dve.tensor_copy(comb_tg[:], comb[:, bass.ds(4 * g, 4)]).then_inc(comb_set, 1)
                dve.wait_ge(comb_set, g + 1)
                for e in range(NX):
                    for t in range(4):
                        prev = y[:, bass.ds(2 * g + t // 2, 1), t % 2].rearrange("p b e -> p (b e)") if e == 0 \
                            else acc[:, t // 2, t % 2]
                        last = dve.scalar_tensor_tensor(acc[:, t // 2, t % 2], be2_sb[:, e], comb_tg[:, t, e:e + 1],
                                                        prev, ALU.mult, ALU.add)
                    last.then_inc(acc_step, 1)
                    dve.wait_ge(acc_step, 4 * g + e + 1)

                def gelu_low(m):
                    dve.wait_ge(gelu_high_done, 8 * g + m + 1)
                    dve.tensor_tensor(gelu_part[1][:, m % 4], gelu_full[m % 2], gelu_part[0][:, m % 4].bitcast(F32),
                                      ALU.subtract).then_inc(gelu_low_done, 1)

                def add_expert(e):
                    for p in range(2):
                        dve.wait_ge(moe_done, 8 * g + 2 * e + p + 1)
                        if e:
                            dve.wait_ge(moe_added, 8 * g + 2 * e + p - 1)
                        for t in range(2):
                            last = dve.scalar_tensor_tensor(acc[:, p, t], ps_tr[p][:, t * E:(t + 1) * E],
                                                            comb_tg[:, 2 * p + t, e:e + 1], acc[:, p, t], ALU.mult, ALU.add)
                        last.then_inc(moe_added, 1)

                for e in range(NX):
                    gelu_low(2 * e)
                    gelu_low(2 * e + 1)
                    if e:
                        add_expert(e - 1)
                add_expert(NX - 1)
                dve.wait_ge(moe_added, 8 * g + 8)
                for p in range(2):
                    b = 2 * g + p
                    dve.wait_ge(out_stored, 16 * b)
                    layer_norm(lambda t: acc[:, p, t], tile_of(xn), 5 * NB + b).then_inc(z_done, 1)
                    dve.wait_ge(z_done, NB + b + 1)
                    dve.wait_ge(res_in, 16 * (2 * NB + b) + 16)
                    dve.tensor_tensor(xn[:].rearrange("p t e -> p (t e)"), res[:].rearrange("p t e -> p (t e)"),
                                      xn[:].rearrange("p t e -> p (t e)"), ALU.add).then_inc(out_ready, 1)
                    dve.wait_ge(out_ready, b + 1)
                    dve.sem_inc(res_free, 1)

        @block.tensor
        def _(pe):
            pe.wait_ge(const_in, 16 * 10)

            def project(V, i, layer):
                m, t = i // 2, i % 2
                if i == 0:
                    pe.wait_ge(xq_in, 32 * V + 32)
                if i == 4:
                    pe.wait_ge(xv_in, 32 * V + 32)
                if isinstance(V, int) and V == 0:
                    pe.wait_ge(w_split, 2 * m + 2)
                    if i >= 2:
                        pe.wait_ge(qk_ready, i - 1)
                else:
                    if i == 0:
                        pe.wait_ge(w_split, V + STEPS)
                    if i < 2:
                        pe.wait_ge(v_copied, 2 * V - 1 + i)
                    elif layer == 0:
                        pe.wait_ge(qk_ready, 4 * V + i - 1)
                    else:
                        pe.wait_ge(qk_biased, 4 * (V - UL) + i - 1)
                src = xv_part if m == 2 else xq_part
                n = 0
                for c in range(NE):
                    for a, w in PASSES:
                        last = pe.matmul(ps_proj[i % 2][:], src[a][:, c, t * P:(t + 1) * P], w_cols(V, 2 * m + c, 0, GW, w),
                                         start=(n == 0), stop=(n == 5))
                        n += 1
                last.then_inc(proj_done, 1)

            def transpose_qk(U, j):
                which, pair = j % 2, j // 2
                if j == 0:
                    pe.wait_ge(qk_ready, 4 * U + 4)
                if j < 2:
                    pe.wait_ge(probsT_copied, 4 * U)
                else:
                    pe.wait_ge(qkT_low_done, 4 * U + j - 1)
                for hh in range(2):
                    for t in range(NT):
                        h = 2 * pair + hh
                        last = pe.transpose(ps_tr[j % 2][:, hh * T + t * P:hh * T + (t + 1) * P],
                                            qk[:, 2 * which + t, h * D:(h + 1) * D], ident_sb[:])
                last.then_inc(tr_done, 1)

            def scores(U, h, layer, bank_free=None):
                if h % 2 == 0:
                    pe.wait_ge(qkT_low_done, 4 * U + h + 2)
                if bank_free is not None:
                    pe.wait_ge(*bank_free)
                if h >= 2:
                    pe.wait_ge(exp_done, 4 * U + h - 1)
                else:
                    pe.wait_ge(exp_done, 4 * U)
                for t in range(NT):
                    n = T if layer == 0 or t else P
                    dst = ps_s[h % 2][:, t * T:t * T + n]
                    for a, w in PASSES:
                        last = pe.matmul(dst, qkT_part[a][:, 0, h, t * P:(t + 1) * P], qkT_part[w][:, 1, h, 0:n],
                                         start=((a, w) == PASSES[0]), stop=((a, w) == PASSES[-1]))
                    if layer == 1:
                        last = pe.matmul(ps_s[h % 2][:, t * T + n - P:t * T + n], mask_sb[:, 0], mask_sb[:, 1],
                                         start=False, stop=True, skip_group_check=True)
                last.then_inc(s_done, 1)

            def transpose_probs(U, h, layer):
                pe.wait_ge(probs_done, 4 * U + h + 1)
                if h < 2:
                    pe.wait_ge(qkT_low_done, 4 * U + 3 + h)
                else:
                    pe.wait_ge(probsT_copied, 4 * U + h - 1)
                for k in range(NT):
                    for q in range(NT):
                        if layer == 0 or k <= q:
                            last = pe.transpose(ps_tr[h % 2][:, k * T + q * P:k * T + (q + 1) * P],
                                                probs[:, h, q, k * P:(k + 1) * P], ident_sb[:])
                last.then_inc(tr_done, 1)

            def probs_v(U, h, layer):
                pe.wait_ge(probsT_copied, 4 * U + h + 1)
                if h == 0:
                    pe.wait_ge(v_copied, 2 * U + 2)
                    pe.wait_ge(o_low_done, 2 * U)
                if h == 2:
                    pe.wait_ge(o_low_done, 2 * U + 1)
                base = (h % 2) * T
                pe.matmul(ps_o[:, base:base + T], v[:, 0, h * D:(h + 1) * D], probsT[:, h % 2, 0], start=True, stop=(layer == 1))
                q0 = 0 if layer == 0 else P
                pe.matmul(ps_o[:, base + q0:base + T], v[:, 1, h * D:(h + 1) * D], probsT[:, h % 2, 1, q0:T],
                          start=False, stop=True, skip_group_check=(layer == 1)).then_inc(pv_done, 1)

            def out_project(U, h):
                if h == 0:
                    pe.wait_ge(y_added, U)
                if h % 2 == 0:
                    pe.wait_ge(o_low_done, 2 * U + h // 2 + 1)
                for t in range(NT):
                    for a, w in PASSES:
                        last = pe.matmul(ps_y[:, t * E:(t + 1) * E], oT_part[a][:, h, t * P:(t + 1) * P],
                                         w_cols(U, 6 + h // 2, (h % 2) * E, E, w),
                                         start=(h == 0 and t == 0 and (a, w) == (0, 0)), stop=(h == GH - 1),
                                         skip_group_check=True)
                if h == GH - 1:
                    last.then_inc(y_done, 1)

            def transpose_x(n, U=None):
                pe.wait_ge(xn_ready, n + 1)
                if U is not None:
                    pe.wait_ge(exp_done, 4 * U + 3)
                for c in range(NE):
                    for t in range(NT):
                        last = pe.transpose(ps_s[0][:, c * T + t * P:c * T + (t + 1) * P], xn[:, t, c * P:(c + 1) * P], ident_sb[:])
                last.then_inc(xT_done, 1)

            def gate_logits(b):
                pe.wait_ge(xT_copied, 2 * NB + b + 1)
                for t in range(NT):
                    for c in range(NE):
                        last = pe.matmul(ps_s[1][:, t * NX:(t + 1) * NX], xT_full[:, c, t * P:(t + 1) * P], w_gate_sb[:, c],
                                         start=(c == 0), stop=(c == NE - 1))
                last.then_inc(logits_done, 1)

            def unit_1(U, nl, xT_count, n=None):
                V = U + 1
                transpose_qk(U, 0)
                transpose_qk(U, 1)
                project(V, 0, nl)
                transpose_qk(U, 2)
                scores(U, 0, 0, (xT_copied, xT_count))
                transpose_qk(U, 3)
                scores(U, 1, 0)
                project(V, 1, nl)
                project(V, 2, nl)
                transpose_probs(U, 0, 0)
                scores(U, 2, 0)
                scores(U, 3, 0)
                probs_v(U, 0, 0)
                transpose_probs(U, 1, 0)
                project(V, 3, nl)
                probs_v(U, 1, 0)
                transpose_probs(U, 2, 0)
                project(V, 4, nl)
                transpose_probs(U, 3, 0)
                out_project(U, 0)
                probs_v(U, 2, 0)
                probs_v(U, 3, 0)
                project(V, 5, nl)
                out_project(U, 1)
                if n is not None:
                    transpose_x(n, U)
                out_project(U, 2)
                out_project(U, 3)

            def unit_2(U, nl, xT_count, n=None, logits_count=0):
                V = U + 1
                transpose_qk(U, 0)
                transpose_qk(U, 1)
                if nl:
                    project(V, 0, nl)
                transpose_qk(U, 2)
                scores(U, 0, 1, (xT_copied, xT_count))
                transpose_qk(U, 3)
                scores(U, 1, 1, (logits_copied, logits_count))
                if nl:
                    project(V, 1, nl)
                    project(V, 2, nl)
                transpose_probs(U, 0, 1)
                scores(U, 2, 1)
                transpose_probs(U, 1, 1)
                scores(U, 3, 1)
                probs_v(U, 0, 1)
                probs_v(U, 1, 1)
                if nl:
                    project(V, 3, nl)
                    project(V, 4, nl)
                transpose_probs(U, 2, 1)
                transpose_probs(U, 3, 1)
                out_project(U, 0)
                probs_v(U, 2, 1)
                probs_v(U, 3, 1)
                out_project(U, 1)
                if nl:
                    project(V, 5, nl)
                if n is not None:
                    transpose_x(n, U)
                out_project(U, 2)
                out_project(U, 3)

            transpose_x(0)
            for b in range(1, PRE):
                pe.wait_ge(xT_copied, b)
                transpose_x(b)
            for i in range(6):
                project(0, i, 0)
            with pe.Fori(0, NB - PRE) as U:
                unit_1(U, 0, U + PRE, U + PRE)
            with pe.Fori(NB - PRE, LAG) as U:
                unit_1(U, 0, NB)
            with pe.Fori(LAG, UL - 1) as U:
                unit_1(U, 0, U - LAG + NB, U - LAG + NB)
            unit_1(UL - 1, 1, 2 * NB - 2, 2 * NB - 2)
            unit_2(UL, 1, 2 * NB - 1, 2 * NB - 1)
            with pe.Fori(UL + 1, UL + LAG) as U:
                unit_2(U, 1, 2 * NB)
            with pe.Fori(UL + LAG, 2 * UL - 1) as U:
                unit_2(U, 1, U - UL - LAG + 2 * NB, U - UL - LAG + 2 * NB, U - UL - LAG)
                gate_logits(U - UL - LAG)
            unit_2(2 * UL - 1, None, 3 * NB - 2, 3 * NB - 2, NB - 2)
            gate_logits(NB - 2)
            transpose_x(3 * NB - 1)
            pe.wait_ge(logits_copied, NB - 1)
            gate_logits(NB - 1)

            pe.wait_ge(w_split, NSTEP)
            pe.wait_ge(xT_ready, 3 * NB)
            with pe.Fori(0, NB // 2) as g:
                def expert_in(m):
                    e, ic = m // 2, m % 2
                    pe.wait_ge(gelu_done, 8 * g + (m - 1 if m >= 2 else 0))
                    n = 0
                    for c in range(NE):
                        for a, w in PASSES:
                            last = pe.matmul(ps_proj[m % 2][:].rearrange("p (b t) -> p b t", b=2),
                                             w_part[a][:, (2 * e) * GW + c * IM + ic * P:(2 * e) * GW + c * IM + (ic + 1) * P],
                                             xT_part[w][:, bass.ds(2 * g, 2), c], start=(n == 0), stop=(n == 5))
                            n += 1
                    last.then_inc(h1_done, 1)

                def expert_out(e):
                    pe.wait_ge(gelu_low_done, 8 * g + 2 * e + 2)
                    for p in range(2):
                        pe.wait_ge(moe_added, 8 * g + (2 * e - 1 + p if e else 0))
                        for t in range(2):
                            n = 0
                            for ic in range(2):
                                for a, w in PASSES:
                                    lo = (2 * e + 1) * GW + ic * E
                                    last = pe.matmul(ps_tr[p][:, t * E:(t + 1) * E],
                                                     gelu_part[a][:, (2 * e + ic) % 4, (2 * p + t) * P:(2 * p + t + 1) * P],
                                                     w_part[w][:, lo:lo + E], start=(n == 0), stop=(n == 5))
                                    n += 1
                        last.then_inc(moe_done, 1)

                for e in range(NX):
                    expert_in(2 * e)
                    expert_in(2 * e + 1)
                    if e:
                        expert_out(e - 1)
                expert_out(NX - 1)
    return nc


def kernel(**inputs):
    import concourse.bacc as _bacc
    from concourse.bass_utils import run_bass_kernel_spmd as _run

    a = {k.replace("L0_", ""): np.asarray(v_) for k, v_ in inputs.items()}

    pieces = []
    for blk in ("attn", "ffn"):
        wq, wk, wv, wo = (a[f"{blk}_w{c}"] for c in "qkvo")
        wo = wo.reshape(H, D, E)
        for g in range(NG):
            for w in (wq, wk, wv):
                w = w.reshape(E, H * D)[:, g * GW:(g + 1) * GW]
                pieces += [w[0:P], w[P:2 * P]]
            for j in range(2):
                pieces.append(wo[g * GH + 2 * j:g * GH + 2 * j + 2].transpose(1, 0, 2).reshape(P, GW))
    for e in range(NX):
        for w in (a["ffn_we1"][e], a["ffn_we2"][e]):
            pieces.append(w.reshape(2, P, 256).transpose(1, 0, 2).reshape(P, GW))

    def column(v_):
        return np.ascontiguousarray(v_.reshape(-1, P).T)

    inv_freq = (1.0 / 10000.0 ** (np.arange(0, D, 2, dtype=np.float32) / np.float32(D))).astype(np.float32)
    angle = np.arange(T, dtype=np.float32)[:, None] * inv_freq[None, :]
    cos, sin = np.cos(angle), np.sin(angle)
    rope = np.stack([np.concatenate([cos, cos], 1), np.concatenate([-sin, sin], 1)])
    rope = rope.reshape(2, NT, P, D).transpose(2, 0, 1, 3).astype(np.float32)
    bf16 = mybir.dt.np(BF16) if hasattr(mybir.dt, "np") else __import__("ml_dtypes").bfloat16
    fill = np.where(np.arange(P)[:, None] >= np.arange(P)[None, :], 0.0, -3.0e38)
    masks = np.stack([np.eye(P), fill], 1).astype(bf16)

    arrays = {
        "x": a["attn_x"],
        "weights": np.stack(pieces),
        "qk_scale": np.stack([a["attn_q_scale"], a["attn_k_scale"]], 1),
        "bias_qk": np.concatenate([a["ffn_bq"].reshape(NG, GW), a["ffn_bk"].reshape(NG, GW)], 1),
        "bv": column(a["ffn_bv"]),
        "bo": a["ffn_bo"],
        "ln1": np.stack([column(a["ffn_ln1_w"]), column(a["ffn_ln1_b"])], 1),
        "ln2": np.stack([column(a["ffn_ln2_w"]), column(a["ffn_ln2_b"])], 1),
        "w_gate": a["ffn_w_gate"].reshape(NE, P, NX).transpose(1, 0, 2),
        "be1": a["ffn_be1"].reshape(NX * IM // P, P).T,
        "be2": a["ffn_be2"].reshape(-1),
        "rope": rope,
        "masks": masks,
        "ident": np.eye(P, dtype=np.float32),
    }
    nc = _bacc.Bacc("TRN2", target_bir_lowering=False, num_devices=1)
    arrays = {f"in_{k}": np.ascontiguousarray(v_) for k, v_ in arrays.items()}
    args = [nc.dram_tensor(k, v_.shape, mybir.dt.from_np(v_.dtype), kind="ExternalInput").ap() for k, v_ in arrays.items()]
    out = nc.dram_tensor("out", (NB, T, E), F32, kind="ExternalOutput").ap()
    build(nc, *args, out)
    r = _run(nc, [arrays], core_ids=[0])
    return r.results[0]["out"]
```

```python
from contextlib import ExitStack

import numpy as np
import concourse.bass as bass
from concourse import mybir

F32 = mybir.dt.float32
F32R = mybir.dt.float32r
BF16 = mybir.dt.bfloat16
ALU = mybir.AluOpType
ACT = mybir.ActivationFunctionType
X = mybir.AxisListType.X

P = 128
NB, T, E = 8, 256, 256
H, D = 16, 128
GH = 4
NG = H // GH
NT, NE = T // P, E // P
UL = NG * NB
GW = GH * D
NX, IM = 4, 256
STEPS = 8
SLOTS = 2 * STEPS
NSTEP = (2 * NG + 1) * STEPS
AHEAD = STEPS + 1
LAG = UL - NB + 1
PRE = 3
LN_EPS, RMS_EPS = 1e-5, 1e-6
GATE_TILES = (slice(0, (NB - 1) * NT), slice((NB - 1) * NT, NB * NT))
GATE_STEPS, GATE_EXP_STEPS = 15, (2, 12)
PASSES = ((0, 0), (0, 1), (1, 0))


def build(nc, x, weights, qk_scale, bias_qk, bv, bo, ln1, ln2, w_gate, be1, be2, rope, masks, ident, out):
    x1_dram = nc.dram_tensor("x1_dram", (NB, P, NT, E), F32).ap()
    x_d = x.rearrange("b (t p) e -> b p t e", p=P)
    out_d = out.rearrange("b (t p) e -> b p t e", p=P)

    with ExitStack() as ctx:
        def sb(name, shape, dt=F32):
            return ctx.enter_context(nc.sbuf_tensor(name, [P, *shape], dt))

        def sem(name):
            return ctx.enter_context(nc.semaphore(name))

        w_part = [sb("w_high", [SLOTS * GW], F32R), sb("w_low", [SLOTS * GW], F32R)]
        w_stage = sb("w_stage", [2 * GW])
        xT_part = [sb("xT_high", [NB, NE, T], F32R), sb("xT_low", [NB, NE, T], F32R)]
        xq_part = [sb("xq_high", [NE, T], F32R), sb("xq_low", [NE, T], F32R)]
        xv_part = [sb("xv_high", [NE, T], F32R), sb("xv_low", [NE, T], F32R)]
        y = sb("y", [NB, NT, E])
        bias_sb = sb("bias_sb", [2 * GW])
        qk = sb("qk", [4, GW])
        scratch = sb("scratch", [2, GW])
        rot_a = sb("rot_a", [2, GW])
        rot_b = sb("rot_b", [2, GW])
        sumsq = sb("sumsq", [4, GH])
        meansq = sb("meansq", [4, GH])
        rstd_qk = sb("rstd_qk", [4, GH])
        qkT_part = [sb("qkT_high", [2, GH, T], F32R), sb("qkT_low", [2, GH, T], F32R)]
        v = sb("v", [NT, GW])
        probs = sb("probs", [GH, NT, T])
        neg_max = sb("neg_max", [GH, NT])
        row_sum = sb("row_sum", [GH, NT])
        inv_sum = sb("inv_sum", [GH, NT])
        probsT = sb("probsT", [2, NT, T])
        oT_part = [sb("oT_high", [GH, T], F32R), sb("oT_low", [GH, T], F32R)]
        res = sb("res", [NT, E])
        xn = sb("xn", [NT, E])
        xT_full = sb("xT_full", [NE, T])
        stats, mean_var, var_eps, rstd = ([sb(f"{name}{i}", shape) for i in range(2)] for name, shape in (
            ("stats", [NT, 6]), ("mean_var", [NT, 2]), ("var_eps", [NT]), ("rstd", [NT])))
        minus_half = sb("minus_half", [16])
        eps_sum = sb("eps_sum", [GH])
        pause = sb("pause", [1])
        ident_sb = sb("ident_sb", [P])
        mask_sb = sb("mask_sb", [2, P], BF16)
        rope_sb = sb("rope_sb", [2, NT, D])
        qk_scale_sb = sb("qk_scale_sb", [2])
        qk_root_sb = sb("qk_root_sb", [2])
        bv_sb = sb("bv_sb", [H])
        bo_sb = sb("bo_sb", [E])
        ln_sb = sb("ln_sb", [2, 2, NE])
        w_gate_sb = sb("w_gate_sb", [NE, NX])
        logits = sb("logits", [NB * NT, NX])
        be1_sb = sb("be1_sb", [NX * NE])
        gate = [sb(f"gate{i}", [NB * NT, NX]) for i in range(3)]
        gate_1 = [sb(f"gate_1{i}", [NB * NT]) for i in range(3)]
        base_sum = sb("base_sum", [2, NT, E])
        beats = sb("beats", [NB * NT, NX, NX])
        first_x = [res, *(rot_b[:, i].rearrange("p (t e) -> p t e", t=NT) for i in range(2))]
        first_xn = [xn, *(rot_a[:, i].rearrange("p (t e) -> p t e", t=NT) for i in range(2))]
        first_w = y[:].rearrange("p b t e -> p (b t e)")
        gelu_full = [scratch[:, i, :] for i in range(2)]
        last_x = [res, w_stage[:, 0:GW].rearrange("p (t e) -> p t e", t=NT)]
        last_out = [xn, w_stage[:, GW:2 * GW].rearrange("p (t e) -> p t e", t=NT)]
        bias_terms = [rot_a[:, 0, :], rot_a[:, 1, :], rot_b[:, 0, :], rot_b[:, 1, :]]
        gelu_part = [w[:, STEPS * GW:(STEPS + 4) * GW].rearrange("p (s c) -> p s c", s=4) for w in w_part]
        be2_sb = probs[:, :, :, :].rearrange("p a b c -> p (a b c)")[:, 0:NX * E].rearrange("p (x e) -> p x e", x=NX)

        def bank(name):
            return ctx.enter_context(nc.psum_tensor(name, [P, 512], F32))
        ps_proj = [bank("ps_proj0"), bank("ps_proj1")]
        ps_tr = [bank("ps_tr0"), bank("ps_tr1")]
        ps_s = [bank("ps_s0"), bank("ps_s1")]
        ps_o = bank("ps_o")
        ps_y = bank("ps_y")
        ps_first = [*ps_proj, ps_o, ps_y, ps_tr[1], ps_s[0]]
        ps_first_x = [ps_s[0], ps_s[1], ps_tr[0]]
        ps_expert = [ps_tr, [ps_o, ps_y], ps_s, [ps_o, ps_y]]

        ident_in = sem("ident_in")
        const_in = sem("const_in")
        first_w_in = sem("first_w_in")
        eps_set = sem("eps_set")
        root_set = sem("root_set")
        w_in = sem("w_in")
        w_high_done = sem("w_high_done")
        w_split = sem("w_split")
        bias_in = sem("bias_in")
        xq_in = sem("xq_in")
        xv_in = sem("xv_in")
        proj_done = sem("proj_done")
        sq_done = sem("sq_done")
        sumsq_done = sem("sumsq_done")
        meansq_done = sem("meansq_done")
        rstd_qk_done = sem("rstd_qk_done")
        qk_biased = sem("qk_biased")
        rot_a_done = sem("rot_a_done")
        rot_b_done = sem("rot_b_done")
        qk_ready = sem("qk_ready")
        v_copied = sem("v_copied")
        tr_done = sem("tr_done")
        qkT_high_done = sem("qkT_high_done")
        qkT_low_done = sem("qkT_low_done")
        s_done = sem("s_done")
        max_done = sem("max_done")
        exp_done = sem("exp_done")
        inv_done = sem("inv_done")
        probs_done = sem("probs_done")
        probsT_copied = sem("probsT_copied")
        pv_done = sem("pv_done")
        o_high_done = sem("o_high_done")
        o_low_done = sem("o_low_done")
        y_done = sem("y_done")
        y_added = sem("y_added")
        res_in = sem("res_in")
        res_free = sem("res_free")
        x1_ready = sem("x1_ready")
        x1_out = sem("x1_out")
        ln_stats = sem("ln_stats")
        ln_aggr = sem("ln_aggr")
        ln_var = sem("ln_var")
        ln_rstd = sem("ln_rstd")
        h0_done = sem("h0_done")
        z_done = sem("z_done")
        y_set = sem("y_set")
        xn_ready = sem("xn_ready")
        xT_done = sem("xT_done")
        xT_copied = sem("xT_copied")
        xT_high_done = sem("xT_high_done")
        xT_ready = sem("xT_ready")
        logits_done = sem("logits_done")
        logits_copied = sem("logits_copied")
        gate_step = sem("gate_step")
        gate_exp = sem("gate_exp")
        be2_in = sem("be2_in")
        comb_ready = sem("comb_ready")
        terms_done = sem("terms_done")
        base_step = sem("base_step")
        base_added = sem("base_added")
        h1_done = sem("h1_done")
        gelu_done = sem("gelu_done")
        gelu_high_done = sem("gelu_high_done")
        gelu_low_done = sem("gelu_low_done")
        moe_done = sem("moe_done")
        moe_added = sem("moe_added")
        out_ready = sem("out_ready")
        out_stored = sem("out_stored")

        block = ctx.enter_context(nc.Block())


        def w_cols(base, step, lo, n, part):
            return w_part[part][:, bass.ds(base + step * GW + lo, n)]

        def seq(unit):
            return unit % NB

        def first_head(engine, U):
            head = ((U - UL) // NB) * GH
            return head if isinstance(head, int) else engine.snap(head)

        def qkT_of(part, which, pair):
            return qkT_part[part][:, which, 2 * pair:2 * pair + 2].rearrange("p h t -> p (h t)")

        def score_scale(which, layer):
            if layer == 0:
                return qk_root_sb[:, which:which + 1]
            return float(D) ** -0.5 if which == 0 else 1.0

        @block.sync
        def _(sp):
            def load_weight(s):
                if not isinstance(s, int) or s > STEPS:
                    sp.wait_ge(w_split, s)
                sp.dma_start(w_stage[:, bass.ds((s % 2) * GW, GW)],
                             weights[bass.ds(s, 1)].rearrange("s p c -> p (s c)")).then_inc(w_in, 16)

            def load_first_weights(lo, hi):
                sp.dma_start(first_w[:, lo * GW:hi * GW].rearrange("p (s c) -> p s c", c=GW),
                             weights[lo:hi].rearrange("s p c -> p s c")).then_inc(first_w_in, 16)

            def load_xq(V):
                for part in range(2):
                    sp.dma_start(xq_part[part][:].bitcast(F32), xT_part[part][:, bass.ds(seq(V), 1)]
                                 .rearrange("p b c t -> p (b c) t").bitcast(F32)).then_inc(xq_in, 16)

            def load_xv(V):
                for part in range(2):
                    sp.dma_start(xv_part[part][:].bitcast(F32), xT_part[part][:, bass.ds(seq(V), 1)]
                                 .rearrange("p b c t -> p (b c) t").bitcast(F32)).then_inc(xv_in, 16)

            def load_bias(g):
                if g:
                    sp.wait_ge(qk_biased, 4 * g * NB)
                    sp.wait_ge(bias_in, 16 * g)
                sp.dma_start(bias_sb[:], bias_qk[g:g + 1, :].rearrange("g c -> (g c)").partition_broadcast(P)).then_inc(bias_in, 16)

            sp.dma_start(first_x[0][:], x_d[0]).then_inc(res_in, 16)
            load_first_weights(0, 2)
            sp.wait_ge(res_in, 16)
            sp.dma_start(first_x[1], x_d[1]).then_inc(res_in, 16)
            sp.wait_ge(first_w_in, 16)
            load_first_weights(2, STEPS)
            sp.wait_ge(res_in, 32)
            sp.dma_start(first_x[2], x_d[2]).then_inc(res_in, 16)
            for dst, src in ((qk_scale_sb[:], qk_scale), (mask_sb[:], masks), (rope_sb[:], rope), (bv_sb[:], bv),
                             (bo_sb[:], bo.partition_broadcast(P)), (ln_sb[:, 0], ln1), (ln_sb[:, 1], ln2),
                             (w_gate_sb[:], w_gate), (be1_sb[:], be1)):
                sp.dma_start(dst, src).then_inc(const_in, 16)
            load_weight(STEPS)
            sp.wait_ge(xT_ready, 2)
            load_xq(1)

            def unit(U, xT_count=None, bias=None, x1=None):
                V = U + 1
                sp.wait_ge(proj_done, 6 * U + 6)
                load_xv(V)
                load_weight(U + AHEAD)
                if x1 is not None:
                    store_x1(x1)
                if not (isinstance(V, int) and V == 2 * UL - 1):
                    sp.wait_ge(proj_done, 6 * V + 4)
                    if xT_count is not None:
                        sp.wait_ge(xT_ready, xT_count)
                    load_xq(V + 1)
                    if bias is not None:
                        load_bias(bias)

            def load_x(b):
                sp.wait_ge(res_free, b)
                sp.dma_start(res[:], x_d[bass.ds(b, 1)].rearrange("b p t e -> p (b t) e")).then_inc(res_in, 16)

            def first_epilogue(b):
                sp.wait_ge(res_free, b + NB)
                sp.dma_start(res[:], x_d[bass.ds(b, 1)].rearrange("b p t e -> p (b t) e")).then_inc(res_in, 16)

            def store_x1(b):
                sp.wait_ge(x1_ready, b + 1)
                sp.dma_start(x1_dram[bass.ds(b, 1)].rearrange("b p t e -> p (b t) e"), res[:]).then_inc(x1_out, 16)
                sp.wait_ge(x1_out, 16 * b + 16)

            load_x(PRE)
            unit(0, PRE)
            with sp.Fori(1, NB - PRE) as U:
                load_x(U + PRE)
                unit(U, U + PRE)
            with sp.Fori(NB - PRE, LAG) as U:
                unit(U)
            load_bias(0)
            with sp.Fori(LAG, UL - 1) as U:
                first_epilogue(U - LAG)
                unit(U, U - LAG + NB, x1=U - LAG)
            first_epilogue(NB - 2)
            unit(UL - 1, NB + 2, x1=NB - 2)
            first_epilogue(NB - 1)
            unit(UL, NB + 3, x1=NB - 1)
            sp.wait_ge(xT_ready, 2 * NB)
            for g in range(NG):
                with sp.Fori(UL + max(g * NB - 1, 1), UL + (g + 1) * NB - 2) as U:
                    unit(U)
                if g + 1 < NG:
                    unit(UL + (g + 1) * NB - 2, bias=g + 1)
                else:
                    unit(2 * UL - 2)

            sp.wait_ge(tr_done, 8 * 2 * UL)
            sp.dma_start(be2_sb, be2.partition_broadcast(P).rearrange("p (x e) -> p x e", x=NX)).then_inc(be2_in, 16)
            sp.wait_ge(w_split, NSTEP)
            with sp.Fori(0, NB // 2) as g:
                sp.wait_ge(res_free, 2 * g + 2 * NB)
                for p in range(2):
                    sp.dma_start(last_x[p][:],
                                 x1_dram[bass.ds(2 * g + p, 1)].rearrange("b p t e -> p (b t) e")).then_inc(res_in, 16)
                    sp.wait_ge(res_in, 32 * g + 16 * (2 * NB + p + 1))
                for p in range(2):
                    sp.wait_ge(out_ready, 2 * g + p + 1)
                    sp.dma_start(out_d[bass.ds(2 * g + p, 1)].rearrange("b p t e -> p (b t) e"),
                                 last_out[p][:]).then_inc(out_stored, 16)
            sp.wait_ge(x1_out, 16 * NB)
            sp.wait_ge(out_stored, 16 * NB)

        @block.gpsimd
        def _(pool):
            pool.memset(minus_half[:], -0.5)
            pool.memset(eps_sum[:], D * RMS_EPS).then_inc(eps_set, 1)
            pool.wait_ge(eps_set, 1)

            def w_slot(part, s):
                return w_part[part][:, bass.ds((s % SLOTS) * GW, GW)]

            def split_weight(s, half):
                src = w_stage[:, bass.ds((s % 2) * GW, GW)]
                if half == 0:
                    pool.wait_ge(w_in, 16 * (s - STEPS) + 16)
                    pool.tensor_copy(w_slot(0, s), src).then_inc(w_high_done, 1)
                else:
                    pool.wait_ge(w_high_done, s + 1)
                    pool.tensor_tensor(w_slot(1, s), src, w_slot(0, s).bitcast(F32), ALU.subtract).then_inc(w_split, 1)

            def ln_power(k, i=0):
                pool.wait_ge(ln_var, k + 1)
                pool.tensor_tensor(rstd[i][:], var_eps[i][:], minus_half[:, 0:NT], ALU.pow).then_inc(ln_rstd, 1)

            def xT_low(n, b):
                low = xT_part[1][:, bass.ds(b, 1)].rearrange("p b c t -> p (b c t)")
                high = xT_part[0][:, bass.ds(b, 1)].rearrange("p b c t -> p (b c t)").bitcast(F32)
                pool.wait_ge(xT_high_done, n + 1)
                pool.tensor_tensor(low, xT_full[:].rearrange("p c t -> p (c t)"), high, ALU.subtract).then_inc(xT_ready, 1)

            def residual_x1(b):
                pool.wait_ge(z_done, b + 1)
                pool.wait_ge(res_in, 16 * (NB + b) + 16)
                pool.tensor_tensor(res[:].rearrange("p t e -> p (t e)"), res[:].rearrange("p t e -> p (t e)"),
                                   xn[:].rearrange("p t e -> p (t e)"), ALU.add).then_inc(x1_ready, 1)

            def start_y(b):
                pool.wait_ge(h0_done, b + 1)
                pool.tensor_tensor(y[:, bass.ds(b, 1)].rearrange("p b t e -> p (b t) e"), xn[:],
                                   bo_sb[:].unsqueeze(1).to_broadcast([P, NT, E]), ALU.add).then_inc(y_set, 1)

            def rms_power(V, i):
                pool.wait_ge(sumsq_done, 4 * V + i + 1)
                pool.tensor_tensor(meansq[:, i], sumsq[:, i], eps_sum[:], ALU.add).then_inc(meansq_done, 1)
                pool.wait_ge(meansq_done, 4 * V + i + 1)
                pool.tensor_tensor(rstd_qk[:, i], meansq[:, i], minus_half[:, 0:GH], ALU.pow).then_inc(rstd_qk_done, 1)

            def rotate_a(V, i):
                n = 4 * (V - UL) + i
                pool.wait_ge(qk_biased, n + 1)
                if not isinstance(V, int) or V > UL or i >= 2:
                    pool.wait_ge(qk_ready, 4 * V + i - 1)
                cos = rope_sb[:, 0, i % 2].unsqueeze(1).to_broadcast([P, GH, D])
                pool.tensor_tensor(rot_a[:, i % 2].rearrange("p (h d) -> p h d", h=GH),
                                   scratch[:, i % 2].rearrange("p (h d) -> p h d", h=GH), cos,
                                   ALU.mult).then_inc(rot_a_done, 1)

            def qk_part(V, i, layer):
                rms_power(V, i) if layer == 0 else rotate_a(V, i)

            def split_high(U):
                pool.wait_ge(proj_done, 6 * U + 6)
                pool.wait_ge(y_done, U)
                split_weight(U + AHEAD, 0)

            def split_low(U):
                split_weight(U + AHEAD, 1)

            def unit_1(U):
                V = U + 1
                rms_power(V, 0)
                split_high(U)
                rms_power(V, 1)
                rms_power(V, 2)
                rms_power(V, 3)
                split_low(U)

            def unit_1_prologue(U, n, b, ln):
                V = U + 1
                rms_power(V, 0)
                split_high(U)
                ln_power(ln)
                rms_power(V, 1)
                rms_power(V, 2)
                xT_low(n, b)
                rms_power(V, 3)
                split_low(U)

            def unit_1_epilogue(U, nl, n, b, ln):
                V = U + 1
                ln_power(ln + 0)
                residual_x1(b)
                qk_part(V, 0, nl)
                qk_part(V, 1, nl)
                split_high(U)
                split_low(U)
                ln_power(ln + 1)
                qk_part(V, 2, nl)
                start_y(b)
                ln_power(ln + 2)
                qk_part(V, 3, nl)
                xT_low(n, b)

            def unit_2_first(U, n, b, ln):
                V = U + 1
                ln_power(ln + 0)
                residual_x1(b)
                rotate_a(V, 0)
                split_high(U)
                rotate_a(V, 1)
                split_low(U)
                ln_power(ln + 1)
                start_y(b)
                ln_power(ln + 2)
                rotate_a(V, 2)
                rotate_a(V, 3)
                xT_low(n, b)

            def unit_2(U):
                V = U + 1
                split_high(U)
                split_low(U)
                rotate_a(V, 0)
                rotate_a(V, 1)
                rotate_a(V, 2)
                rotate_a(V, 3)

            def unit_2_epilogue(U, nl, n, b, ln):
                V = U + 1
                if nl is not None:
                    rotate_a(V, 0)
                    rotate_a(V, 1)
                ln_power(ln)
                if nl is not None:
                    split_high(U)
                    rotate_a(V, 2)
                    rotate_a(V, 3)
                    split_low(U)
                xT_low(n, b)

            ln_power(0)
            ln_power(1)
            rms_power(0, 0)
            ln_power(2)
            for i in range(1, 4):
                rms_power(0, i)
            split_weight(STEPS, 0)
            split_weight(STEPS, 1)
            unit_1_prologue(0, PRE, PRE, PRE)
            with pool.Fori(1, NB - PRE) as U:
                unit_1_prologue(U, U + PRE, U + PRE, U + PRE)
            with pool.Fori(NB - PRE, LAG) as U:
                unit_1(U)
            with pool.Fori(LAG, UL - 1) as U:
                unit_1_epilogue(U, 0, U - LAG + NB, U - LAG, NB + 3 * (U - LAG))
            unit_1_epilogue(UL - 1, 1, 2 * NB - 2, NB - 2, NB + 3 * (NB - 2))
            unit_2_first(UL, 2 * NB - 1, NB - 1, NB + 3 * (NB - 1))
            with pool.Fori(UL + 1, UL + LAG) as U:
                unit_2(U)
            with pool.Fori(UL + LAG, 2 * UL - 1) as U:
                unit_2_epilogue(U, 1, U - UL - LAG + 2 * NB, U - UL - LAG, 4 * NB + U - UL - LAG)
            unit_2_epilogue(2 * UL - 1, None, 3 * NB - 2, NB - 2, 5 * NB - 2)
            ln_power(5 * NB - 1)

            def sum_bias_terms(g, p):
                b = 2 * g + p
                base = base_sum[:, p].rearrange("p t e -> p (t e)")
                pool.wait_ge(terms_done, b + 1)
                if not isinstance(g, int) or g:
                    pool.wait_ge(base_added, b - 1)
                pool.tensor_tensor(base, bias_terms[0], bias_terms[1], ALU.add)
                pool.tensor_tensor(bias_terms[2], bias_terms[2], bias_terms[3], ALU.add).then_inc(base_step, 1)
                pool.wait_ge(base_step, 2 * b + 1)
                pool.tensor_tensor(base, base, bias_terms[2], ALU.add).then_inc(base_step, 1)

            def add_expert_bias(g):
                for p in range(2):
                    b = 2 * g + p
                    pool.wait_ge(base_step, 2 * b + 2)
                    pool.wait_ge(moe_added, 8 * g + 5 + p)
                    y_b = y[:, bass.ds(b, 1)].rearrange("p b t e -> p (b t e)")
                    pool.tensor_tensor(y_b, y_b, base_sum[:, p].rearrange("p t e -> p (t e)"), ALU.add).then_inc(base_added, 1)

            for p in range(2):
                sum_bias_terms(0, p)
            with pool.Fori(0, NB // 2 - 1) as g:
                add_expert_bias(g)
                for p in range(2):
                    sum_bias_terms(g + 1, p)
                    ln_power(5 * NB + 2 * g + p, p)
            add_expert_bias(NB // 2 - 1)
            for p in range(2):
                ln_power(6 * NB - 2 + p, p)

        @block.scalar
        def _(act):
            act.dma_start(ident_sb[:], ident).then_inc(ident_in, 16)

            def copy_qkT(U, j, layer):
                which, pair = j % 2, j // 2
                act.wait_ge(tr_done, 8 * U + j + 1)
                act.activation(qkT_of(0, which, pair), ps_tr[j % 2][:], ACT.Copy,
                               scale=score_scale(which, layer)).then_inc(qkT_high_done, 1)

            def copy_probsT(U, h, layer):
                act.wait_ge(tr_done, 8 * U + 5 + h)
                if h < 2:
                    act.wait_ge(pv_done, 4 * U)
                else:
                    act.wait_ge(pv_done, 4 * U + h - 1)
                dst = probsT[:, h % 2].rearrange("p k q -> p (k q)")
                if layer == 0:
                    last = act.activation(dst, ps_tr[h % 2][:], ACT.Copy)
                else:
                    act.activation(dst[:, 0:T], ps_tr[h % 2][:, 0:T], ACT.Copy)
                    last = act.activation(dst[:, T + P:2 * T], ps_tr[h % 2][:, T + P:2 * T], ACT.Copy)
                last.then_inc(probsT_copied, 1)

            def square(V, i):
                act.wait_ge(proj_done, 6 * V + i + 1)
                if i >= 2:
                    act.wait_ge(sumsq_done, 4 * V + i - 1)
                else:
                    act.wait_ge(sumsq_done, 4 * V)
                src = ps_first[i] if isinstance(V, int) and V == 0 else ps_proj[i % 2]
                act.activation(scratch[:, i % 2], src[:], ACT.Square).then_inc(sq_done, 1)

            def exp_head(U, h, layer):
                act.wait_ge(max_done, 4 * U + h + 1)
                for t in range(NT):
                    n = T if layer == 0 or t else P
                    last = act.activation(probs[:, h, t, 0:n], ps_s[h % 2][:, t * T:t * T + n], ACT.Exp,
                                          bias=neg_max[:, h, t:t + 1], accum_out=row_sum[:, h, t:t + 1])
                last.then_inc(exp_done, 1)

            def copy_v(U, t, V):
                act.wait_ge(proj_done, 6 * V + 5 + t)
                if t == 0:
                    act.wait_ge(pv_done, 4 * U + 4)
                act.activation(v[:, t], ps_proj[t][:], ACT.Copy).then_inc(v_copied, 1)

            def o_high(U, pair, layer, heads=0):
                act.wait_ge(pv_done, 4 * U + 2 * pair + 2)
                for h in range(2):
                    bias = 0.0 if layer == 0 else bv_sb[:, bass.ds(heads + 2 * pair + h, 1)]
                    if layer == 0:
                        if h == 0:
                            last = act.activation(oT_part[0][:, 2 * pair:2 * pair + 2].rearrange("p h t -> p (h t)"),
                                                  ps_o[:], ACT.Copy)
                    else:
                        last = act.activation(oT_part[0][:, 2 * pair + h], ps_o[:, h * T:(h + 1) * T], ACT.Identity, bias=bias)
                last.then_inc(o_high_done, 1)

            def first_w_high(lo, hi):
                act.activation(w_part[0][:, lo * GW:hi * GW], first_w[:, lo * GW:hi * GW], ACT.Copy).then_inc(w_high_done, hi - lo)

            def xT_out(n, b, which, bank=ps_s[0]):
                act.wait_ge(xT_done, n + 1)
                if not isinstance(n, int) or n:
                    act.wait_ge(xT_ready, n)
                for c in range(NE):
                    src = bank[:, c * T:(c + 1) * T]
                    if which is None:
                        last = act.activation(xT_full[:, c], src, ACT.Copy)
                    else:
                        last = act.activation(xT_full[:, c], src, ACT.Identity, bias=ln_sb[:, which, 1, c:c + 1],
                                              scale=ln_sb[:, which, 0, c:c + 1])
                last.then_inc(xT_copied, 1)
                act.wait_ge(xT_copied, n + 1)
                act.activation(xT_part[0][:, bass.ds(b, 1)].rearrange("p b c t -> p (b c t)"),
                               xT_full[:].rearrange("p c t -> p (c t)"), ACT.Copy).then_inc(xT_high_done, 1)

            def unit_1(U):
                V = U + 1
                copy_qkT(U, 0, 0)
                copy_qkT(U, 1, 0)
                square(V, 0)
                copy_qkT(U, 2, 0)
                copy_qkT(U, 3, 0)
                exp_head(U, 0, 0)
                square(V, 1)
                exp_head(U, 1, 0)
                copy_probsT(U, 0, 0)
                square(V, 2)
                copy_probsT(U, 1, 0)
                exp_head(U, 2, 0)
                exp_head(U, 3, 0)
                o_high(U, 0, 0)
                square(V, 3)
                copy_probsT(U, 2, 0)
                copy_probsT(U, 3, 0)
                o_high(U, 1, 0)
                copy_v(U, 0, V)
                copy_v(U, 1, V)

            def unit_1_prologue(U, n, b):
                V = U + 1
                copy_qkT(U, 0, 0)
                copy_qkT(U, 1, 0)
                square(V, 0)
                copy_qkT(U, 2, 0)
                copy_qkT(U, 3, 0)
                exp_head(U, 0, 0)
                exp_head(U, 1, 0)
                square(V, 1)
                copy_probsT(U, 0, 0)
                exp_head(U, 2, 0)
                copy_probsT(U, 1, 0)
                square(V, 2)
                exp_head(U, 3, 0)
                o_high(U, 0, 0)
                xT_out(n, b, None)
                copy_probsT(U, 2, 0)
                square(V, 3)
                copy_probsT(U, 3, 0)
                o_high(U, 1, 0)
                copy_v(U, 0, V)
                copy_v(U, 1, V)

            def unit_1_epilogue(U, nl, n, b):
                V = U + 1
                copy_qkT(U, 0, 0)
                copy_qkT(U, 1, 0)
                if nl == 0:
                    square(V, 0)
                copy_qkT(U, 2, 0)
                copy_qkT(U, 3, 0)
                exp_head(U, 0, 0)
                if nl == 0:
                    square(V, 1)
                exp_head(U, 1, 0)
                exp_head(U, 2, 0)
                copy_probsT(U, 0, 0)
                copy_probsT(U, 1, 0)
                exp_head(U, 3, 0)
                if nl == 0:
                    square(V, 2)
                o_high(U, 0, 0)
                copy_probsT(U, 2, 0)
                if nl == 0:
                    square(V, 3)
                copy_probsT(U, 3, 0)
                o_high(U, 1, 0)
                xT_out(n, b, 0)
                copy_v(U, 0, V)
                copy_v(U, 1, V)

            def unit_2_first(U, n, b):
                V = U + 1
                heads = first_head(act, U)
                copy_qkT(U, 0, 1)
                copy_qkT(U, 1, 1)
                copy_qkT(U, 2, 1)
                copy_qkT(U, 3, 1)
                exp_head(U, 0, 1)
                exp_head(U, 1, 1)
                copy_probsT(U, 0, 1)
                exp_head(U, 2, 1)
                copy_probsT(U, 1, 1)
                exp_head(U, 3, 1)
                o_high(U, 0, 1, heads)
                copy_probsT(U, 2, 1)
                copy_probsT(U, 3, 1)
                copy_v(U, 0, V)
                o_high(U, 1, 1, heads)
                xT_out(n, b, 0)
                copy_v(U, 1, V)

            def unit_2(U):
                V = U + 1
                heads = first_head(act, U)
                copy_qkT(U, 0, 1)
                copy_qkT(U, 1, 1)
                copy_qkT(U, 2, 1)
                copy_qkT(U, 3, 1)
                exp_head(U, 0, 1)
                exp_head(U, 1, 1)
                copy_probsT(U, 0, 1)
                copy_probsT(U, 1, 1)
                exp_head(U, 2, 1)
                exp_head(U, 3, 1)
                o_high(U, 0, 1, heads)
                copy_probsT(U, 2, 1)
                copy_probsT(U, 3, 1)
                o_high(U, 1, 1, heads)
                copy_v(U, 0, V)
                copy_v(U, 1, V)

            def unit_2_epilogue(U, nl, n, b):
                V = U + 1
                heads = first_head(act, U)
                copy_qkT(U, 0, 1)
                copy_qkT(U, 1, 1)
                copy_qkT(U, 2, 1)
                copy_qkT(U, 3, 1)
                exp_head(U, 0, 1)
                exp_head(U, 1, 1)
                exp_head(U, 2, 1)
                copy_probsT(U, 0, 1)
                copy_probsT(U, 1, 1)
                exp_head(U, 3, 1)
                o_high(U, 0, 1, heads)
                copy_probsT(U, 2, 1)
                copy_probsT(U, 3, 1)
                o_high(U, 1, 1, heads)
                if nl is not None:
                    copy_v(U, 0, V)
                xT_out(n, b, 1)
                if nl is not None:
                    copy_v(U, 1, V)

            act.wait_ge(first_w_in, 16)
            first_w_high(0, 2)
            xT_out(0, 0, None, ps_first_x[0])
            act.wait_ge(first_w_in, 32)
            first_w_high(2, 4)
            first_w_high(4, 6)
            xT_out(1, 1, None, ps_first_x[1])
            square(0, 0)
            square(0, 1)
            square(0, 2)
            first_w_high(6, 8)
            xT_out(2, 2, None, ps_first_x[2])
            square(0, 3)
            act.wait_ge(const_in, 16 * 9)
            act.activation(qk_root_sb[:], qk_scale_sb[:], ACT.Copy, scale=float(D) ** 0.5).then_inc(root_set, 1)
            act.wait_ge(root_set, 1)
            for t in range(NT):
                act.wait_ge(proj_done, 5 + t)
                act.activation(v[:, t], ps_first[4 + t][:], ACT.Copy).then_inc(v_copied, 1)
            unit_1_prologue(0, PRE, PRE)
            with act.Fori(1, NB - PRE) as U:
                unit_1_prologue(U, U + PRE, U + PRE)
            with act.Fori(NB - PRE, LAG) as U:
                unit_1(U)
            with act.Fori(LAG, UL - 1) as U:
                unit_1_epilogue(U, 0, U - LAG + NB, U - LAG)
            unit_1_epilogue(UL - 1, 1, 2 * NB - 2, NB - 2)
            unit_2_first(UL, 2 * NB - 1, NB - 1)
            with act.Fori(UL + 1, UL + LAG) as U:
                unit_2(U)
            with act.Fori(UL + LAG, 2 * UL - 1) as U:
                unit_2_epilogue(U, 1, U - UL - LAG + 2 * NB, U - UL - LAG)
            unit_2_epilogue(2 * UL - 1, None, 3 * NB - 2, NB - 2)

            def gelu(g, m):
                act.wait_ge(h1_done, 8 * g + m + 1)
                if not isinstance(g, int) or m >= 2:
                    act.wait_ge(gelu_low_done, 8 * g + m - 1)
                act.activation(gelu_full[m % 2], ps_proj[m % 2][:], ACT.Gelu, bias=be1_sb[:, m:m + 1]).then_inc(gelu_done, 1)
                act.wait_ge(gelu_done, 8 * g + m + 1)
                if not isinstance(g, int) or m >= 4:
                    act.wait_ge(moe_done, 8 * g + 2 * (m // 2) - 2)
                act.activation(gelu_part[0][:, m % 4], gelu_full[m % 2], ACT.Copy).then_inc(gelu_high_done, 1)

            def make_bias_terms(g, p):
                b = 2 * g + p
                if not isinstance(b, int) or b:
                    act.wait_ge(base_step, 2 * b)
                for e in range(NX):
                    for t in range(NT):
                        last = act.activation(bias_terms[e][:, t * E:(t + 1) * E], be2_sb[:, e], ACT.Copy,
                                              scale=gate[0][:, bass.ds(NT * b + t, 1), e])
                last.then_inc(terms_done, 1)

            def gate_exp_of(part, k):
                tiles = GATE_TILES[part]
                act.wait_ge(gate_step, GATE_STEPS * part + GATE_EXP_STEPS[k])
                act.activation(gate[k + 1][:, tiles], gate[0][:, tiles], ACT.Exp).then_inc(gate_exp, 1)

            gelu(0, 0)
            gelu(0, 1)
            gate_exp_of(0, 0)
            gelu(0, 2)
            gelu(0, 3)
            xT_out(3 * NB - 1, NB - 1, 1)
            gate_exp_of(0, 1)
            gelu(0, 4)
            gelu(0, 5)
            gate_exp_of(1, 0)
            act.wait_ge(be2_in, 16)
            act.wait_ge(comb_ready, 1)
            make_bias_terms(0, 0)
            gate_exp_of(1, 1)
            gelu(0, 6)
            gelu(0, 7)
            make_bias_terms(0, 1)
            act.wait_ge(comb_ready, 2)
            with act.Fori(1, NB // 2) as g:
                for m in range(8):
                    gelu(g, m)
                    if m in (1, 3):
                        make_bias_terms(g, m // 2)

        @block.vector
        def _(dve):
            def ln_step_stats(src, i=0):
                for t in range(NT):
                    last = dve.bn_stats(stats[i][:, t], src(t))
                last.then_inc(ln_stats, 1)

            def ln_step_mean(k, i=0):
                dve.wait_ge(ln_stats, k + 1)
                dve.memset(pause[:], 0.0)
                for t in range(NT):
                    last = dve.bn_aggr(mean_var[i][:, t], stats[i][:, t])
                last.then_inc(ln_aggr, 1)

            def ln_step_var(k, i=0):
                dve.wait_ge(ln_aggr, k + 1)
                dve.tensor_scalar(var_eps[i][:], mean_var[i][:, :, 1], LN_EPS, None, ALU.add).then_inc(ln_var, 1)

            def ln_step_out(src, dst, k, i=0):
                dve.wait_ge(ln_rstd, k + 1)
                for t in range(NT):
                    last = dve.tensor_scalar(dst(t), src(t), mean_var[i][:, t, 0:1], rstd[i][:, t:t + 1], ALU.subtract, ALU.mult)
                return last

            def y_tile(b):
                return lambda t: y[:, bass.ds(b, 1), t].rearrange("p b e -> p (b e)")

            def tile_of(buf):
                return lambda t: buf[:, t]

            def xT_low(n, b):
                low = xT_part[1][:, bass.ds(b, 1)].rearrange("p b c t -> p (b c t)")
                high = xT_part[0][:, bass.ds(b, 1)].rearrange("p b c t -> p (b c t)").bitcast(F32)
                dve.wait_ge(xT_high_done, n + 1)
                dve.tensor_tensor(low, xT_full[:].rearrange("p c t -> p (c t)"), high, ALU.subtract).then_inc(xT_ready, 1)

            def low_qkT(U, j, layer):
                which, pair = j % 2, j // 2
                dve.wait_ge(qkT_high_done, 4 * U + j + 1)
                dve.scalar_tensor_tensor(qkT_of(1, which, pair), ps_tr[j % 2][:], score_scale(which, layer),
                                         qkT_of(0, which, pair).bitcast(F32), ALU.mult, ALU.subtract).then_inc(qkT_low_done, 1)

            def sum_squares(V, i):
                dve.wait_ge(sq_done, 4 * V + i + 1)
                dve.tensor_reduce(sumsq[:, i], scratch[:, i % 2].rearrange("p (h d) -> p h d", h=GH),
                                  axis=X, op=ALU.add).then_inc(sumsq_done, 1)

            def scale_qk(V, i):
                dve.wait_ge(rstd_qk_done, 4 * V + i + 1)
                dve.wait_ge(tr_done, 8 * V - (5 if i < 2 else 4))
                dve.tensor_tensor(qk[:, i].rearrange("p (h d) -> p h d", h=GH),
                                  ps_proj[i % 2][:].rearrange("p (h d) -> p h d", h=GH),
                                  rstd_qk[:, i].unsqueeze(2).to_broadcast([P, GH, D]), ALU.mult).then_inc(qk_ready, 1)

            def add_bias(V, i):
                n = 4 * (V - UL) + i
                dve.wait_ge(proj_done, 6 * V + i + 1)
                if i >= 2:
                    dve.wait_ge(rot_a_done, n - 1)
                    dve.wait_ge(rot_b_done, n - 1)
                if isinstance(V, int) and V % NB == 0 and i == 0:
                    dve.wait_ge(bias_in, 16 * ((V - UL) // NB + 1))
                bias = bias_sb[:, (i // 2) * GW:(i // 2 + 1) * GW]
                dve.tensor_tensor(scratch[:, i % 2], ps_proj[i % 2][:], bias, ALU.add).then_inc(qk_biased, 1)

            def rotate_b(V, i):
                n = 4 * (V - UL) + i
                dve.wait_ge(qk_biased, n + 1)
                if not isinstance(V, int) or V > UL or i >= 2:
                    dve.wait_ge(qk_ready, 4 * V + i - 1)
                swapped = scratch[:, i % 2].rearrange("p (h s d) -> p h s d", h=GH, s=2)[:, :, ::-1, :]
                sin = rope_sb[:, 1, i % 2].rearrange("p (s d) -> p s d", s=2).unsqueeze(1).to_broadcast([P, GH, 2, D // 2])
                dve.tensor_tensor(rot_b[:, i % 2].rearrange("p (h s d) -> p h s d", h=GH, s=2), swapped, sin,
                                  ALU.mult).then_inc(rot_b_done, 1)

            def rotate_sum(V, i):
                n = 4 * (V - UL) + i
                dve.wait_ge(rot_a_done, n + 1)
                dve.wait_ge(rot_b_done, n + 1)
                dve.wait_ge(tr_done, 8 * V - (5 if i < 2 else 4))
                dve.tensor_tensor(qk[:, i], rot_a[:, i % 2], rot_b[:, i % 2], ALU.add).then_inc(qk_ready, 1)

            def row_max(U, h, layer):
                dve.wait_ge(s_done, 4 * U + h + 1)
                if layer == 0:
                    last = dve.tensor_reduce(neg_max[:, h], ps_s[h % 2][:].rearrange("p (t k) -> p t k", t=NT),
                                             axis=X, op=ALU.max, negate=True)
                else:
                    dve.tensor_reduce(neg_max[:, h, 0:1], ps_s[h % 2][:, 0:P], axis=X, op=ALU.max, negate=True)
                    last = dve.tensor_reduce(neg_max[:, h, 1:2], ps_s[h % 2][:, T:2 * T], axis=X, op=ALU.max, negate=True)
                last.then_inc(max_done, 1)

            def normalise(U, h, layer):
                dve.wait_ge(exp_done, 4 * U + h + 1)
                dve.reciprocal(inv_sum[:, h], row_sum[:, h]).then_inc(inv_done, 1)
                dve.wait_ge(inv_done, 4 * U + h + 1)
                for t in range(NT):
                    n = T if layer == 0 or t else P
                    last = dve.tensor_scalar(probs[:, h, t, 0:n], probs[:, h, t, 0:n], inv_sum[:, h, t:t + 1], None, ALU.mult)
                last.then_inc(probs_done, 1)

            def o_low(U, pair, layer, heads=0):
                dve.wait_ge(o_high_done, 2 * U + pair + 1)
                if layer == 0:
                    last = dve.tensor_tensor(oT_part[1][:, 2 * pair:2 * pair + 2].rearrange("p h t -> p (h t)"), ps_o[:],
                                             oT_part[0][:, 2 * pair:2 * pair + 2].rearrange("p h t -> p (h t)").bitcast(F32),
                                             ALU.subtract)
                else:
                    for h in range(2):
                        bias = bv_sb[:, bass.ds(heads + 2 * pair + h, 1)]
                        last = dve.scalar_tensor_tensor(oT_part[1][:, 2 * pair + h], ps_o[:, h * T:(h + 1) * T], bias,
                                                        oT_part[0][:, 2 * pair + h].bitcast(F32), ALU.add, ALU.subtract)
                last.then_inc(o_low_done, 1)

            def add_y(U):
                dve.wait_ge(y_done, U + 1)
                y_b = y[:, bass.ds(seq(U), 1)].rearrange("p b t e -> p (b t e)")
                dve.tensor_tensor(y_b, ps_y[:], y_b, ALU.add).then_inc(y_added, 1)

            def prologue_stats(b, x=res):
                dve.wait_ge(res_in, 16 * b + 16)
                dve.memset(pause[:], 0.0)
                ln_step_stats(tile_of(x))

            def prologue_mean(b):
                ln_step_mean(b)
                ln_step_var(b)

            def prologue_out(b, x=res, out=xn):
                if not isinstance(b, int) or b >= PRE:
                    dve.wait_ge(xT_done, b)
                ln_step_out(tile_of(x), tile_of(out), b).then_inc(xn_ready, 1)
                dve.wait_ge(xn_ready, b + 1)
                dve.sem_inc(res_free, 1)

            def epilogue_1_stats(b, k):
                if k == 0:
                    dve.wait_ge(y_added, UL - NB + b + 1)
                    ln_step_stats(y_tile(b))
                elif k == 1:
                    dve.wait_ge(x1_ready, b + 1)
                    dve.memset(pause[:], 0.0)
                    ln_step_stats(tile_of(res))
                else:
                    dve.wait_ge(h0_done, b + 1)
                    dve.sem_inc(res_free, 1)
                    ln_step_stats(tile_of(xn))

            def epilogue_1_mean(b, k):
                ln_step_mean(NB + 3 * b + k)
                ln_step_var(NB + 3 * b + k)

            def epilogue_1_out(b, k):
                n = NB + 3 * b + k
                if k == 0:
                    dve.wait_ge(xT_done, NB + b)
                    ln_step_out(y_tile(b), tile_of(xn), n).then_inc(z_done, 1)
                elif k == 1:
                    ln_step_out(tile_of(res), tile_of(xn), n).then_inc(h0_done, 1)
                else:
                    dve.wait_ge(y_set, b + 1)
                    ln_step_out(tile_of(xn), tile_of(xn), n).then_inc(xn_ready, 1)

            def epilogue_2_stats(b):
                dve.wait_ge(y_added, 2 * UL - NB + b + 1)
                ln_step_stats(y_tile(b))

            def epilogue_2_mean(b):
                ln_step_mean(4 * NB + b)
                ln_step_var(4 * NB + b)

            def epilogue_2_out(b):
                dve.wait_ge(xT_done, 2 * NB + b)
                ln_step_out(y_tile(b), tile_of(xn), 4 * NB + b).then_inc(xn_ready, 1)

            def copy_logits(b):
                dve.wait_ge(logits_done, b + 1)
                dve.tensor_copy(logits[:, bass.ds(b * NT, NT)].rearrange("p t x -> p (t x)"),
                                ps_s[1][:, 0:NT * NX]).then_inc(logits_copied, 1)

            def qk_first(V, i, layer):
                if layer == 0:
                    sum_squares(V, i)
                elif layer == 1:
                    add_bias(V, i)
                    rotate_b(V, i)

            def qk_last(V, i, layer):
                if layer == 0:
                    scale_qk(V, i)
                elif layer == 1:
                    rotate_sum(V, i)

            def unit_1(U):
                V = U + 1
                low_qkT(U, 0, 0)
                low_qkT(U, 1, 0)
                sum_squares(V, 0)
                low_qkT(U, 2, 0)
                row_max(U, 0, 0)
                low_qkT(U, 3, 0)
                scale_qk(V, 0)
                row_max(U, 1, 0)
                normalise(U, 0, 0)
                sum_squares(V, 1)
                normalise(U, 1, 0)
                row_max(U, 2, 0)
                scale_qk(V, 1)
                sum_squares(V, 2)
                row_max(U, 3, 0)
                normalise(U, 2, 0)
                scale_qk(V, 2)
                normalise(U, 3, 0)
                o_low(U, 0, 0)
                sum_squares(V, 3)
                scale_qk(V, 3)
                o_low(U, 1, 0)
                add_y(U)

            def unit_1_prologue(U, b):
                V = U + 1
                prologue_stats(b)
                prologue_mean(b)
                low_qkT(U, 0, 0)
                low_qkT(U, 1, 0)
                sum_squares(V, 0)
                low_qkT(U, 2, 0)
                row_max(U, 0, 0)
                low_qkT(U, 3, 0)
                scale_qk(V, 0)
                row_max(U, 1, 0)
                normalise(U, 0, 0)
                row_max(U, 2, 0)
                normalise(U, 1, 0)
                sum_squares(V, 1)
                prologue_out(b)
                row_max(U, 3, 0)
                normalise(U, 2, 0)
                scale_qk(V, 1)
                sum_squares(V, 2)
                o_low(U, 0, 0)
                normalise(U, 3, 0)
                scale_qk(V, 2)
                sum_squares(V, 3)
                o_low(U, 1, 0)
                scale_qk(V, 3)
                add_y(U)

            def unit_1_epilogue(U, nl, b):
                V = U + 1
                epilogue_1_stats(b, 0)
                epilogue_1_mean(b, 0)
                low_qkT(U, 0, 0)
                low_qkT(U, 1, 0)
                epilogue_1_out(b, 0)
                qk_first(V, 0, nl)
                row_max(U, 0, 0)
                low_qkT(U, 2, 0)
                row_max(U, 1, 0)
                low_qkT(U, 3, 0)
                qk_last(V, 0, nl)
                normalise(U, 0, 0)
                row_max(U, 2, 0)
                qk_first(V, 1, nl)
                normalise(U, 1, 0)
                epilogue_1_stats(b, 1)
                row_max(U, 3, 0)
                normalise(U, 2, 0)
                qk_last(V, 1, nl)
                normalise(U, 3, 0)
                epilogue_1_mean(b, 1)
                o_low(U, 0, 0)
                qk_first(V, 2, nl)
                epilogue_1_out(b, 1)
                epilogue_1_stats(b, 2)
                qk_last(V, 2, nl)
                epilogue_1_mean(b, 2)
                qk_first(V, 3, nl)
                o_low(U, 1, 0)
                epilogue_1_out(b, 2)
                qk_last(V, 3, nl)
                add_y(U)

            def unit_2_first(U, b):
                V = U + 1
                heads = first_head(dve, U)
                epilogue_1_stats(b, 0)
                add_bias(V, 0)
                epilogue_1_mean(b, 0)
                low_qkT(U, 0, 1)
                low_qkT(U, 1, 1)
                epilogue_1_out(b, 0)
                rotate_b(V, 0)
                low_qkT(U, 2, 1)
                row_max(U, 0, 1)
                row_max(U, 1, 1)
                low_qkT(U, 3, 1)
                normalise(U, 0, 1)
                epilogue_1_stats(b, 1)
                add_bias(V, 1)
                add_bias(V, 2)
                row_max(U, 2, 1)
                normalise(U, 1, 1)
                row_max(U, 3, 1)
                epilogue_1_mean(b, 1)
                normalise(U, 2, 1)
                rotate_sum(V, 0)
                epilogue_1_out(b, 1)
                normalise(U, 3, 1)
                o_low(U, 0, 1, heads)
                epilogue_1_stats(b, 2)
                rotate_b(V, 1)
                epilogue_1_mean(b, 2)
                rotate_sum(V, 1)
                add_bias(V, 3)
                epilogue_1_out(b, 2)
                o_low(U, 1, 1, heads)
                rotate_b(V, 2)
                rotate_b(V, 3)
                rotate_sum(V, 2)
                add_y(U)
                rotate_sum(V, 3)

            def unit_2(U):
                V = U + 1
                heads = first_head(dve, U)
                low_qkT(U, 0, 1)
                low_qkT(U, 1, 1)
                add_bias(V, 0)
                low_qkT(U, 2, 1)
                row_max(U, 0, 1)
                low_qkT(U, 3, 1)
                row_max(U, 1, 1)
                normalise(U, 0, 1)
                rotate_b(V, 0)
                normalise(U, 1, 1)
                row_max(U, 2, 1)
                add_bias(V, 1)
                add_bias(V, 2)
                row_max(U, 3, 1)
                rotate_b(V, 1)
                normalise(U, 2, 1)
                normalise(U, 3, 1)
                rotate_sum(V, 0)
                o_low(U, 0, 1, heads)
                rotate_b(V, 2)
                add_bias(V, 3)
                rotate_sum(V, 1)
                rotate_sum(V, 2)
                o_low(U, 1, 1, heads)
                rotate_b(V, 3)
                rotate_sum(V, 3)
                add_y(U)

            def unit_2_epilogue(U, nl, b):
                V = U + 1
                heads = first_head(dve, U)
                low_qkT(U, 0, 1)
                low_qkT(U, 1, 1)
                epilogue_2_stats(b)
                if nl is not None:
                    add_bias(V, 0)
                row_max(U, 0, 1)
                low_qkT(U, 2, 1)
                low_qkT(U, 3, 1)
                normalise(U, 0, 1)
                row_max(U, 1, 1)
                if nl is not None:
                    rotate_b(V, 0)
                row_max(U, 2, 1)
                normalise(U, 1, 1)
                if nl is not None:
                    add_bias(V, 1)
                    rotate_b(V, 1)
                normalise(U, 2, 1)
                epilogue_2_mean(b)
                row_max(U, 3, 1)
                if nl is not None:
                    add_bias(V, 2)
                epilogue_2_out(b)
                normalise(U, 3, 1)
                o_low(U, 0, 1, heads)
                if nl is not None:
                    rotate_sum(V, 0)
                    rotate_sum(V, 1)
                    add_bias(V, 3)
                    rotate_b(V, 2)
                    rotate_b(V, 3)
                o_low(U, 1, 1, heads)
                if nl is not None:
                    rotate_sum(V, 2)
                    rotate_sum(V, 3)
                add_y(U)

            def first_w_low(lo, hi):
                dve.wait_ge(w_high_done, hi)
                dve.tensor_tensor(w_part[1][:, lo * GW:hi * GW], first_w[:, lo * GW:hi * GW],
                                  w_part[0][:, lo * GW:hi * GW].bitcast(F32), ALU.subtract).then_inc(w_split, hi - lo)

            def first_sequence(b):
                prologue_stats(b, first_x[b])
                prologue_mean(b)
                prologue_out(b, first_x[b], first_xn[b])

            def first_scale(i):
                dve.wait_ge(rstd_qk_done, i + 1)
                dve.tensor_tensor(qk[:, i].rearrange("p (h d) -> p h d", h=GH),
                                  ps_first[i][:].rearrange("p (h d) -> p h d", h=GH),
                                  rstd_qk[:, i].unsqueeze(2).to_broadcast([P, GH, D]), ALU.mult).then_inc(qk_ready, 1)

            def clear_y(quarter):
                n = NB // 4
                dve.memset(y[:, quarter * n:(quarter + 1) * n], 0.0)

            first_sequence(0)
            first_w_low(0, 2)
            first_sequence(1)
            xT_low(0, 0)
            first_w_low(2, 4)
            first_w_low(4, 6)
            xT_low(1, 1)
            sum_squares(0, 0)
            prologue_stats(2, first_x[2])
            prologue_mean(2)
            first_scale(0)
            sum_squares(0, 1)
            prologue_out(2, first_x[2], first_xn[2])
            first_scale(1)
            sum_squares(0, 2)
            first_w_low(6, 8)
            first_scale(2)
            sum_squares(0, 3)
            xT_low(2, 2)
            dve.wait_ge(w_split, STEPS)
            clear_y(0)
            first_scale(3)
            dve.wait_ge(const_in, 16 * 9)
            dve.wait_ge(root_set, 1)
            unit_1_prologue(0, PRE)
            clear_y(1)
            clear_y(2)
            with dve.Fori(1, NB - PRE) as U:
                unit_1_prologue(U, U + PRE)
            clear_y(3)
            with dve.Fori(NB - PRE, LAG) as U:
                unit_1(U)
            with dve.Fori(LAG, UL - 1) as U:
                unit_1_epilogue(U, 0, U - LAG)
            unit_1_epilogue(UL - 1, 1, NB - 2)
            unit_2_first(UL, NB - 1)
            for g in range(NG - 1):
                with dve.Fori(UL + max(g * NB, 1), UL + (g + 1) * NB - 1) as U:
                    unit_2(U)
                unit_2(UL + (g + 1) * NB - 1)
            unit_2(UL + LAG - 1)
            with dve.Fori(UL + LAG, 2 * UL - 1) as U:
                unit_2_epilogue(U, 1, U - UL - LAG)
                copy_logits(U - UL - LAG)
            unit_2_epilogue(2 * UL - 1, None, NB - 2)
            copy_logits(NB - 2)

            def gelu_low(g, m):
                dve.wait_ge(gelu_high_done, 8 * g + m + 1)
                dve.tensor_tensor(gelu_part[1][:, m % 4], gelu_full[m % 2], gelu_part[0][:, m % 4].bitcast(F32),
                                  ALU.subtract).then_inc(gelu_low_done, 1)

            comb = gate[0]

            def make_gate(part, phase):
                steps = [GATE_STEPS * part + (0, *GATE_EXP_STEPS)[phase]]

                def link(instruction):
                    steps[0] += 1
                    instruction.then_inc(gate_step, 1)
                    dve.wait_ge(gate_step, steps[0])

                tiles = GATE_TILES[part]
                n = tiles.stop - tiles.start
                g0, g1, g2 = (g[:, tiles] for g in gate)
                r0, r1, r2 = (g[:, tiles] for g in gate_1)
                first = beats[:, tiles]
                chosen = first[:, :, 0]
                shape = [P, n, NX]
                raw = g1
                if phase == 0:
                    dve.wait_ge(logits_copied, NB - 1 + part)
                    link(dve.tensor_reduce(r0, logits[:, tiles], axis=X, op=ALU.max))
                    link(dve.tensor_tensor(g0, logits[:, tiles], r0.unsqueeze(2).to_broadcast(shape), ALU.subtract))
                elif phase == 1:
                    dve.wait_ge(gate_exp, 2 * part + 1)
                    link(dve.tensor_reduce(r0, g1, axis=X, op=ALU.add))
                    link(dve.reciprocal(r1, r0))
                    link(dve.tensor_tensor(raw, g1, r1.unsqueeze(2).to_broadcast(shape), ALU.mult))
                    link(dve.memset(first, 0.0))
                    for j in range(NX):
                        for lo, hi, op in ((0, j, ALU.is_gt), (j + 1, NX, ALU.is_ge)):
                            if hi > lo:
                                last = dve.tensor_tensor(first[:, :, j, lo:hi], raw[:, :, j:j + 1].to_broadcast([P, n, hi - lo]),
                                                         raw[:, :, lo:hi], op)
                    link(last)
                    link(dve.tensor_reduce(g2, first.rearrange("p t j e -> p t e j"), axis=X, op=ALU.add))
                    link(dve.tensor_scalar(g2, g2, 1.5, None, ALU.is_lt))
                    link(dve.tensor_copy(chosen, g2))
                    link(dve.tensor_reduce(r2, raw, axis=X, op=ALU.max))
                    link(dve.tensor_tensor(g0, raw, r2.unsqueeze(2).to_broadcast(shape), ALU.subtract))
                else:
                    dve.wait_ge(gate_exp, 2 * part + 2)
                    link(dve.tensor_tensor(g0, g2, chosen, ALU.mult))
                    link(dve.tensor_reduce(r0, g0, axis=X, op=ALU.add))
                    link(dve.reciprocal(r1, r0))
                    dve.tensor_tensor(comb[:, tiles], g0, r1.unsqueeze(2).to_broadcast(shape), ALU.mult).then_inc(comb_ready, 1)
                    dve.wait_ge(comb_ready, part + 1)

            make_gate(0, 0)
            epilogue_2_stats(NB - 1)
            epilogue_2_mean(NB - 1)
            gelu_low(0, 0)
            gelu_low(0, 1)
            epilogue_2_out(NB - 1)
            gelu_low(0, 2)
            gelu_low(0, 3)
            make_gate(0, 1)
            make_gate(0, 2)
            xT_low(3 * NB - 1, NB - 1)
            copy_logits(NB - 1)
            make_gate(1, 0)

            def add_expert_to(g, e, p):
                b = 2 * g + p
                dve.wait_ge(moe_done, 8 * g + 2 * e + p + 1)
                if e == NX - 1:
                    dve.wait_ge(base_added, b + 1)
                elif e:
                    dve.wait_ge(moe_added, 8 * g + 2 * e + p - 1)
                for t in range(NT):
                    last = dve.scalar_tensor_tensor(y_tile(b)(t), ps_expert[e][p][:, t * E:(t + 1) * E],
                                                    comb[:, bass.ds(NT * b + t, 1), e], y_tile(b)(t), ALU.mult, ALU.add)
                last.then_inc(moe_added, 1)

            def add_expert(g, e):
                for p in range(2):
                    add_expert_to(g, e, p)

            def final_norm(g, p, k):
                b = 2 * g + p
                n = 5 * NB + b
                if k == 0:
                    dve.wait_ge(moe_added, 8 * g + 7 + p)
                    dve.memset(pause[:], 0.0)
                    ln_step_stats(y_tile(b), p)
                elif k == 1:
                    ln_step_mean(n, p)
                elif k == 2:
                    ln_step_var(n, p)
                elif k == 3:
                    if p == 0 and (not isinstance(g, int) or g):
                        dve.wait_ge(out_stored, 32 * g)
                    ln_step_out(y_tile(b), tile_of(last_out[p]), n, p).then_inc(z_done, 1)
                elif k == 4:
                    dve.wait_ge(z_done, NB + b + 1)
                    dve.wait_ge(res_in, 16 * (2 * NB + b) + 16)
                    dve.tensor_tensor(last_out[p][:], last_x[p][:], last_out[p][:], ALU.add).then_inc(out_ready, 1)
                    dve.wait_ge(out_ready, b + 1)
                    dve.sem_inc(res_free, 1)

            add_expert(0, 0)
            gelu_low(0, 4)
            gelu_low(0, 5)
            make_gate(1, 1)
            add_expert(0, 1)
            make_gate(1, 2)
            gelu_low(0, 6)
            gelu_low(0, 7)
            add_expert(0, 2)

            def group(g, before):
                gelu_low(g, 0)
                gelu_low(g, 1)
                add_expert(before, NX - 1)
                final_norm(before, 0, 0)
                gelu_low(g, 2)
                final_norm(before, 0, 1)
                gelu_low(g, 3)
                final_norm(before, 0, 2)
                add_expert(g, 0)
                final_norm(before, 0, 3)
                gelu_low(g, 4)
                final_norm(before, 0, 4)
                gelu_low(g, 5)
                final_norm(before, 1, 0)
                final_norm(before, 1, 1)
                final_norm(before, 1, 2)
                add_expert(g, 1)
                gelu_low(g, 6)
                gelu_low(g, 7)
                final_norm(before, 1, 3)
                final_norm(before, 1, 4)
                add_expert(g, 2)

            with dve.Fori(1, NB // 2) as g:
                group(g, g - 1)
            for p in range(2):
                add_expert_to(NB // 2 - 1, NX - 1, p)
                for k in range(3):
                    final_norm(NB // 2 - 1, p, k)
            for p in range(2):
                for k in (3, 4):
                    final_norm(NB // 2 - 1, p, k)

        @block.tensor
        def _(pe):
            pe.wait_ge(ident_in, 16)

            def project(V, i, layer, base):
                m, t = i // 2, i % 2
                src, dst = (xv_part if m == 2 else xq_part), ps_proj[i % 2]
                if isinstance(V, int) and V == 0:
                    src = [x[:, 0] for x in xT_part]
                    pe.wait_ge(xT_ready, 1)
                    pe.wait_ge(w_split, 2 * m + 2)
                    dst = ps_first[i]
                else:
                    if i == 0:
                        pe.wait_ge(xq_in, 32 * V)
                        pe.wait_ge(w_split, STEPS if isinstance(V, int) and V < NB else V + STEPS)
                    if i == 4:
                        pe.wait_ge(xv_in, 32 * V)
                    if i < 2:
                        pe.wait_ge(v_copied, 2 * V - 1 + i)
                    elif layer == 0:
                        pe.wait_ge(qk_ready, 4 * V + i - 1)
                    else:
                        pe.wait_ge(qk_biased, 4 * (V - UL) + i - 1)
                n = 0
                for c in range(NE):
                    for a, w in PASSES:
                        last = pe.matmul(dst[:], src[a][:, c, t * P:(t + 1) * P], w_cols(base, 2 * m + c, 0, GW, w),
                                         start=(n == 0), stop=(n == 5))
                        n += 1
                last.then_inc(proj_done, 1)

            def transpose_qk(U, j):
                which, pair = j % 2, j // 2
                if j == 0:
                    pe.wait_ge(qk_ready, 4 * U + 4)
                if j < 2:
                    pe.wait_ge(probsT_copied, 4 * U)
                else:
                    pe.wait_ge(qkT_low_done, 4 * U + j - 1)
                for hh in range(2):
                    for t in range(NT):
                        h = 2 * pair + hh
                        last = pe.transpose(ps_tr[j % 2][:, hh * T + t * P:hh * T + (t + 1) * P],
                                            qk[:, 2 * which + t, h * D:(h + 1) * D], ident_sb[:])
                last.then_inc(tr_done, 1)

            def scores(U, h, layer, bank_free=None):
                if h % 2 == 0:
                    pe.wait_ge(qkT_low_done, 4 * U + h + 2)
                if bank_free is not None:
                    pe.wait_ge(*bank_free)
                if h >= 2:
                    pe.wait_ge(exp_done, 4 * U + h - 1)
                else:
                    pe.wait_ge(exp_done, 4 * U)
                for t in range(NT):
                    n = T if layer == 0 or t else P
                    for a, w in PASSES:
                        last = pe.matmul(ps_s[h % 2][:, t * T:t * T + n], qkT_part[a][:, 0, h, t * P:(t + 1) * P],
                                         qkT_part[w][:, 1, h, 0:n], start=(t == 0 and (a, w) == PASSES[0]),
                                         stop=((a, w) == PASSES[-1]), skip_group_check=True)
                if layer == 1:
                    diagonals = ps_s[h % 2][:].rearrange("p (a k) -> p a k", k=P)[:, 0:4:3]
                    last = pe.matmul(diagonals, mask_sb[:, 0], mask_sb[:, 1].unsqueeze(1).to_broadcast([P, NT, P]),
                                     start=False, stop=True, skip_group_check=True)
                last.then_inc(s_done, 1)

            def transpose_probs(U, h, layer):
                pe.wait_ge(probs_done, 4 * U + h + 1)
                if h < 2:
                    pe.wait_ge(qkT_low_done, 4 * U + 3 + h)
                else:
                    pe.wait_ge(probsT_copied, 4 * U + h - 1)
                for k in range(NT):
                    for q in range(NT):
                        if layer == 0 or k <= q:
                            last = pe.transpose(ps_tr[h % 2][:, k * T + q * P:k * T + (q + 1) * P],
                                                probs[:, h, q, k * P:(k + 1) * P], ident_sb[:])
                last.then_inc(tr_done, 1)

            def probs_v(U, h, layer):
                pe.wait_ge(probsT_copied, 4 * U + h + 1)
                if h == 0:
                    pe.wait_ge(v_copied, 2 * U + 2)
                    pe.wait_ge(o_low_done, 2 * U)
                if h == 2:
                    pe.wait_ge(o_low_done, 2 * U + 1)
                base = (h % 2) * T
                pe.matmul(ps_o[:, base:base + T], v[:, 0, h * D:(h + 1) * D], probsT[:, h % 2, 0], start=True, stop=(layer == 1))
                q0 = 0 if layer == 0 else P
                pe.matmul(ps_o[:, base + q0:base + T], v[:, 1, h * D:(h + 1) * D], probsT[:, h % 2, 1, q0:T],
                          start=False, stop=True, skip_group_check=(layer == 1)).then_inc(pv_done, 1)

            def out_project(U, h, base):
                if h == 0:
                    pe.wait_ge(y_added, U)
                if h % 2 == 0:
                    pe.wait_ge(o_low_done, 2 * U + h // 2 + 1)
                for t in range(NT):
                    for a, w in PASSES:
                        last = pe.matmul(ps_y[:, t * E:(t + 1) * E], oT_part[a][:, h, t * P:(t + 1) * P],
                                         w_cols(base, 6 + h // 2, (h % 2) * E, E, w),
                                         start=(h == 0 and t == 0 and (a, w) == (0, 0)), stop=(h == GH - 1),
                                         skip_group_check=True)
                if h == GH - 1:
                    last.then_inc(y_done, 1)

            def transpose_x(n, U=None, src=xn, bank=ps_s[0]):
                pe.wait_ge(xn_ready, n + 1)
                if U is not None:
                    pe.wait_ge(exp_done, 4 * U + 3)
                for c in range(NE):
                    for t in range(NT):
                        last = pe.transpose(bank[:, c * T + t * P:c * T + (t + 1) * P], src[:, t, c * P:(c + 1) * P], ident_sb[:])
                last.then_inc(xT_done, 1)

            def gate_logits(b):
                pe.wait_ge(xT_copied, 2 * NB + b + 1)
                for t in range(NT):
                    for c in range(NE):
                        last = pe.matmul(ps_s[1][:, t * NX:(t + 1) * NX], xT_full[:, c, t * P:(t + 1) * P], w_gate_sb[:, c],
                                         start=(c == 0), stop=(c == NE - 1))
                last.then_inc(logits_done, 1)

            def expert_in(g, m):
                e, ic = m // 2, m % 2
                if isinstance(g, int) and m < 2:
                    pe.wait_ge(v_copied, 2 * 2 * UL)
                    pe.wait_ge(w_split, 2 * NG * STEPS + 2)
                    pe.wait_ge(xT_ready, 2 * NB + 2)
                else:
                    pe.wait_ge(gelu_done, 8 * g + m - 1)
                n = 0
                for c in range(NE):
                    for a, w in PASSES:
                        last = pe.matmul(ps_proj[m % 2][:].rearrange("p (b t) -> p b t", b=2),
                                         w_part[a][:, (2 * e) * GW + c * IM + ic * P:(2 * e) * GW + c * IM + (ic + 1) * P],
                                         xT_part[w][:, bass.ds(2 * g, 2), c], start=(n == 0), stop=(n == 5))
                        n += 1
                last.then_inc(h1_done, 1)

            def expert_out(g, e):
                pe.wait_ge(gelu_low_done, 8 * g + 2 * e + 2)
                for p in range(2):
                    if e == 3:
                        pe.wait_ge(moe_added, 8 * g + 3 + p)
                    elif not isinstance(g, int) or g:
                        pe.wait_ge(moe_added, 8 * g + (p - 7, p - 1, p - 3)[e])
                    for t in range(NT):
                        n = 0
                        for ic in range(2):
                            for a, w in PASSES:
                                lo = (2 * e + 1) * GW + ic * E
                                last = pe.matmul(ps_expert[e][p][:, t * E:(t + 1) * E],
                                                 gelu_part[a][:, (2 * e + ic) % 4, (2 * p + t) * P:(2 * p + t + 1) * P],
                                                 w_part[w][:, lo:lo + E], start=(n == 0), stop=(n == 5))
                                n += 1
                    last.then_inc(moe_done, 1)

            def w_base(unit):
                base = ((unit // NB) % 2) * (STEPS * GW)
                return base if isinstance(base, int) else pe.snap(base)

            def unit_1(U, xT_count):
                V = U + 1
                nl = 0
                w_u, w_v = w_base(U), w_base(V)
                transpose_qk(U, 0)
                transpose_qk(U, 1)
                project(V, 0, nl, w_v)
                transpose_qk(U, 2)
                scores(U, 0, 0, (xT_copied, xT_count))
                transpose_qk(U, 3)
                scores(U, 1, 0)
                project(V, 1, nl, w_v)
                scores(U, 2, 0)
                project(V, 2, nl, w_v)
                transpose_probs(U, 0, 0)
                scores(U, 3, 0)
                transpose_probs(U, 1, 0)
                probs_v(U, 0, 0)
                project(V, 3, nl, w_v)
                probs_v(U, 1, 0)
                transpose_probs(U, 2, 0)
                project(V, 4, nl, w_v)
                transpose_probs(U, 3, 0)
                probs_v(U, 2, 0)
                out_project(U, 0, w_u)
                probs_v(U, 3, 0)
                out_project(U, 1, w_u)
                project(V, 5, nl, w_v)
                out_project(U, 2, w_u)
                out_project(U, 3, w_u)

            def unit_1_prologue(U, n):
                V = U + 1
                nl = 0
                xT_count = n
                w_u, w_v = w_base(U), w_base(V)
                transpose_qk(U, 0)
                transpose_qk(U, 1)
                project(V, 0, nl, w_v)
                transpose_qk(U, 2)
                transpose_qk(U, 3)
                scores(U, 0, 0, (xT_copied, xT_count))
                scores(U, 1, 0)
                project(V, 1, nl, w_v)
                scores(U, 2, 0)
                project(V, 2, nl, w_v)
                transpose_probs(U, 0, 0)
                scores(U, 3, 0)
                transpose_probs(U, 1, 0)
                probs_v(U, 0, 0)
                transpose_x(n, U)
                probs_v(U, 1, 0)
                transpose_probs(U, 2, 0)
                project(V, 3, nl, w_v)
                out_project(U, 0, w_u)
                transpose_probs(U, 3, 0)
                probs_v(U, 2, 0)
                probs_v(U, 3, 0)
                project(V, 4, nl, w_v)
                out_project(U, 1, w_u)
                out_project(U, 2, w_u)
                out_project(U, 3, w_u)
                project(V, 5, nl, w_v)

            def unit_1_epilogue(U, nl, n):
                V = U + 1
                xT_count = n
                w_u, w_v = w_base(U), w_base(V)
                transpose_qk(U, 0)
                transpose_qk(U, 1)
                project(V, 0, nl, w_v)
                transpose_qk(U, 2)
                scores(U, 0, 0, (xT_copied, xT_count))
                scores(U, 1, 0)
                transpose_qk(U, 3)
                project(V, 1, nl, w_v)
                scores(U, 2, 0)
                project(V, 2, nl, w_v)
                transpose_probs(U, 0, 0)
                scores(U, 3, 0)
                transpose_probs(U, 1, 0)
                probs_v(U, 0, 0)
                probs_v(U, 1, 0)
                transpose_probs(U, 2, 0)
                project(V, 3, nl, w_v)
                transpose_probs(U, 3, 0)
                probs_v(U, 2, 0)
                out_project(U, 0, w_u)
                probs_v(U, 3, 0)
                out_project(U, 1, w_u)
                project(V, 4, nl, w_v)
                out_project(U, 2, w_u)
                transpose_x(n, U)
                out_project(U, 3, w_u)
                project(V, 5, nl, w_v)

            def unit_2_first(U, n):
                V = U + 1
                nl = 1
                xT_count = n
                w_u, w_v = w_base(U), w_base(V)
                project(V, 0, nl, w_v)
                transpose_qk(U, 0)
                transpose_qk(U, 1)
                project(V, 1, nl, w_v)
                transpose_qk(U, 2)
                scores(U, 0, 1, (xT_copied, xT_count))
                transpose_qk(U, 3)
                scores(U, 1, 1)
                project(V, 2, nl, w_v)
                scores(U, 2, 1)
                transpose_probs(U, 0, 1)
                scores(U, 3, 1)
                probs_v(U, 0, 1)
                project(V, 3, nl, w_v)
                transpose_probs(U, 1, 1)
                probs_v(U, 1, 1)
                transpose_probs(U, 2, 1)
                project(V, 4, nl, w_v)
                transpose_probs(U, 3, 1)
                probs_v(U, 2, 1)
                probs_v(U, 3, 1)
                out_project(U, 0, w_u)
                out_project(U, 1, w_u)
                project(V, 5, nl, w_v)
                out_project(U, 2, w_u)
                out_project(U, 3, w_u)
                transpose_x(n, U)

            def unit_2(U, xT_count):
                V = U + 1
                nl = 1
                w_u, w_v = w_base(U), w_base(V)
                transpose_qk(U, 0)
                transpose_qk(U, 1)
                project(V, 0, nl, w_v)
                transpose_qk(U, 2)
                scores(U, 0, 1, (xT_copied, xT_count))
                transpose_qk(U, 3)
                scores(U, 1, 1)
                project(V, 1, nl, w_v)
                scores(U, 2, 1)
                project(V, 2, nl, w_v)
                transpose_probs(U, 0, 1)
                transpose_probs(U, 1, 1)
                scores(U, 3, 1)
                probs_v(U, 0, 1)
                probs_v(U, 1, 1)
                project(V, 3, nl, w_v)
                transpose_probs(U, 2, 1)
                transpose_probs(U, 3, 1)
                project(V, 4, nl, w_v)
                probs_v(U, 2, 1)
                probs_v(U, 3, 1)
                out_project(U, 0, w_u)
                out_project(U, 1, w_u)
                project(V, 5, nl, w_v)
                out_project(U, 2, w_u)
                out_project(U, 3, w_u)

            def unit_2_epilogue(U, nl, n, logits_free):
                V = U + 1
                xT_count = n
                w_u, w_v = w_base(U), w_base(V) if nl is not None else None
                transpose_qk(U, 0)
                transpose_qk(U, 1)
                if nl is not None:
                    project(V, 0, nl, w_v)
                else:
                    expert_in(0, 0)
                transpose_qk(U, 2)
                scores(U, 0, 1, (xT_copied, xT_count))
                transpose_qk(U, 3)
                if nl is not None:
                    project(V, 1, nl, w_v)
                else:
                    expert_in(0, 1)
                scores(U, 1, 1, logits_free)
                scores(U, 2, 1)
                transpose_probs(U, 0, 1)
                if nl is not None:
                    project(V, 2, nl, w_v)
                scores(U, 3, 1)
                transpose_probs(U, 1, 1)
                if nl is not None:
                    project(V, 3, nl, w_v)
                probs_v(U, 0, 1)
                probs_v(U, 1, 1)
                transpose_probs(U, 2, 1)
                if nl is not None:
                    project(V, 4, nl, w_v)
                transpose_probs(U, 3, 1)
                transpose_x(n, U)
                probs_v(U, 2, 1)
                probs_v(U, 3, 1)
                out_project(U, 0, w_u)
                if nl is not None:
                    project(V, 5, nl, w_v)
                out_project(U, 1, w_u)
                out_project(U, 2, w_u)
                out_project(U, 3, w_u)

            transpose_x(0, src=first_xn[0], bank=ps_first_x[0])
            transpose_x(1, src=first_xn[1], bank=ps_first_x[1])
            for i in range(4):
                project(0, i, 0, 0)
            transpose_x(2, src=first_xn[2], bank=ps_first_x[2])
            for i in range(4, 6):
                project(0, i, 0, 0)
            pe.wait_ge(const_in, 16 * 9)
            pe.wait_ge(xT_copied, PRE)
            pe.wait_ge(v_copied, 2)
            unit_1_prologue(0, PRE)
            with pe.Fori(1, NB - PRE) as U:
                unit_1_prologue(U, U + PRE)
            with pe.Fori(NB - PRE, LAG) as U:
                unit_1(U, NB)
            with pe.Fori(LAG, UL - 1) as U:
                unit_1_epilogue(U, 0, U - LAG + NB)
            unit_1_epilogue(UL - 1, 1, 2 * NB - 2)
            unit_2_first(UL, 2 * NB - 1)
            with pe.Fori(UL + 1, UL + LAG) as U:
                unit_2(U, 2 * NB)
            unit_2_epilogue(UL + LAG, 1, 2 * NB, None)
            gate_logits(0)
            with pe.Fori(UL + LAG + 1, 2 * UL - 1) as U:
                unit_2_epilogue(U, 1, U - UL - LAG + 2 * NB, (logits_copied, U - UL - LAG))
                gate_logits(U - UL - LAG)
            unit_2_epilogue(2 * UL - 1, None, 3 * NB - 2, (logits_copied, NB - 2))
            gate_logits(NB - 2)
            expert_in(0, 2)
            expert_in(0, 3)
            transpose_x(3 * NB - 1)
            pe.wait_ge(w_split, NSTEP)
            expert_out(0, 0)
            pe.wait_ge(logits_copied, NB - 1)
            gate_logits(NB - 1)
            expert_in(0, 4)
            expert_in(0, 5)
            pe.wait_ge(y_added, 2 * UL)
            expert_out(0, 1)
            expert_in(0, 6)
            expert_in(0, 7)
            pe.wait_ge(logits_copied, NB)
            expert_out(0, 2)
            pe.wait_ge(xT_ready, 3 * NB)
            with pe.Fori(1, NB // 2) as g:
                expert_in(g, 0)
                expert_in(g, 1)
                expert_out(g - 1, NX - 1)
                for e in range(1, NX):
                    expert_in(g, 2 * e)
                    expert_in(g, 2 * e + 1)
                    expert_out(g, e - 1)
            expert_out(NB // 2 - 1, NX - 1)
    return nc


def kernel(**inputs):
    import concourse.bacc as _bacc
    from concourse.bass_utils import run_bass_kernel_spmd as _run

    a = {k.replace("L0_", ""): np.asarray(v_) for k, v_ in inputs.items()}

    pieces = []
    for blk in ("attn", "ffn"):
        wq, wk, wv, wo = (a[f"{blk}_w{c}"] for c in "qkvo")
        wo = wo.reshape(H, D, E)
        for g in range(NG):
            for w in (wq, wk, wv):
                w = w.reshape(E, H * D)[:, g * GW:(g + 1) * GW]
                pieces += [w[0:P], w[P:2 * P]]
            for j in range(2):
                pieces.append(wo[g * GH + 2 * j:g * GH + 2 * j + 2].transpose(1, 0, 2).reshape(P, GW))
    for e in range(NX):
        for w in (a["ffn_we1"][e], a["ffn_we2"][e]):
            pieces.append(w.reshape(2, P, 256).transpose(1, 0, 2).reshape(P, GW))

    def column(v_):
        return np.ascontiguousarray(v_.reshape(-1, P).T)

    inv_freq = (1.0 / 10000.0 ** (np.arange(0, D, 2, dtype=np.float32) / np.float32(D))).astype(np.float32)
    angle = np.arange(T, dtype=np.float32)[:, None] * inv_freq[None, :]
    cos, sin = np.cos(angle), np.sin(angle)
    rope = np.stack([np.concatenate([cos, cos], 1), np.concatenate([-sin, sin], 1)])
    rope = rope.reshape(2, NT, P, D).transpose(2, 0, 1, 3).astype(np.float32)
    bf16 = mybir.dt.np(BF16) if hasattr(mybir.dt, "np") else __import__("ml_dtypes").bfloat16
    fill = np.where(np.arange(P)[:, None] >= np.arange(P)[None, :], 0.0, -3.0e38)
    masks = np.stack([np.eye(P), fill], 1).astype(bf16)

    arrays = {
        "x": a["attn_x"],
        "weights": np.stack(pieces),
        "qk_scale": np.stack([a["attn_q_scale"], a["attn_k_scale"]], 1),
        "bias_qk": np.concatenate([a["ffn_bq"].reshape(NG, GW), a["ffn_bk"].reshape(NG, GW)], 1),
        "bv": column(a["ffn_bv"]),
        "bo": a["ffn_bo"],
        "ln1": np.stack([column(a["ffn_ln1_w"]), column(a["ffn_ln1_b"])], 1),
        "ln2": np.stack([column(a["ffn_ln2_w"]), column(a["ffn_ln2_b"])], 1),
        "w_gate": a["ffn_w_gate"].reshape(NE, P, NX).transpose(1, 0, 2),
        "be1": a["ffn_be1"].reshape(NX * IM // P, P).T,
        "be2": a["ffn_be2"].reshape(-1),
        "rope": rope,
        "masks": masks,
        "ident": np.eye(P, dtype=np.float32),
    }
    nc = _bacc.Bacc("TRN2", target_bir_lowering=False, num_devices=1)
    arrays = {f"in_{k}": np.ascontiguousarray(v_) for k, v_ in arrays.items()}
    args = [nc.dram_tensor(k, v_.shape, mybir.dt.from_np(v_.dtype), kind="ExternalInput").ap() for k, v_ in arrays.items()]
    out = nc.dram_tensor("out", (NB, T, E), F32, kind="ExternalOutput").ap()
    build(nc, *args, out)
    r = _run(nc, [arrays], core_ids=[0])
    return r.results[0]["out"]
```
